# Optimizing a Trainium2 kernel written in Bass

```python
import numpy as np
import jax
import jax.numpy as jnp

def _softmax(x, axis=-1):
    return jax.nn.softmax(x, axis=axis)

def _gelu(x):
    return jax.nn.gelu(x, approximate=True)

def _silu(x):
    return jax.nn.silu(x)

def _sigmoid(x):
    return jax.nn.sigmoid(x)

def _layernorm(x, axis=-1, eps=1e-05):
    m = jnp.mean(x, axis=axis, keepdims=True)
    v = jnp.var(x, axis=axis, keepdims=True)
    return (x - m) / jnp.sqrt(v + eps)

def _scatter_add(tgt, idx, src, axis=0):
    return tgt.at[idx].add(src)

def _segment_sum(src, seg, n):
    return jax.ops.segment_sum(src, seg, n)
kernel_name = 'mk_hybrid_d1_jaxref_r8_a8e1de'

def setup_inputs(seed: int=0):
    np.random.seed(seed)
    _w = jnp.asarray

    def _L0_attn_a_setup():
        import jax, jax.numpy as jnp
        import numpy as np
        D_IN = 256
        D_OUT = 256
        DL = 128
        NUM_HEAD = 16
        SEQ = 256
        BATCH = 2
        key = jax.random.key(seed)
        ks = jax.random.split(key, 15)
        s = lambda fan_in: 1.0 / np.sqrt(fan_in)
        u = lambda k, shape, fan: jax.random.uniform(k, shape, jnp.float32, -s(fan), s(fan))
        return {'x': jax.random.normal(ks[0], (BATCH, SEQ, D_IN), jnp.float32), 'wk': u(ks[1], (D_IN, D_OUT), D_IN), 'bk': u(ks[2], (D_OUT,), D_IN), 'wq': u(ks[3], (D_IN, D_OUT), D_IN), 'bq': u(ks[4], (D_OUT,), D_IN), 'wv': u(ks[5], (D_IN, D_OUT), D_IN), 'bv': u(ks[6], (D_OUT,), D_IN), 'wkl': u(ks[7], (D_OUT, DL), D_OUT), 'bkl': u(ks[8], (DL,), D_OUT), 'wql': u(ks[9], (D_OUT, DL), D_OUT), 'bql': u(ks[10], (DL,), D_OUT), 'wvl': u(ks[11], (D_OUT, DL), D_OUT), 'bvl': u(ks[12], (DL,), D_OUT), 'wo': u(ks[13], (DL, D_OUT), DL), 'bo': u(ks[14], (D_OUT,), DL)}
    _L0_attn_a_in = _L0_attn_a_setup()

    def _L0_attn_b_setup():
        import jax, jax.numpy as jnp
        import numpy as np
        B, S, HIDDEN, H = (4, 512, 256, 16)
        HD = HIDDEN // H

        def apply_rope(x, inv_freq):
            seq_len = x.shape[1]
            t = jnp.arange(seq_len, dtype=jnp.float32)[:, None]
            angle = t * inv_freq[None, :]
            sin = jnp.sin(angle)[None, :, None, :]
            cos = jnp.cos(angle)[None, :, None, :]
            x1, x2 = (x[..., ::2], x[..., 1::2])
            return jnp.concatenate([x1 * cos - x2 * sin, x1 * sin + x2 * cos], axis=-1)
        key = jax.random.key(seed)
        ks = jax.random.split(key, 5)
        x = jax.random.normal(ks[0], (B, S, HIDDEN), dtype=jnp.float32)
        scale = 1.0 / np.sqrt(HIDDEN)
        wq = jax.random.normal(ks[1], (HIDDEN, HIDDEN), dtype=jnp.float32) * scale
        wk = jax.random.normal(ks[2], (HIDDEN, HIDDEN), dtype=jnp.float32) * scale
        wv = jax.random.normal(ks[3], (HIDDEN, HIDDEN), dtype=jnp.float32) * scale
        wo = jax.random.normal(ks[4], (HIDDEN, HIDDEN), dtype=jnp.float32) * scale
        inv_freq = (1.0 / 10000.0 ** (np.arange(0, HD, 2, dtype=np.float32) / HD)).astype(np.float32)
        inv_freq = jnp.asarray(inv_freq)
        return {'x': x, 'wq': wq, 'wk': wk, 'wv': wv, 'wo': wo, 'inv_freq': inv_freq}
    _L0_attn_b_in = _L0_attn_b_setup()

    def _L0_ffn_setup():
        import jax, jax.numpy as jnp
        import numpy as np
        B, S, D, F, E, SH, K = (2, 256, 256, 128, 16, 2, 2)

        def _experts_all(x, g, gb, w1, b1, w2, b2):
            y = jax.nn.gelu(jnp.einsum('bsd,edf->bsef', x, g) + gb, approximate=False)
            y = y * (jnp.einsum('bsd,edf->bsef', x, w1) + b1)
            return jnp.einsum('bsef,efd->bsed', y, w2) + b2
        key = jax.random.key(seed)
        ks = jax.random.split(key, 8)
        std = 0.02
        mk = lambda k, sh: jax.random.normal(k, sh, jnp.float32) * std
        return {'x': jax.random.normal(ks[0], (B, S, D), jnp.float32), 'wa': mk(ks[1], (D, E)), 'rg': mk(ks[2], (E, D, F)), 'rgb': jnp.zeros((E, F), jnp.float32), 'rw1': mk(ks[3], (E, D, F)), 'rb1': jnp.zeros((E, F), jnp.float32), 'rw2': mk(ks[4], (E, F, D)), 'rb2': jnp.zeros((E, D), jnp.float32), 'sg': mk(ks[5], (SH, D, F)), 'sgb': jnp.zeros((SH, F), jnp.float32), 'sw1': mk(ks[6], (SH, D, F)), 'sb1': jnp.zeros((SH, F), jnp.float32), 'sw2': mk(ks[7], (SH, F, D)), 'sb2': jnp.zeros((SH, D), jnp.float32)}
    _L0_ffn_in = _L0_ffn_setup()
    _d = {'L0_attn_a_x': _L0_attn_a_in['x'], 'L0_attn_a_wk': _L0_attn_a_in['wk'], 'L0_attn_a_bk': _L0_attn_a_in['bk'], 'L0_attn_a_wq': _L0_attn_a_in['wq'], 'L0_attn_a_bq': _L0_attn_a_in['bq'], 'L0_attn_a_wv': _L0_attn_a_in['wv'], 'L0_attn_a_bv': _L0_attn_a_in['bv'], 'L0_attn_a_wkl': _L0_attn_a_in['wkl'], 'L0_attn_a_bkl': _L0_attn_a_in['bkl'], 'L0_attn_a_wql': _L0_attn_a_in['wql'], 'L0_attn_a_bql': _L0_attn_a_in['bql'], 'L0_attn_a_wvl': _L0_attn_a_in['wvl'], 'L0_attn_a_bvl': _L0_attn_a_in['bvl'], 'L0_attn_a_wo': _L0_attn_a_in['wo'], 'L0_attn_a_bo': _L0_attn_a_in['bo'], 'L0_attn_b_wq': _L0_attn_b_in['wq'], 'L0_attn_b_wk': _L0_attn_b_in['wk'], 'L0_attn_b_wv': _L0_attn_b_in['wv'], 'L0_attn_b_wo': _L0_attn_b_in['wo'], 'L0_attn_b_inv_freq': _L0_attn_b_in['inv_freq'], 'L0_ffn_wa': _L0_ffn_in['wa'], 'L0_ffn_rg': _L0_ffn_in['rg'], 'L0_ffn_rgb': _L0_ffn_in['rgb'], 'L0_ffn_rw1': _L0_ffn_in['rw1'], 'L0_ffn_rb1': _L0_ffn_in['rb1'], 'L0_ffn_rw2': _L0_ffn_in['rw2'], 'L0_ffn_rb2': _L0_ffn_in['rb2'], 'L0_ffn_sg': _L0_ffn_in['sg'], 'L0_ffn_sgb': _L0_ffn_in['sgb'], 'L0_ffn_sw1': _L0_ffn_in['sw1'], 'L0_ffn_sb1': _L0_ffn_in['sb1'], 'L0_ffn_sw2': _L0_ffn_in['sw2'], 'L0_ffn_sb2': _L0_ffn_in['sb2']}
    _x0 = _d['L0_attn_a_x']
    _d['L0_attn_a_x'] = jax.random.normal(jax.random.fold_in(jax.random.key(seed), 1), (2, 1024, 256), dtype=_x0.dtype)
    del _x0
    return _d

def reference(L0_attn_a_x, L0_attn_a_wk, L0_attn_a_bk, L0_attn_a_wq, L0_attn_a_bq, L0_attn_a_wv, L0_attn_a_bv, L0_attn_a_wkl, L0_attn_a_bkl, L0_attn_a_wql, L0_attn_a_bql, L0_attn_a_wvl, L0_attn_a_bvl, L0_attn_a_wo, L0_attn_a_bo, L0_attn_b_wq, L0_attn_b_wk, L0_attn_b_wv, L0_attn_b_wo, L0_attn_b_inv_freq, L0_ffn_wa, L0_ffn_rg, L0_ffn_rgb, L0_ffn_rw1, L0_ffn_rb1, L0_ffn_rw2, L0_ffn_rb2, L0_ffn_sg, L0_ffn_sgb, L0_ffn_sw1, L0_ffn_sb1, L0_ffn_sw2, L0_ffn_sb2):

    def _L0_attn_a_ref(x, wk, bk, wq, bq, wv, bv, wkl, bkl, wql, bql, wvl, bvl, wo, bo):
        import jax, jax.numpy as jnp
        import numpy as np
        D_IN = 256
        D_OUT = 256
        DL = 128
        NUM_HEAD = 16
        SEQ = 256
        BATCH = 2
        b, t, _ = x.shape
        hd = DL // NUM_HEAD
        k = ((x @ wk + bk) @ wkl + bkl).reshape(b, t, NUM_HEAD, hd)
        q = ((x @ wq + bq) @ wql + bql).reshape(b, t, NUM_HEAD, hd)
        v = ((x @ wv + bv) @ wvl + bvl).reshape(b, t, NUM_HEAD, hd)
        scores = jnp.einsum('bthd,bshd->bhts', q, k)
        causal = jnp.tril(jnp.ones((t, t), dtype=bool))
        scores = jnp.where(causal, scores, -jnp.inf)
        attn = jax.nn.softmax(scores / jnp.sqrt(jnp.float32(hd)), axis=-1)
        out = jnp.einsum('bhts,bshd->bthd', attn, v).reshape(b, t, DL)
        return out @ wo + bo

    def _L0_attn_b_ref(x, wq, wk, wv, wo, inv_freq):
        import jax, jax.numpy as jnp
        import numpy as np
        B, S, HIDDEN, H = (4, 512, 256, 16)
        HD = HIDDEN // H

        def apply_rope(x, inv_freq):
            seq_len = x.shape[1]
            t = jnp.arange(seq_len, dtype=jnp.float32)[:, None]
            angle = t * inv_freq[None, :]
            sin = jnp.sin(angle)[None, :, None, :]
            cos = jnp.cos(angle)[None, :, None, :]
            x1, x2 = (x[..., ::2], x[..., 1::2])
            return jnp.concatenate([x1 * cos - x2 * sin, x1 * sin + x2 * cos], axis=-1)
        b, s, _ = x.shape
        q = (x @ wq.T).reshape(b, s, H, HD)
        k = (x @ wk.T).reshape(b, s, H, HD)
        v = (x @ wv.T).reshape(b, s, H, HD)
        q = apply_rope(q, inv_freq)
        k = apply_rope(k, inv_freq)
        scores = jnp.einsum('bshd,bstd->bsht', q, k) / jnp.sqrt(jnp.float32(HD))
        weights = jax.nn.softmax(scores, axis=-1)
        attn = jnp.einsum('bsht,bstd->bshd', weights, v)
        attn = attn.reshape(b, s, HIDDEN)
        return attn @ wo.T

    def _L0_ffn_ref(x, wa, rg, rgb, rw1, rb1, rw2, rb2, sg, sgb, sw1, sb1, sw2, sb2):
        import jax, jax.numpy as jnp
        import numpy as np
        B, S, D, F, E, SH, K = (2, 256, 256, 128, 16, 2, 2)

        def _experts_all(x, g, gb, w1, b1, w2, b2):
            y = jax.nn.gelu(jnp.einsum('bsd,edf->bsef', x, g) + gb, approximate=False)
            y = y * (jnp.einsum('bsd,edf->bsef', x, w1) + b1)
            return jnp.einsum('bsef,efd->bsed', y, w2) + b2
        aff = jax.nn.sigmoid(jnp.einsum('bsd,de->bse', x, wa))
        topk_p, topk_i = jax.lax.top_k(aff, K)
        topk_p = topk_p / jnp.sum(topk_p, axis=-1, keepdims=True)
        combine = jnp.sum(jax.nn.one_hot(topk_i, E, dtype=x.dtype) * topk_p[..., None], axis=2)
        routed = jnp.einsum('bsed,bse->bsd', _experts_all(x, rg, rgb, rw1, rb1, rw2, rb2), combine)
        shared = jnp.sum(_experts_all(x, sg, sgb, sw1, sb1, sw2, sb2), axis=2)
        return x + shared + routed
    x = L0_attn_a_x
    x = x + _L0_attn_a_ref(_layernorm(x, axis=-1), L0_attn_a_wk, L0_attn_a_bk, L0_attn_a_wq, L0_attn_a_bq, L0_attn_a_wv, L0_attn_a_bv, L0_attn_a_wkl, L0_attn_a_bkl, L0_attn_a_wql, L0_attn_a_bql, L0_attn_a_wvl, L0_attn_a_bvl, L0_attn_a_wo, L0_attn_a_bo)
    x = x + _L0_ffn_ref(_layernorm(x, axis=-1), L0_ffn_wa, L0_ffn_rg, L0_ffn_rgb, L0_ffn_rw1, L0_ffn_rb1, L0_ffn_rw2, L0_ffn_rb2, L0_ffn_sg, L0_ffn_sgb, L0_ffn_sw1, L0_ffn_sb1, L0_ffn_sw2, L0_ffn_sb2)
    x = x + _L0_attn_b_ref(_layernorm(x, axis=-1), L0_attn_b_wq, L0_attn_b_wk, L0_attn_b_wv, L0_attn_b_wo, L0_attn_b_inv_freq)
    x = x + _L0_ffn_ref(_layernorm(x, axis=-1), L0_ffn_wa, L0_ffn_rg, L0_ffn_rgb, L0_ffn_rw1, L0_ffn_rb1, L0_ffn_rw2, L0_ffn_rb2, L0_ffn_sg, L0_ffn_sgb, L0_ffn_sw1, L0_ffn_sb1, L0_ffn_sw2, L0_ffn_sb2)
    return x

_drawn_inputs = setup_inputs


def setup_inputs(seed=0):
    import zlib

    import numpy as np

    out = dict(_drawn_inputs(seed))
    spreads = {'L0_ffn_rgb': (0.0, 0.8),
     'L0_ffn_rb1': (0.0, 0.8),
     'L0_ffn_rb2': (0.0, 0.1),
     'L0_ffn_sgb': (0.0, 0.8),
     'L0_ffn_sb1': (0.0, 0.8),
     'L0_ffn_sb2': (0.0, 0.1)}
    factors = {'L0_attn_a_wk': 8.0,
     'L0_attn_a_bk': 8.0,
     'L0_attn_a_wq': 8.0,
     'L0_attn_a_bq': 8.0,
     'L0_attn_a_wv': 3.364,
     'L0_attn_a_bv': 4.212,
     'L0_attn_a_wkl': 8.0,
     'L0_attn_a_bkl': 8.0,
     'L0_attn_a_wql': 8.0,
     'L0_attn_a_bql': 8.0,
     'L0_attn_b_inv_freq': 8.0,
     'L0_ffn_rg': 7.725,
     'L0_ffn_rw1': 7.542,
     'L0_ffn_rw2': 7.235,
     'L0_ffn_sg': 3.754,
     'L0_ffn_sw1': 3.628,
     'L0_ffn_sw2': 3.471}
    for name, (base, spread) in spreads.items():
        noise = np.random.default_rng([zlib.crc32(name.encode()), seed]).standard_normal(out[name].shape)
        drawn = base * np.exp(spread * noise) if base else spread * noise
        out[name] = jnp.asarray(drawn.astype(out[name].dtype))
    for name, factor in factors.items():
        out[name] = (out[name] * factor).astype(out[name].dtype)
    return out
```

```python
from contextlib import ExitStack

import concourse.bass as bass
from concourse import mybir

P = 128
F32 = mybir.dt.float32
BF16 = mybir.dt.bfloat16
I32 = mybir.dt.int32
U32 = mybir.dt.uint32
ALU = mybir.AluOpType
ACT = mybir.ActivationFunctionType
AX = mybir.AxisListType

B, T, D = 2, 1024, 256
TOK = B * T
NT = TOK // P
NC = D // P
CH = 512
NCH = TOK // CH
TPC = CH // P
EPS = 1e-5

HA = 16
DL = 128
HDA = DL // HA
QUAD = 4
NQ = B * HA // QUAD
QPB = NQ // B
PARTS = 3
COMBOS = PARTS * PARTS
KR = COMBOS * HDA
KM = KR + PARTS
NB = T // P
BIG = 1e30


def link_on(eng, sem, start=0):
    count = [start]

    def link(ins):
        count[0] = count[0] + 1
        ins.then_inc(sem, 1)
        eng.wait_ge(sem, count[0])

    return link


def constants(nc, ctx, tiles):
    ident, identb, mask_s, mask_t = tiles["ident"], tiles["identb"], tiles["mask_s"], tiles["mask_t"]
    with ExitStack() as c:
        cleared = c.enter_context(nc.semaphore("const_cleared"))
        made = c.enter_context(nc.semaphore("const_made"))
        block = c.enter_context(nc.Block())

        @block.gpsimd
        def _(pool):
            nc.gpsimd.memset(ident[:, :], 0.0).then_inc(cleared, 1)
            nc.gpsimd.memset(identb[:, :], 0.0).then_inc(cleared, 1)
            nc.gpsimd.memset(mask_s[:, :], 0.0).then_inc(cleared, 1)
            nc.gpsimd.memset(mask_t[:, :], 0.0).then_inc(cleared, 1)
            nc.gpsimd.memset(tiles["neg_half"][:, :], -0.5).then_inc(made, 1)
            pool.wait_ge(cleared, 4)
            for m in (ident, identb):
                nc.gpsimd.affine_select(out=m[:, :], in_=m[:, :], compare_op=ALU.not_equal, fill=1.0, base=0,
                                        pattern=[[-1, P]], channel_multiplier=1).then_inc(made, 1)
            nc.gpsimd.affine_select(out=mask_s[:, :], in_=mask_s[:, :], compare_op=ALU.is_ge, fill=-BIG, base=0,
                                    pattern=[[-1, P]], channel_multiplier=1).then_inc(made, 1)
            nc.gpsimd.affine_select(out=mask_t[:, :], in_=mask_t[:, :], compare_op=ALU.is_ge, fill=-BIG, base=0,
                                    pattern=[[1, P]], channel_multiplier=-1).then_inc(made, 1)
            nc.gpsimd.iota(tiles["experts"][:, :, :], [[0, NT], [1, E]], base=E, channel_multiplier=0,
                           allow_small_or_imprecise_dtypes=True).then_inc(made, 1)
            pool.wait_ge(made, 6)


def norm_statistics(nc, dve, pool_pow, x_sb, s, sem):
    st, small = s["st"], s["small"]
    mean, rstd, veps, r0, dif, cvs, tmp = (small[:, k, :] for k in range(7))
    with dve.Fori(0, NT) as i:
        nc.vector.bn_stats(st[:, bass.ds(i, 1), :], x_sb[:, bass.ds(i, 1), :]).then_inc(sem["stats"], 1)
    dve.wait_ge(sem["stats"], NT)
    link = link_on(dve, sem["dve_chain"])
    nc.vector.tensor_tensor(tmp, st[:, :, 1], st[:, :, 4], ALU.add)
    nc.vector.tensor_tensor(dif, st[:, :, 1], st[:, :, 4], ALU.subtract)
    link(nc.vector.tensor_tensor(cvs, st[:, :, 2], st[:, :, 5], ALU.add))
    nc.vector.tensor_scalar(mean, tmp, 0.5, None, ALU.mult)
    nc.vector.tensor_scalar(cvs, cvs, 1.0 / D, EPS, ALU.mult, ALU.add)
    link(nc.vector.tensor_tensor(dif, dif, dif, ALU.mult))
    nc.vector.scalar_tensor_tensor(veps, dif, 0.25, cvs, ALU.mult, ALU.add).then_inc(sem["veps"], 1)
    dve.wait_ge(sem["veps"], 1)
    dve.wait_ge(sem["pow"], 1)
    link(nc.vector.tensor_tensor(tmp, r0, r0, ALU.mult))
    link(nc.vector.tensor_tensor(tmp, tmp, veps, ALU.mult))
    link(nc.vector.tensor_scalar(tmp, tmp, -0.5, 1.5, ALU.mult, ALU.add))
    link(nc.vector.tensor_tensor(rstd, r0, tmp, ALU.mult))
    return mean, rstd


def fold_weights(nc, t, w):
    x_sb, ident = t["x"], t["ident"]
    with ExitStack() as c:
        sb = lambda n, s, d=F32: c.enter_context(nc.sbuf_tensor(n, s, d))
        sem = lambda n: c.enter_context(nc.semaphore(n))
        w1 = {k: sb(f"w1_{k}", [P, NC, D]) for k in "qkv"}
        w1t = {k: sb(f"w1t_{k}", [P, NC, D]) for k in "qkv"}
        w2 = {k: sb(f"w2_{k}", [P, NC, DL]) for k in "qkv"}
        bcol = sb("bcol", [P, 3, NC])
        blcol = sb("blcol", [P, 3, 1])
        tp = c.enter_context(nc.psum_tensor("fold_tp", [P, 3, NC, D], F32))
        fp = c.enter_context(nc.psum_tensor("fold_fp", [P, 3, 512], F32))
        loaded = {k: sem(f"fold_loaded_{k}") for k in "qkv"}
        bias_in = sem("fold_bias_in")
        turned, turned_out, folded, out = sem("fold_turned"), sem("fold_turned_out"), sem("fold_done"), sem("fold_out")
        block = c.enter_context(nc.Block())

        @block.sync
        def _(sp):
            for k in "qkv":
                sp.dma_start(w1[k][:, :, :], w[f"w{k}"].rearrange("(c p) n -> p c n", p=P)).then_inc(loaded[k], 16)
                sp.dma_start(w2[k][:, :, :], w[f"w{k}l"].rearrange("(c p) n -> p c n", p=P)).then_inc(loaded[k], 16)
            sp.dma_start(x_sb[:, :, :], w["x"].rearrange("b (i p) d -> p (b i) d", p=P)).then_inc(t["x_loaded"], 16)
            sp.dma_start(t["wo_a"][:, :], w["wo"]).then_inc(t["x_loaded"], 16)
            sp.dma_start(t["bo_a"][:, :], w["bo"].rearrange("(o n) -> o n", o=1).partition_broadcast(P)
                         ).then_inc(t["x_loaded"], 16)

        @block.scalar
        def _(act):
            for i, k in enumerate("qkv"):
                act.dma_start(bcol[:, i, :], w[f"b{k}"].rearrange("(c p) -> p c", p=P),
                              allow_slow_non_contiguous=True).then_inc(bias_in, 16)
                act.dma_start(blcol[:, i, :], w[f"b{k}l"].rearrange("(p o) -> p o", o=1)).then_inc(bias_in, 16)

        @block.tensor
        def _(pe):
            for i, k in enumerate("qkv"):
                pe.wait_ge(loaded[k], 32)
                for m in range(NC):
                    for n in range(NC):
                        ins = nc.tensor.transpose(tp[:, i, n, m * P:(m + 1) * P], w1[k][:, m, n * P:(n + 1) * P],
                                                  ident[:, :])
                ins.then_inc(turned, 1)
            pe.wait_ge(bias_in, 96)
            for i, k in enumerate("qkv"):
                pe.wait_ge(turned_out, i + 1)
                for m in range(NC):
                    for n in range(NC):
                        nc.tensor.matmul(fp[:, i, m * DL:(m + 1) * DL], w1t[k][:, n, m * P:(m + 1) * P],
                                         w2[k][:, n, :], start=n == 0, stop=n == NC - 1)
                for n in range(NC):
                    ins = nc.tensor.matmul(fp[:, i, NC * DL:NC * DL + 1], w2[k][:, n, :], bcol[:, i, n:n + 1],
                                           start=n == 0, stop=n == NC - 1)
                ins.then_inc(folded, 1)

        @block.vector
        def _(dve):
            for i, k in enumerate("qkv"):
                dve.wait_ge(turned, i + 1)
                nc.vector.tensor_copy(w1t[k][:, :, :], tp[:, i, :, :]).then_inc(turned_out, 1)
            for i, k in enumerate("qkv"):
                dve.wait_ge(folded, i + 1)
                nc.vector.tensor_copy(t["wf"][:, i, :, :], fp[:, i, 0:NC * DL].rearrange("p (c n) -> p c n", c=NC)
                                      ).then_inc(out, 1)
                nc.vector.tensor_tensor(t["bf"][:, i:i + 1], fp[:, i, NC * DL:NC * DL + 1], blcol[:, i, :],
                                        ALU.add).then_inc(out, 1)
            dve.wait_ge(out, 6)


def project_a(nc, t):
    x_sb, ident, wf, bf = t["x"], t["ident"], t["wf"], t["bf"]
    qs, ks = t["q_parts"], t["k_parts"]
    with ExitStack() as c:
        sb = lambda n, s, d=F32: c.enter_context(nc.sbuf_tensor(n, s, d))
        sem = lambda n: c.enter_context(nc.semaphore(n))
        s = {"st": sb("pa_st", [P, NT, 6]), "small": sb("pa_small", [P, 7, NT])}
        xn = sb("pa_xn", [P, 2 * TPC, D])
        xT = sb("pa_xT", [P, 2, NC, CH])
        rest = sb("pa_rest", [P, 2, CH])
        parts = sb("pa_parts", [P, 2, 2, PARTS, CH], BF16)
        vT = sb("pa_vT", [P, CH])
        xt_ps = c.enter_context(nc.psum_tensor("pa_xt", [P, NC, CH], F32))
        qk_ps = c.enter_context(nc.psum_tensor("pa_qk", [P, 2, CH], F32))
        v_ps = c.enter_context(nc.psum_tensor("pa_v", [P, CH], F32))
        vt_ps = c.enter_context(nc.psum_tensor("pa_vt", [P, CH], F32))
        ns = {k: sem(f"pa_{k}") for k in ("stats", "dve_chain", "veps", "pow")}
        xn_ready, xt_done, xT_ready = sem("pa_xn_ready"), sem("pa_xt_done"), sem("pa_xT_ready")
        qk_done, qk_free = sem("pa_qk_done"), sem("pa_qk_free")
        high, mid, low = sem("pa_high"), sem("pa_mid"), sem("pa_low")
        v_done, vT_ready, vt_done, v_out = sem("pa_v_done"), sem("pa_vT_ready"), sem("pa_vt_done"), sem("pa_v_out")
        saved = [sem("pa_saved0"), sem("pa_saved1")]
        block = c.enter_context(nc.Block())

        @block.gpsimd
        def _(pool):
            pool.wait_ge(ns["veps"], 1)
            nc.gpsimd.tensor_tensor(s["small"][:, 3, :], s["small"][:, 2, :], t["neg_half"][:, :], ALU.pow
                                    ).then_inc(ns["pow"], 1)

        @block.vector
        def _(dve):
            dve.wait_ge(t["x_loaded"], 48)
            mean, rstd = norm_statistics(nc, dve, None, x_sb, s, ns)
            for j in range(NCH):
                u = j % 2
                for k in range(TPC):
                    i = j * TPC + k
                    if j >= 2:
                        dve.wait_ge(xt_done, j - 1)
                    nc.vector.tensor_scalar(xn[:, u * TPC + k, :], x_sb[:, i, :], mean[:, i:i + 1], rstd[:, i:i + 1],
                                            ALU.subtract, ALU.mult).then_inc(xn_ready, 1)
                for g in range(2):
                    n = 2 * j + g
                    dve.wait_ge(high, n + 1)
                    if n >= 2:
                        dve.wait_ge(low, n - 1)
                    nc.vector.scalar_tensor_tensor(rest[:, g, :], qk_ps[:, g, :], bf[:, g:g + 1],
                                                   parts[:, u, g, 0, :], ALU.add, ALU.subtract).then_inc(qk_free, 1)
                for g in range(2):
                    n = 2 * j + g
                    dve.wait_ge(mid, n + 1)
                    nc.vector.tensor_tensor(parts[:, u, g, 2, :], rest[:, g, :], parts[:, u, g, 1, :],
                                            ALU.subtract).then_inc(low, 1)
                dve.wait_ge(vt_done, j + 1)
                b, k0 = j * TPC // NB, j * TPC % NB
                nc.vector.tensor_copy(t["v"][:, b * QPB:(b + 1) * QPB, k0:k0 + TPC, :],
                                      vt_ps[:, :].rearrange("p (i q n) -> p q i n", i=TPC, q=QPB)).then_inc(v_out, 1)

        @block.tensor
        def _(pe):
            for j in range(NCH):
                u = j % 2
                for k in range(TPC):
                    pe.wait_ge(xn_ready, j * TPC + k + 1)
                    if j >= 1:
                        pe.wait_ge(xT_ready, 2 * j)
                    for m in range(NC):
                        ins = nc.tensor.transpose(xt_ps[:, m, k * P:(k + 1) * P], xn[:, u * TPC + k, m * P:(m + 1) * P],
                                                  ident[:, :])
                ins.then_inc(xt_done, 1)
                pe.wait_ge(xT_ready, 2 * j + 2)
                if j >= 1:
                    pe.wait_ge(qk_free, 2 * j)
                    pe.wait_ge(vT_ready, j)
                for g in range(3):
                    dst = v_ps[:, :] if g == 2 else qk_ps[:, g, :]
                    for m in range(NC):
                        ins = nc.tensor.matmul(dst, wf[:, g, m, :], xT[:, u, m, :], start=m == 0, stop=m == NC - 1)
                    ins.then_inc(v_done if g == 2 else qk_done, 1)
                pe.wait_ge(vT_ready, j + 1)
                if j >= 1:
                    pe.wait_ge(v_out, j)
                for k in range(TPC):
                    ins = nc.tensor.transpose(vt_ps[:, k * P:(k + 1) * P], vT[:, k * P:(k + 1) * P], ident[:, :])
                ins.then_inc(vt_done, 1)

        @block.scalar
        def _(act):
            for j in range(NCH):
                u = j % 2
                act.wait_ge(xt_done, j + 1)
                if j >= 2:
                    act.wait_ge(v_done, j - 1)
                for m in range(NC):
                    nc.scalar.activation(xT[:, u, m, :], xt_ps[:, m, :], ACT.Copy).then_inc(xT_ready, 1)
                for g in range(2):
                    act.wait_ge(qk_done, 2 * j + g + 1)
                    if j >= 2:
                        act.wait_ge(saved[u], 16 * (5 + 3) * (j // 2))
                    nc.scalar.activation(parts[:, u, g, 0, :], qk_ps[:, g, :], ACT.Identity,
                                         bias=bf[:, g:g + 1]).then_inc(high, 1)
                act.wait_ge(v_done, j + 1)
                if j >= 1:
                    act.wait_ge(vt_done, j)
                nc.scalar.activation(vT[:, :], v_ps[:, :], ACT.Identity, bias=bf[:, 2:3]).then_inc(vT_ready, 1)
                for g in range(2):
                    act.wait_ge(qk_free, 2 * j + g + 1)
                    nc.scalar.activation(parts[:, u, g, 1, :], rest[:, g, :], ACT.Copy).then_inc(mid, 1)

        @block.sync
        def _(sp):
            for j in range(NCH):
                u, b, t0 = j % 2, j * CH // T, j * CH % T
                for g, (dst, n) in enumerate(((qs, 5), (ks, 3))):
                    sp.wait_ge(mid, 2 * j + g + 1)
                    sp.wait_ge(low, 2 * j + g + 1)
                    for r in range(n):
                        sp.dma_start(dst[b * HA:(b + 1) * HA, r, :, t0:t0 + CH], parts[:, u, g, r % PARTS, :]).then_inc(saved[u], 16)
            for u in range(2):
                sp.wait_ge(saved[u], 16 * 8 * NCH // 2)


PIECES1 = [(tb, s0, min(s0 + CH, (tb + 1) * P)) for tb in range(NB) for s0 in range(0, (tb + 1) * P, CH)]
GROUPS2 = [(c, sb) for c in range(T // CH) for sb in range((c + 1) * CH // P)]
N1 = QUAD * len(PIECES1)
NG = len(GROUPS2)
N2 = QUAD * NG
FIRST_GROUPS = NG - 2
RS = 3


def share(g):
    per = -(-N1 // FIRST_GROUPS)
    return range(min(g * per, N1), min((g + 1) * per, N1)) if g < FIRST_GROUPS else range(0)


def piece1(n):
    h, k = divmod(n, len(PIECES1))
    tb, s0, s1 = PIECES1[k]
    col = tb if s0 == 0 else NB + tb - CH // P
    return h, tb, s0, s1, col


def attention_a(nc, t):
    qs, ks, v_all, identb, ident = t["q_parts"], t["k_parts"], t["v"], t["identb"], t["ident"]
    att = t["att"]
    NM = NB + NB - CH // P
    with ExitStack() as c:
        sb = lambda n, s, d=F32: c.enter_context(nc.sbuf_tensor(n, s, d))
        sem = lambda n: c.enter_context(nc.semaphore(n))
        qst = sb("qst", [KM, 2, QUAD, T], BF16)
        kst = sb("kst", [KM, 2, QUAD, T], BF16)
        vq = sb("vq", [P, 2, NB, QUAD, 32])
        pt = sb("pt", [P, RS, QUAD, CH])
        mx = sb("mx", [P, QUAD, NM])
        mrest = sb("mrest", [P, QUAD, NB])
        mparts = sb("mparts", [P, PARTS, QUAD, NB], BF16)
        mrow = sb("mrow", [PARTS * QUAD * NB, P], BF16)
        oT = sb("oT", [P, CH])
        rden = sb("rden", [P, TPC, QUAD])
        s1 = [c.enter_context(nc.psum_tensor(f"s1_{i}", [P, CH], F32)) for i in range(RS)]
        st = [c.enter_context(nc.psum_tensor(f"st_{i}", [P, CH], F32)) for i in range(RS)]
        o_ps = c.enter_context(nc.psum_tensor("o_ps", [P, CH], F32))
        tr = c.enter_context(nc.psum_tensor("tr", [P, CH], F32))
        rows_set, v_set, bias_added = sem("aa_rows_set"), sem("aa_v_set"), sem("aa_bias_added")
        stack = [sem("aa_stack0"), sem("aa_stack1")]
        s1_done, s1_used = sem("aa_s1_done"), sem("aa_s1_used")
        max_chain, rden_ready = sem("aa_max_chain"), sem("aa_rden_ready")
        mparts_ready, mt_done, mrow_ready = sem("aa_mparts"), sem("aa_mt_done"), sem("aa_mrow_ready")
        mrow_in = [sem("aa_mrow_in0"), sem("aa_mrow_in1")]
        st_done, exp_done, av_done = sem("aa_st_done"), sem("aa_exp_done"), sem("aa_av_done")
        v_ready, oT_ready, ot_done, norm_done = (sem("aa_v_ready"), sem("aa_oT_ready"), sem("aa_ot_done"),
                                                 sem("aa_norm_done"))
        block = c.enter_context(nc.Block())
        STACK = 16 * 2 * PARTS
        MROW = 16 * PARTS

        LINKS = 4

        def quads(eng, body):
            body(0, 0, 0, True, False)
            with eng.Fori(0, NQ // 2 - 1) as i:
                body(i * 2 + 1, i, 1, False, False)
                body(i * 2 + 2, i + 1, 0, False, False)
            body(NQ - 1, NQ // 2 - 1, 1, False, True)

        @block.sync
        def _(sp):
            def load(q, u):
                for r in range(PARTS):
                    sp.dma_start(qst[r * PARTS * HDA:(r + 1) * PARTS * HDA, u, :, :],
                                 qs[bass.ds(q * QUAD, QUAD), r:r + PARTS, :, :].rearrange("h r d t -> (r d) h t")
                                 ).then_inc(stack[u], 16)
                    sp.dma_start(kst[r * PARTS * HDA:(r + 1) * PARTS * HDA, u, :, :],
                                 ks[bass.ds(q * QUAD, QUAD), :, :, :].rearrange("h r d t -> (r d) h t")
                                 ).then_inc(stack[u], 16)

            def max_rows(q, u):
                sp.wait_ge(mrow_ready, q + 1)
                n = QUAD * NB
                for r in range(PARTS):
                    sp.dma_start(qst[KR + r:KR + r + 1, u, :, :].rearrange("o h (k p) -> o (h k) p", p=P),
                                 mrow[r * n:(r + 1) * n, :]).then_inc(mrow_in[u], 16)

            def step(q, u):
                max_rows(q + 1, 1 - u)
                sp.wait_ge(st_done, (q + 1) * N2)
                load(q + 2, u)

            sp.wait_ge(rows_set, 2)
            load(0, 0)
            load(1, 1)
            max_rows(0, 0)
            with sp.Fori(0, NQ // 2 - 1) as i:
                step(i * 2, 0)
                step(i * 2 + 1, 1)
            max_rows(NQ - 1, 1)
            for u in range(2):
                sp.wait_ge(mrow_in[u], MROW * NQ // 2)
                sp.wait_ge(stack[u], STACK * NQ // 2)

        @block.gpsimd
        def _(pool):
            nc.gpsimd.memset(kst[64:KM, :, :, :], 1.0).then_inc(rows_set, 1)
            nc.gpsimd.memset(qst[64:KM, :, :, :], 0.0).then_inc(rows_set, 1)
            pool.wait_ge(rows_set, 2)
            nc.gpsimd.memset(vq[:, :, :, :, :], 0.0).then_inc(v_set, 1)
            pool.wait_ge(v_set, 1)
            nc.gpsimd.memset(vq[:, :, :, :, HDA:HDA + 1], 1.0).then_inc(v_set, 1)
            pool.wait_ge(v_set, 2)

            def copy_v(q, u):
                src = v_all[:, q, :, :] if isinstance(q, int) else v_all[:, bass.ds(q, 1), :, :]
                src = src.rearrange("p (o k) (h d) -> p (o k) h d" if isinstance(q, int) else
                                    "p o k (h d) -> p (o k) h d", h=QUAD, **({"o": 1} if isinstance(q, int) else {}))
                nc.gpsimd.tensor_copy(vq[:, u, :, :, 0:HDA], src).then_inc(v_ready, 1)

            copy_v(0, 0)
            copy_v(1, 1)
            with pool.Fori(0, NT) as i:
                xs = t["x"][:, bass.ds(i, 1), :]
                nc.gpsimd.tensor_tensor(xs, xs, t["bo_a"][:, :].rearrange("p (o n) -> p o n", o=1), ALU.add
                                        ).then_inc(bias_added, 1)
            with pool.Fori(0, NQ // 2 - 1) as i:
                for u in range(2):
                    pool.wait_ge(av_done, (i * 2 + 1 + u) * NG)
                    copy_v(i * 2 + 2 + u, u)
            pool.wait_ge(bias_added, NT)

        @block.tensor
        def _(pe):
            def scores(q, u, n):
                h, tb, k0, k1, _col = piece1(n)
                if not (isinstance(q, int) and q == 0 and n < RS):
                    pe.wait_ge(s1_used, q * N1 + (n - RS + 1))
                diagonal = k1 == (tb + 1) * P
                ins = nc.tensor.matmul(s1[n % RS][:, 0:k1 - k0], qst[0:KR, u, h, tb * P:(tb + 1) * P],
                                       kst[0:KR, u, h, k0:k1], start=True, stop=not diagonal)
                if diagonal:
                    ins = nc.tensor.matmul(s1[n % RS][:, k1 - k0 - P:k1 - k0], identb[:, :], t["mask_s"][:, :],
                                           start=False, stop=True)
                ins.then_inc(s1_done, 1)

            def scores_t(q, u, g, h):
                c_, kb = GROUPS2[g]
                t0 = max(c_ * CH, kb * P)
                w = (c_ + 1) * CH - t0
                n = g * QUAD + h
                if not (isinstance(q, int) and q == 0 and n < RS):
                    pe.wait_ge(exp_done, q * N2 + (n - RS + 1))
                diagonal = kb * P >= c_ * CH
                ins = nc.tensor.matmul(st[n % RS][:, 0:w], kst[:, u, h, kb * P:(kb + 1) * P],
                                       qst[:, u, h, t0:t0 + w], start=True, stop=not diagonal)
                if diagonal:
                    ins = nc.tensor.matmul(st[n % RS][:, 0:P], identb[:, :], t["mask_t"][:, :],
                                           start=False, stop=True)
                ins.then_inc(st_done, 1)

            def values(q, u, g):
                c_, kb = GROUPS2[g]
                w = (c_ + 1) * CH - max(c_ * CH, kb * P)
                pe.wait_ge(exp_done, q * N2 + (g + 1) * QUAD)
                if kb == 0:
                    pe.wait_ge(v_ready, q + 1)
                    if not (isinstance(q, int) and q == 0 and c_ == 0):
                        pe.wait_ge(oT_ready, q * 2 + c_)
                last = kb == (c_ + 1) * CH // P - 1
                for h in range(QUAD):
                    ins = nc.tensor.matmul(o_ps[32 * h:32 * h + 32, CH - w:CH], vq[:, u, kb, h, :],
                                           pt[:, g % RS, h, 0:w], start=kb == 0, stop=last, skip_group_check=True)
                ins.then_inc(av_done, 1)

            def turn_output(q, c_):
                pe.wait_ge(oT_ready, q * 2 + (c_ + 1))
                for k in range(TPC):
                    ins = nc.tensor.transpose(tr[:, k * P:(k + 1) * P], oT[:, k * P:(k + 1) * P], ident[:, :])
                ins.then_inc(ot_done, 1)

            def turn_maxima(q):
                pe.wait_ge(mparts_ready, q + 1)
                n = PARTS * QUAD * NB
                nc.tensor.transpose(tr[0:n, 0:P // 2].bitcast(BF16),
                                    mparts[:, :, :, :].rearrange("p r h k -> p (r h k)"), identb[:, :]
                                    ).then_inc(mt_done, 1)

            def quad(q, k, u, first, last):
                pe.wait_ge(mrow_in[u], (k + 1) * MROW)
                if not last:
                    pe.wait_ge(stack[1 - u], (k + u + 1) * STACK)
                for g in range(NG):
                    todo = [] if last else list(share(g))
                    per = -(-len(todo) // QUAD)
                    for h in range(QUAD):
                        scores_t(q, u, g, h)
                        for n in todo[h * per:(h + 1) * per]:
                            scores(q + 1, 1 - u, n)
                    if g > 0:
                        values(q, u, g - 1)
                    elif not first:
                        values(q - 1, 1 - u, NG - 1)
                    if g == 1 and not first:
                        pe.wait_ge(mrow_ready, q + 1)
                        turn_output(q - 1, 1)
                    if g == 5:
                        if first:
                            pe.wait_ge(mrow_ready, 1)
                        else:
                            pe.wait_ge(norm_done, q * 2)
                        turn_output(q, 0)
                    if g == NG - 2 and not last:
                        pe.wait_ge(norm_done, q * 2 + 1)
                        turn_maxima(q + 1)
                if last:
                    values(q, u, NG - 1)
                    pe.wait_ge(norm_done, q * 2 + 1)
                    turn_output(q, 1)

            pe.wait_ge(stack[0], STACK)
            for n in range(N1):
                scores(0, 0, n)
            turn_maxima(0)
            quads(pe, quad)

        @block.scalar
        def _(act):
            nc.scalar.preload_act_table(ACT.Exp)

            def move_maxima(q, k, u):
                act.wait_ge(mt_done, q + 1)
                if not (isinstance(q, int) and q == 0):
                    act.wait_ge(mrow_in[1 - u], (k + u) * MROW)
                n = PARTS * QUAD * NB
                nc.scalar.activation(mrow[:, :], tr[0:n, 0:P // 2].bitcast(BF16), ACT.Copy).then_inc(mrow_ready, 1)

            def move_output(q, c_):
                act.wait_ge(av_done, q * NG + (NG if c_ else CH // P))
                if not (isinstance(q, int) and q == 0 and c_ == 0):
                    act.wait_ge(ot_done, q * 2 + c_)
                nc.scalar.activation(oT[:, :], o_ps[:, :], ACT.Copy).then_inc(oT_ready, 1)

            def quad(q, k, u, first, last):
                for g in range(NG):
                    c_, kb = GROUPS2[g]
                    w = (c_ + 1) * CH - max(c_ * CH, kb * P)
                    if not (first and g < RS):
                        act.wait_ge(av_done, q * NG + (g - RS + 1))
                    for h in range(QUAD):
                        n = g * QUAD + h
                        act.wait_ge(st_done, q * N2 + (n + 1))
                        nc.scalar.activation(pt[:, g % RS, h, 0:w], st[n % RS][:, 0:w], ACT.Exp,
                                             scale=float(HDA) ** -0.5).then_inc(exp_done, 1)
                    if g == 0 and not first:
                        move_output(q - 1, 1)
                    if g == CH // P:
                        move_output(q, 0)
                    if g == NG - 2 and not last:
                        move_maxima(q + 1, k + u, 1 - u)
                if last:
                    move_output(q, 1)

            move_maxima(0, 0, 0)
            quads(act, quad)

        @block.vector
        def _(dve):
            def maximum(q, n):
                h, tb, k0, k1, col = piece1(n)
                dve.wait_ge(s1_done, q * N1 + (n + 1))
                nc.vector.reduce_max(mx[:, h, col:col + 1], s1[n % RS][:, 0:k1 - k0], AX.X).then_inc(s1_used, 1)

            def split_maxima(q):
                dve.wait_ge(s1_used, q * N1 + N1)
                link = link_on(dve, max_chain, q * LINKS)
                two = CH // P
                link(nc.vector.tensor_tensor(mx[:, :, two:NB], mx[:, :, two:NB], mx[:, :, NB:NM], ALU.max))
                if not (isinstance(q, int) and q == 0):
                    dve.wait_ge(mt_done, q)
                link(nc.vector.tensor_scalar(mparts[:, 0, :, :], mx[:, :, 0:NB], -1.0, None, ALU.mult))
                link(nc.vector.scalar_tensor_tensor(mrest[:, :, :], mx[:, :, 0:NB], -1.0, mparts[:, 0, :, :],
                                                    ALU.mult, ALU.subtract))
                link(nc.vector.tensor_copy(mparts[:, 1, :, :], mrest[:, :, :]))
                nc.vector.tensor_tensor(mparts[:, 2, :, :], mrest[:, :, :], mparts[:, 1, :, :], ALU.subtract
                                        ).then_inc(mparts_ready, 1)

            def normalise(q, c_):
                dve.wait_ge(ot_done, q * 2 + (c_ + 1))
                o = tr[:, :].rearrange("p (k h n) -> p k h n", k=TPC, h=QUAD)
                nc.vector.reciprocal(rden[:, :, :], o[:, :, :, HDA]).then_inc(rden_ready, 1)
                dve.wait_ge(rden_ready, q * 2 + (c_ + 1))
                dst = att[:, bass.ds((q * 2 + c_) * TPC * QUAD, TPC * QUAD), :]
                nc.vector.tensor_tensor(dst, o[:, :, :, 0:HDA].rearrange("p k h d -> p (k h) d"),
                                        rden[:, :, :].rearrange("p k (h o) -> p (k h) o", o=1)
                                        .broadcast_to([P, TPC * QUAD, HDA]), ALU.mult).then_inc(norm_done, 1)

            def quad(q, k, u, first, last):
                for g in range(NG):
                    if not last:
                        for n in share(g):
                            maximum(q + 1, n)
                    if g == 1 and not first:
                        normalise(q - 1, 1)
                    if g == 5:
                        normalise(q, 0)
                    if g == FIRST_GROUPS and not last:
                        split_maxima(q + 1)
                if last:
                    normalise(q, 1)

            for n in range(N1):
                maximum(0, n)
            split_maxima(0)
            quads(dve, quad)
            dve.wait_ge(norm_done, 2 * NQ)


def output_a(nc, t):
    x_sb, ident, att = t["x"], t["ident"], t["att"]
    with ExitStack() as c:
        sb = lambda n, s, d=F32: c.enter_context(nc.sbuf_tensor(n, s, d))
        sem = lambda n: c.enter_context(nc.semaphore(n))
        a = sb("oa_a", [P, 2, DL])
        aT = sb("oa_aT", [P, 2, DL])
        tp = [c.enter_context(nc.psum_tensor(f"oa_tp{i}", [P, CH], F32)) for i in range(2)]
        op = [c.enter_context(nc.psum_tensor(f"oa_op{i}", [P, CH], F32)) for i in range(2)]
        picked, turned, ready, done, added = (sem("oa_picked"), sem("oa_turned"), sem("oa_ready"), sem("oa_done"),
                                              sem("oa_added"))
        block = c.enter_context(nc.Block())
        view = att[:, :, :].rearrange("p (b g c k h) d -> p b c k g (h d)", b=B, g=QPB, c=T // CH, k=TPC)

        @block.gpsimd
        def _(pool):
            for i in range(NT):
                b, r = divmod(i, NB)
                if i >= 2:
                    pool.wait_ge(turned, i - 1)
                nc.gpsimd.tensor_copy(a[:, i % 2, :].rearrange("p (g n) -> p g n", g=QPB),
                                      view[:, b, r // TPC, r % TPC, :, :]).then_inc(picked, 1)

        @block.tensor
        def _(pe):
            def product(i):
                pe.wait_ge(ready, i + 1)
                if i >= 2:
                    pe.wait_ge(added, i - 1)
                nc.tensor.matmul(op[i % 2][:, 0:D], aT[:, i % 2, :], t["wo_a"][:, :], start=True, stop=True
                                 ).then_inc(done, 1)
            for i in range(NT):
                pe.wait_ge(picked, i + 1)
                if i >= 2:
                    pe.wait_ge(ready, i - 1)
                nc.tensor.transpose(tp[i % 2][:, 0:P], a[:, i % 2, :], ident[:, :]).then_inc(turned, 1)
                if i:
                    product(i - 1)
            product(NT - 1)

        @block.scalar
        def _(act):
            for i in range(NT):
                act.wait_ge(turned, i + 1)
                if i >= 2:
                    act.wait_ge(done, i - 1)
                nc.scalar.activation(aT[:, i % 2, :], tp[i % 2][:, 0:P], ACT.Copy).then_inc(ready, 1)

        @block.vector
        def _(dve):
            for i in range(NT):
                dve.wait_ge(done, i + 1)
                nc.vector.tensor_tensor(x_sb[:, i, :], op[i % 2][:, 0:D], x_sb[:, i, :], ALU.add).then_inc(added, 1)
            dve.wait_ge(added, NT)


E, SH, F = 16, 2, 128
NE = SH + E


def normalise_and_turn(nc, t, tag, keep_norm):
    x_sb, ident, xT = t["x"], t["ident"], t["xT"]
    with ExitStack() as c:
        sb = lambda n, s, d=F32: c.enter_context(nc.sbuf_tensor(tag + n, s, d))
        sem = lambda n: c.enter_context(nc.semaphore(tag + n))
        s = {"st": sb("st", [P, NT, 6]), "small": sb("small", [P, 7, NT])}
        xn = sb("xn", [P, 2 * TPC, D])
        xt_ps = c.enter_context(nc.psum_tensor(tag + "xt", [P, 2, NC, CH], F32))
        ns = {k: sem(k) for k in ("stats", "dve_chain", "veps", "pow")}
        xn_ready, xt_done, xT_ready, kept = sem("xn_ready"), sem("xt_done"), sem("xT_ready"), sem("kept")
        block = c.enter_context(nc.Block())

        @block.gpsimd
        def _(pool):
            pool.wait_ge(ns["veps"], 1)
            nc.gpsimd.tensor_tensor(s["small"][:, 3, :], s["small"][:, 2, :], t["neg_half"][:, :], ALU.pow
                                    ).then_inc(ns["pow"], 1)
            if keep_norm:
                for i in range(NT):
                    pool.wait_ge(xn_ready, i + 1)
                    nc.gpsimd.tensor_tensor(x_sb[:, i, :], x_sb[:, i, :], xn[:, i % (2 * TPC), :], ALU.add
                                            ).then_inc(kept, 1)
                pool.wait_ge(kept, NT)

        @block.vector
        def _(dve):
            mean, rstd = norm_statistics(nc, dve, None, x_sb, s, ns)
            for i in range(NT):
                j = i // TPC
                if j >= 2:
                    dve.wait_ge(xt_done, j - 1)
                    if keep_norm:
                        dve.wait_ge(kept, i - 2 * TPC + 1)
                nc.vector.tensor_scalar(xn[:, i % (2 * TPC), :], x_sb[:, i, :], mean[:, i:i + 1], rstd[:, i:i + 1],
                                        ALU.subtract, ALU.mult).then_inc(xn_ready, 1)

        @block.tensor
        def _(pe):
            for j in range(NCH):
                for k in range(TPC):
                    i = j * TPC + k
                    pe.wait_ge(xn_ready, i + 1)
                    if j >= 2:
                        pe.wait_ge(xT_ready, NC * (j - 1))
                    for m in range(NC):
                        ins = nc.tensor.transpose(xt_ps[:, j % 2, m, k * P:(k + 1) * P],
                                                  xn[:, i % (2 * TPC), m * P:(m + 1) * P], ident[:, :])
                ins.then_inc(xt_done, 1)

        @block.scalar
        def _(act):
            for j in range(NCH):
                act.wait_ge(xt_done, j + 1)
                for m in range(NC):
                    nc.scalar.activation(xT[:, m, j * CH:(j + 1) * CH], xt_ps[:, j % 2, m, :], ACT.Copy
                                         ).then_inc(xT_ready, 1)


def route(nc, t, w, tag):
    ident, xT, comb = t["ident"], t["xT"], t["comb"]
    with ExitStack() as c:
        sb = lambda n, s, d=F32: c.enter_context(nc.sbuf_tensor(tag + n, s, d))
        sem = lambda n: c.enter_context(nc.semaphore(tag + n))
        wa = sb("wa", [P, NC, E])
        lgT = sb("lgT", [E, TOK])
        aff, eq, key, second = (sb(n, [P, NT, E]) for n in ("aff", "eq", "key", "second"))
        one = [sb("one0", [P, NT, E]), sb("one1", [P, NT, E])]
        top = sb("top", [P, 2, NT])
        idx = sb("idx", [P, NT])
        den = sb("den", [P, NT])
        cT = sb("cT", [E, TOK])
        rb2 = sb("rb2", [E, D])
        sb2 = sb("sb2", [P, SH, D])
        lg_ps = c.enter_context(nc.psum_tensor(tag + "lg", [P, NCH, CH], F32))
        tp = c.enter_context(nc.psum_tensor(tag + "tp", [P, CH], F32))
        bp = [c.enter_context(nc.psum_tensor(tag + f"bp{i}", [P, CH], F32)) for i in range(2)]
        loaded, lg_done, lg_out, turned = sem("loaded"), sem("lg_done"), sem("lg_out"), sem("turned")
        exp_done, chain, comb_ready = sem("exp_done"), sem("chain"), sem("comb_ready")
        cT_done, cT_ready, b2_done, b2_added = sem("cT_done"), sem("cT_ready"), sem("b2_done"), sem("b2_added")
        block = c.enter_context(nc.Block())

        @block.sync
        def _(sp):
            sp.dma_start(wa[:, :, :], w["wa"].rearrange("(c p) e -> p c e", p=P)).then_inc(loaded, 16)
            sp.dma_start(rb2[:, :], w["rb2"]).then_inc(loaded, 16)
            for e in range(SH):
                sp.dma_start(sb2[:, e, :], w["sb2"][e:e + 1, :].partition_broadcast(P)).then_inc(loaded, 16)
            sp.wait_ge(loaded, 16 * (2 + SH))

        @block.tensor
        def _(pe):
            pe.wait_ge(loaded, 16 * (2 + SH))
            for j in range(NCH):
                for m in range(NC):
                    ins = nc.tensor.matmul(lg_ps[0:E, j, :], wa[:, m, :], xT[:, m, j * CH:(j + 1) * CH],
                                           start=m == 0, stop=m == NC - 1)
                ins.then_inc(lg_done, 1)
            for i in range(NT):
                pe.wait_ge(lg_out, i // TPC + 1)
                ins = nc.tensor.transpose(tp[:, i * E:(i + 1) * E], lgT[:, i * P:(i + 1) * P], ident[0:E, 0:E])
            ins.then_inc(turned, 1)
            pe.wait_ge(comb_ready, 1)
            for i in range(NT):
                ins = nc.tensor.transpose(lg_ps[0:E, i // TPC, i % TPC * P:(i % TPC + 1) * P], comb[:, SH:NE, i],
                                          ident[:, :])
                if i % TPC == TPC - 1:
                    ins.then_inc(cT_done, 1)
            for i in range(NT):
                pe.wait_ge(cT_ready, i // TPC + 1)
                if i >= 2:
                    pe.wait_ge(b2_added, i - 1)
                nc.tensor.matmul(bp[i % 2][:, 0:D], cT[:, i * P:(i + 1) * P], rb2[:, :], start=True, stop=True
                                 ).then_inc(b2_done, 1)

        @block.scalar
        def _(act):
            nc.scalar.preload_act_table(ACT.Exp)
            for j in range(NCH):
                act.wait_ge(lg_done, j + 1)
                nc.scalar.activation(lgT[:, j * CH:(j + 1) * CH], lg_ps[0:E, j, :], ACT.Copy).then_inc(lg_out, 1)
            act.wait_ge(turned, 1)
            nc.scalar.activation(aff[:, :, :], tp[:, 0:NT * E].rearrange("p (i e) -> p i e", e=E), ACT.Exp,
                                 scale=-1.0).then_inc(exp_done, 1)
            for j in range(NCH):
                act.wait_ge(cT_done, j + 1)
                nc.scalar.activation(cT[:, j * CH:(j + 1) * CH], lg_ps[0:E, j, :], ACT.Copy).then_inc(cT_ready, 1)

        @block.vector
        def _(dve):
            link = link_on(dve, chain)
            wide = lambda a: a.rearrange("p (i o) -> p i o", o=1).broadcast_to([P, NT, E])
            dve.wait_ge(exp_done, 1)
            link(nc.vector.tensor_scalar(aff[:, :, :], aff[:, :, :], 1.0, None, ALU.add))
            link(nc.vector.reciprocal(aff[:, :, :], aff[:, :, :]))
            src = aff
            for r in range(2):
                link(nc.vector.tensor_reduce(top[:, r, :], src[:, :, :], AX.X, ALU.max))
                link(nc.vector.tensor_tensor(eq[:, :, :], src[:, :, :], wide(top[:, r, :]), ALU.is_equal))
                link(nc.vector.scalar_tensor_tensor(key[:, :, :], eq[:, :, :], -float(E), t["experts"][:, :, :],
                                                    ALU.mult, ALU.add))
                link(nc.vector.tensor_reduce(idx[:, :], key[:, :, :], AX.X, ALU.min))
                link(nc.vector.tensor_tensor(one[r][:, :, :], key[:, :, :], wide(idx[:, :]), ALU.is_equal))
                if r == 0:
                    link(nc.vector.scalar_tensor_tensor(second[:, :, :], one[0][:, :, :], -4.0, aff[:, :, :],
                                                        ALU.mult, ALU.add))
                    src = second
            link(nc.vector.tensor_tensor(den[:, :], top[:, 0, :], top[:, 1, :], ALU.add))
            link(nc.vector.reciprocal(den[:, :], den[:, :]))
            for r in range(2):
                link(nc.vector.tensor_tensor(top[:, r, :], top[:, r, :], den[:, :], ALU.mult))
                link(nc.vector.tensor_tensor(one[r][:, :, :], one[r][:, :, :], wide(top[:, r, :]), ALU.mult))
            nc.vector.memset(comb[:, 0:SH, :], 1.0)
            nc.vector.tensor_tensor(comb[:, SH:NE, :].rearrange("p e i -> p i e"), one[0][:, :, :], one[1][:, :, :],
                                    ALU.add).then_inc(comb_ready, 1)
            for i in range(NT):
                for e in range(SH):
                    link(nc.vector.tensor_tensor(t["x"][:, i, :], t["x"][:, i, :], sb2[:, e, :], ALU.add))
            for i in range(NT):
                dve.wait_ge(b2_done, i + 1)
                nc.vector.tensor_tensor(t["x"][:, i, :], bp[i % 2][:, 0:D], t["x"][:, i, :], ALU.add
                                        ).then_inc(b2_added, 1)
            dve.wait_ge(b2_added, NT)


def experts(nc, t, w, tag):
    x_sb, xT, comb = t["x"], t["xT"], t["comb"]
    with ExitStack() as c:
        sb = lambda n, s, d=F32: c.enter_context(nc.sbuf_tensor(tag + n, s, d))
        sem = lambda n: c.enter_context(nc.semaphore(tag + n))
        up = sb("up", [P, 2, 2, NC, F])
        down = sb("down", [P, 2, D])
        bias = sb("bias", [P, 2, 2])
        gel = sb("gel", [P, 2, CH])
        y = sb("y", [P, 2, CH])
        g_ps = [c.enter_context(nc.psum_tensor(tag + f"g{i}", [P, 2, CH], F32)) for i in range(2)]
        o_ps = [c.enter_context(nc.psum_tensor(tag + f"o{i}", [P, 2, 2, D], F32)) for i in range(2)]
        w_in = [sem("w_in0"), sem("w_in1")]
        gu_done, gel_ready, y_ready, o_done, added = sem("gu"), sem("gel"), sem("y"), sem("o"), sem("added")
        block = c.enter_context(nc.Block())
        LOADS = 16 * 5

        def each_expert(eng, body):
            for n in range(SH):
                body(n, 0, n, n, "s")
            with eng.Fori(0, E // 2) as i:
                for u in range(2):
                    body(i * 2 + SH + u, i + 1, u, i * 2 + u, "r")

        @block.sync
        def _(sp):
            def load(n, k, u, e, kind):
                if kind == "r":
                    sp.wait_ge(o_done, (n - 1) * 8)
                for a, name in enumerate(("g", "w1")):
                    sp.dma_start(up[:, u, a, :, :], w[kind + name][bass.ds(e, 1), :, :]
                                 .rearrange("o (c p) f -> p (o c) f", p=P)).then_inc(w_in[u], 16)
                sp.dma_start(down[:, u, :], w[kind + "w2"][bass.ds(e, 1), :, :].rearrange("o f d -> f (o d)")
                             ).then_inc(w_in[u], 16)
                for a, name in enumerate(("gb", "b1")):
                    sp.dma_start(bias[:, u, a:a + 1], w[kind + name][bass.ds(e, 1), :].rearrange("o f -> f o")
                                 ).then_inc(w_in[u], 16)
            each_expert(sp, load)
            for u in range(2):
                sp.wait_ge(w_in[u], LOADS * NE // 2)

        @block.tensor
        def _(pe):
            def product(n, u, j):
                ch = n * NCH + j
                pe.wait_ge(y_ready, ch + 1)
                if not (isinstance(n, int) and ch < 2):
                    pe.wait_ge(added, (ch - 1) * TPC)
                for k in range(TPC):
                    ins = nc.tensor.matmul(o_ps[j % 2][:, k // 2, k % 2, :], y[:, j % 2, k * P:(k + 1) * P],
                                           down[:, u, :], start=True, stop=True)
                    if k % 2:
                        ins.then_inc(o_done, 1)

            def expert(n, k, u, e, kind):
                pe.wait_ge(w_in[u], (k + 1) * LOADS)
                for j in range(NCH):
                    ch = n * NCH + j
                    if not (isinstance(n, int) and ch < 2):
                        pe.wait_ge(y_ready, ch - 1)
                    for a in range(2):
                        for m in range(NC):
                            ins = nc.tensor.matmul(g_ps[j % 2][:, a, :], up[:, u, a, m, :],
                                                   xT[:, m, j * CH:(j + 1) * CH], start=m == 0, stop=m == NC - 1)
                    ins.then_inc(gu_done, 1)
                    if j:
                        product(n, u, j - 1)
                    elif not (isinstance(n, int) and n == 0):
                        product(n - 1, 1 - u, NCH - 1)

            each_expert(pe, expert)
            product(NE - 1, 1, NCH - 1)

        @block.scalar
        def _(act):
            nc.scalar.preload_act_table(ACT.Gelu)

            def expert(n, k, u, e, kind):
                for j in range(NCH):
                    ch = n * NCH + j
                    act.wait_ge(gu_done, ch + 1)
                    if not (isinstance(n, int) and ch < 2):
                        act.wait_ge(y_ready, ch - 1)
                    nc.scalar.activation(gel[:, j % 2, :], g_ps[j % 2][:, 0, :], ACT.Gelu, bias=bias[:, u, 0:1]
                                         ).then_inc(gel_ready, 1)
            each_expert(act, expert)

        @block.vector
        def _(dve):
            def add(n, j):
                ch = n * NCH + j
                for k in range(TPC):
                    dve.wait_ge(o_done, ch * 2 + (k // 2 + 1))
                    i = j * TPC + k
                    if not (isinstance(n, int) and n == 0):
                        dve.wait_ge(added, (ch - NCH) * TPC + (k + 1))
                    col = comb[:, n, i:i + 1] if isinstance(n, int) else \
                        comb[:, bass.ds(n, 1), i:i + 1].rearrange("p o i -> p (o i)")
                    nc.vector.scalar_tensor_tensor(x_sb[:, i, :], o_ps[j % 2][:, k // 2, k % 2, :], col,
                                                   x_sb[:, i, :], ALU.mult, ALU.add).then_inc(added, 1)

            def expert(n, k, u, e, kind):
                for j in range(NCH):
                    ch = n * NCH + j
                    dve.wait_ge(gel_ready, ch + 1)
                    if not (isinstance(n, int) and ch < 2):
                        dve.wait_ge(o_done, (ch - 1) * 2)
                    nc.vector.scalar_tensor_tensor(y[:, j % 2, :], g_ps[j % 2][:, 1, :], bias[:, u, 1:2],
                                                   gel[:, j % 2, :], ALU.add, ALU.mult).then_inc(y_ready, 1)
                    if j:
                        add(n, j - 1)
                    elif not (isinstance(n, int) and n == 0):
                        add(n - 1, NCH - 1)
            each_expert(dve, expert)
            add(NE - 1, NCH - 1)
            dve.wait_ge(added, NE * NT)


def expert_layer(nc, t, w, tag):
    with ExitStack() as c:
        t["xT"] = c.enter_context(nc.sbuf_tensor(tag + "xT", [P, NC, TOK], F32))
        t["comb"] = c.enter_context(nc.sbuf_tensor(tag + "comb", [P, NE, NT], F32))
        normalise_and_turn(nc, t, tag + "n_", True)
        route(nc, t, w, tag + "r_")
        experts(nc, t, w, tag + "e_")


HB = 16
HDB = D // HB
TWO_PI = 6.283185307179586
PI_IN = 3.1415925
C1 = 6.28125
C2 = 1.9350051879882812e-3
C3 = TWO_PI - C1 - C2
MAGIC = 1.5 * 2 ** 23


def rotation_tables(nc, t, w):
    ident = t["ident"]
    with ExitStack() as c:
        sb = lambda n, s, d=F32: c.enter_context(nc.sbuf_tensor("rt_" + n, s, d))
        sem = lambda n: c.enter_context(nc.semaphore("rt_" + n))
        H2 = HDB // 2
        freq, pos = sb("freq", [P, H2]), sb("pos", [P, NB])
        angle, turns, red = sb("angle", [P, NB, H2]), sb("turns", [P, 2, NB, H2]), sb("red", [P, 2, NB, H2])
        raw = {k: sb("raw_" + k, [P, NC, D]) for k in "qkvo"}
        tp = [c.enter_context(nc.psum_tensor(f"rt_tp{i}", [P, NC, D], F32)) for i in range(4)]
        loaded, w_loaded, pos_ready, chain, reduced, turned, copied, made = (
            sem("loaded"), sem("w_loaded"), sem("pos"), sem("chain"), sem("reduced"), sem("turned"), sem("copied"),
            sem("made"))
        block = c.enter_context(nc.Block())

        @block.sync
        def _(sp):
            sp.dma_start(freq[:, :], w["inv_freq"].rearrange("(o n) -> o n", o=1).partition_broadcast(P)
                         ).then_inc(loaded, 16)
            for k in "qkvo":
                sp.dma_start(raw[k][:, :, :], w["w" + k].rearrange("(c p) n -> p c n", p=P)).then_inc(w_loaded, 16)
            sp.wait_ge(w_loaded, 64)

        @block.gpsimd
        def _(pool):
            nc.gpsimd.iota(pos[:, :], [[P, NB]], base=0, channel_multiplier=1,
                           allow_small_or_imprecise_dtypes=True).then_inc(pos_ready, 1)

        @block.vector
        def _(dve):
            link = link_on(dve, chain)
            dve.wait_ge(loaded, 16)
            dve.wait_ge(pos_ready, 1)
            link(nc.vector.tensor_tensor(
                angle[:, :, :], pos[:, :].rearrange("p (k o) -> p k o", o=1).broadcast_to([P, NB, H2]),
                freq[:, :].rearrange("p (o n) -> p o n", o=1).broadcast_to([P, NB, H2]), ALU.mult))
            for r in range(2):
                tr, rd = turns[:, r, :, :], red[:, r, :, :]
                link(nc.vector.tensor_scalar(tr, angle[:, :, :], 1.0 / TWO_PI, 0.25 * r, ALU.mult, ALU.add))
                link(nc.vector.tensor_scalar(tr, tr, MAGIC, -MAGIC, ALU.add, ALU.add))
                link(nc.vector.scalar_tensor_tensor(rd, tr, -C1, angle[:, :, :], ALU.mult, ALU.add))
                link(nc.vector.scalar_tensor_tensor(rd, tr, -C2, rd, ALU.mult, ALU.add))
                link(nc.vector.scalar_tensor_tensor(rd, tr, -C3, rd, ALU.mult, ALU.add))
                if r:
                    link(nc.vector.tensor_scalar(rd, rd, TWO_PI / 4, None, ALU.add))
                nc.vector.tensor_scalar(rd, rd, PI_IN, -PI_IN, ALU.min, ALU.max).then_inc(reduced, 1)
            for i, k in enumerate("qkvo"):
                dve.wait_ge(turned, i + 1)
                dst = {"q": t["wqk"][:, :, 0:D], "k": t["wqk"][:, :, D:2 * D], "v": t["wv"][:, :, :],
                       "o": t["wo_b"][:, :, :]}[k]
                nc.vector.tensor_copy(dst, tp[i][:, :, :]).then_inc(copied, 1)
            dve.wait_ge(copied, 4)

        @block.scalar
        def _(act):
            for r in range(2):
                act.wait_ge(reduced, r + 1)
                nc.scalar.activation((t["sin"], t["cos"])[r][:, :, :], red[:, r, :, :], ACT.Sin).then_inc(made, 1)
            act.wait_ge(made, 2)

        @block.tensor
        def _(pe):
            pe.wait_ge(w_loaded, 64)
            for i, k in enumerate("qkvo"):
                for m in range(NC):
                    for n in range(NC):
                        ins = nc.tensor.transpose(tp[i][:, n, m * P:(m + 1) * P], raw[k][:, m, n * P:(n + 1) * P],
                                                  ident[:, :])
                ins.then_inc(turned, 1)


def attention_b(nc, t):
    x_sb, ident = t["x"], t["ident"]
    H2 = HDB // 2
    with ExitStack() as c:
        sb = lambda n, s, d=F32: c.enter_context(nc.sbuf_tensor("ab_" + n, s, d))
        sem = lambda n: c.enter_context(nc.semaphore("ab_" + n))
        s = {"st": sb("st", [P, NT, 6]), "small": sb("small", [P, 7, NT])}
        xn, xT = sb("xn", [P, 2, D]), sb("xT", [P, 2, NC, P])
        rot = sb("rot", [P, 2 * HB, HDB])
        cr = sb("cr", [P, 4, 2 * HB, H2])
        v = sb("v", [P, HB, HDB])
        prod = sb("prod", [P, HB, HB, HDB])
        sc, ex = sb("sc", [P, HB, HB]), sb("ex", [P, HB, HB])
        mx, dn = sb("mx", [P, HB]), sb("dn", [P, HB])
        o, oT = sb("o", [P, D]), sb("oT", [P, NC, P])
        ps = lambda n: c.enter_context(nc.psum_tensor("ab_" + n, [P, CH], F32))
        xt_ps = [ps("xt0"), ps("xt1")]
        qk_ps, v_ps, ot_ps, y_ps = [ps("qk0"), ps("qk1")], [ps("v0"), ps("v1")], ps("ot"), ps("y")
        ns = {k: sem(k) for k in ("stats", "dve_chain", "veps", "pow")}
        xn_ready, xt_done, xT_ready, qkv_done, qkv_used = (sem("xn_ready"), sem("xt_done"), sem("xT_ready"),
                                                           sem("qkv_done"), sem("qkv_used"))
        chain, sc_ready, ex_ready, o_ready, ot_done, oT_ready, y_done, added = (
            sem("chain"), sem("sc"), sem("ex"), sem("o"), sem("otd"), sem("oTr"), sem("y"), sem("added"))
        block = c.enter_context(nc.Block())

        @block.gpsimd
        def _(pool):
            pool.wait_ge(ns["veps"], 1)
            nc.gpsimd.tensor_tensor(s["small"][:, 3, :], s["small"][:, 2, :], t["neg_half"][:, :], ALU.pow
                                    ).then_inc(ns["pow"], 1)

        @block.vector
        def _(dve):
            mean, rstd = norm_statistics(nc, dve, None, x_sb, s, ns)

            def norm(i):
                if i >= 2:
                    dve.wait_ge(xt_done, i - 1)
                nc.vector.tensor_scalar(xn[:, i % 2, :], x_sb[:, i, :], mean[:, i:i + 1], rstd[:, i:i + 1],
                                        ALU.subtract, ALU.mult).then_inc(xn_ready, 1)

            link = link_on(dve, chain)
            norm(0)
            for i in range(NT):
                if i + 1 < NT:
                    norm(i + 1)
                dve.wait_ge(qkv_done, i + 1)
                qk = qk_ps[i % 2][:, :].rearrange("p (h n e) -> p h n e", n=H2, e=2)
                cos = t["cos"][:, i % NB:i % NB + 1, :].broadcast_to([P, 2 * HB, H2])
                sin = t["sin"][:, i % NB:i % NB + 1, :].broadcast_to([P, 2 * HB, H2])
                nc.vector.tensor_tensor(cr[:, 0, :, :], qk[:, :, :, 0], cos, ALU.mult)
                nc.vector.tensor_tensor(cr[:, 1, :, :], qk[:, :, :, 1], sin, ALU.mult)
                nc.vector.tensor_tensor(cr[:, 2, :, :], qk[:, :, :, 0], sin, ALU.mult)
                nc.vector.tensor_copy(v[:, :, :], v_ps[i % 2][:, 0:D].rearrange("p (h n) -> p h n", h=HB))
                link(nc.vector.tensor_tensor(cr[:, 3, :, :], qk[:, :, :, 1], cos, ALU.mult))
                nc.vector.tensor_tensor(rot[:, :, 0:H2], cr[:, 0, :, :], cr[:, 1, :, :], ALU.subtract
                                        ).then_inc(qkv_used, 1)
                link(nc.vector.tensor_tensor(rot[:, :, H2:HDB], cr[:, 2, :, :], cr[:, 3, :, :], ALU.add))
                bq = rot[:, 0:HB, :].rearrange("p h (o n) -> p h o n", o=1).broadcast_to([P, HB, HB, HDB])
                bk = rot[:, HB:2 * HB, :].rearrange("p (o h) n -> p o h n", o=1).broadcast_to([P, HB, HB, HDB])
                link(nc.vector.tensor_tensor(prod[:, :, :, :], bq, bk, ALU.mult))
                link(nc.vector.tensor_reduce(sc[:, :, :], prod[:, :, :, :], AX.X, ALU.add))
                link(nc.vector.tensor_reduce(mx[:, :], sc[:, :, :], AX.X, ALU.max))
                wide = lambda a, n: a.rearrange("p (h o) -> p h o", o=1).broadcast_to([P, HB, n])
                nc.vector.tensor_tensor(sc[:, :, :], sc[:, :, :], wide(mx[:, :], HB), ALU.subtract
                                        ).then_inc(sc_ready, 1)
                dve.wait_ge(ex_ready, i + 1)
                link(nc.vector.tensor_reduce(dn[:, :], ex[:, :, :], AX.X, ALU.add))
                bp = ex[:, :, :].rearrange("p h (o t) -> p h o t", o=1).broadcast_to([P, HB, HDB, HB])
                bv = v[:, :, :].rearrange("p (o t) n -> p o n t", o=1).broadcast_to([P, HB, HDB, HB])
                link(nc.vector.tensor_tensor(prod[:, :, :, :], bp, bv, ALU.mult))
                link(nc.vector.reciprocal(dn[:, :], dn[:, :]))
                oh = o[:, :].rearrange("p (h n) -> p h n", h=HB)
                if i:
                    dve.wait_ge(ot_done, i)
                link(nc.vector.tensor_reduce(oh, prod[:, :, :, :], AX.X, ALU.add))
                nc.vector.tensor_tensor(oh, oh, wide(dn[:, :], HDB), ALU.mult).then_inc(o_ready, 1)
                if i:
                    dve.wait_ge(y_done, i)
                    nc.vector.tensor_tensor(x_sb[:, i - 1, :], y_ps[:, 0:D], x_sb[:, i - 1, :], ALU.add
                                            ).then_inc(added, 1)
            dve.wait_ge(y_done, NT)
            nc.vector.tensor_tensor(x_sb[:, NT - 1, :], y_ps[:, 0:D], x_sb[:, NT - 1, :], ALU.add).then_inc(added, 1)
            dve.wait_ge(added, NT)

        @block.tensor
        def _(pe):
            def project(i):
                u = i % 2
                pe.wait_ge(xn_ready, i + 1)
                if i >= 2:
                    pe.wait_ge(xT_ready, i - 1)
                for m in range(NC):
                    ins = nc.tensor.transpose(xt_ps[u][:, m * P:(m + 1) * P], xn[:, u, m * P:(m + 1) * P], ident[:, :])
                ins.then_inc(xt_done, 1)
                pe.wait_ge(xT_ready, i + 1)
                if i >= 2:
                    pe.wait_ge(qkv_used, i - 1)
                for m in range(NC):
                    nc.tensor.matmul(qk_ps[u][:, :], xT[:, u, m, :], t["wqk"][:, m, :], start=m == 0, stop=m == NC - 1)
                for m in range(NC):
                    ins = nc.tensor.matmul(v_ps[u][:, 0:D], xT[:, u, m, :], t["wv"][:, m, :], start=m == 0,
                                           stop=m == NC - 1)
                ins.then_inc(qkv_done, 1)

            project(0)
            for i in range(NT):
                if i + 1 < NT:
                    project(i + 1)
                pe.wait_ge(o_ready, i + 1)
                if i:
                    pe.wait_ge(oT_ready, i)
                for m in range(NC):
                    ins = nc.tensor.transpose(ot_ps[:, m * P:(m + 1) * P], o[:, m * P:(m + 1) * P], ident[:, :])
                ins.then_inc(ot_done, 1)
                pe.wait_ge(oT_ready, i + 1)
                if i:
                    pe.wait_ge(added, i)
                for m in range(NC):
                    ins = nc.tensor.matmul(y_ps[:, 0:D], oT[:, m, :], t["wo_b"][:, m, :], start=m == 0, stop=m == NC - 1)
                ins.then_inc(y_done, 1)

        @block.scalar
        def _(act):
            nc.scalar.preload_act_table(ACT.Exp)

            def turn(i):
                act.wait_ge(xt_done, i + 1)
                if i >= 2:
                    act.wait_ge(qkv_done, i - 1)
                nc.scalar.activation(xT[:, i % 2, :, :], xt_ps[i % 2][:, 0:D].rearrange("p (c n) -> p c n", c=NC),
                                     ACT.Copy).then_inc(xT_ready, 1)
            turn(0)
            for i in range(NT):
                if i + 1 < NT:
                    turn(i + 1)
                act.wait_ge(sc_ready, i + 1)
                nc.scalar.activation(ex[:, :, :], sc[:, :, :], ACT.Exp, scale=float(HDB) ** -0.5).then_inc(ex_ready, 1)
                act.wait_ge(ot_done, i + 1)
                if i:
                    act.wait_ge(y_done, i)
                nc.scalar.activation(oT[:, :, :], ot_ps[:, 0:D].rearrange("p (c n) -> p c n", c=NC), ACT.Copy
                                     ).then_inc(oT_ready, 1)


def rest_of_layers(nc, t, w, stop):
    ffn = {k.removeprefix("L0_ffn_"): v for k, v in w.items() if "ffn" in k}
    b = {k.removeprefix("L0_attn_b_"): v for k, v in w.items() if "attn_b" in k}
    expert_layer(nc, t, ffn, "l2")
    if stop > 2:
        with ExitStack() as c:
            sb = lambda n, s, d=F32: c.enter_context(nc.sbuf_tensor(n, s, d))
            t["sin"], t["cos"] = sb("sin", [P, NB, HDB // 2]), sb("cos", [P, NB, HDB // 2])
            t["wqk"], t["wv"], t["wo_b"] = sb("wqk", [P, NC, 2 * D]), sb("wv", [P, NC, D]), sb("wo_b", [P, NC, D])
            rotation_tables(nc, t, b)
            attention_b(nc, t)
    if stop > 3:
        expert_layer(nc, t, ffn, "l4")


def build(nc, stop=9, out=None, **w):
    nc.disable_value_cache = True
    with ExitStack() as c:
        sb = lambda n, s, d=F32: c.enter_context(nc.sbuf_tensor(n, s, d))
        t = {
            "x": sb("x_sb", [P, NT, D]), "ident": sb("ident", [P, P]), "identb": sb("identb", [P, P], BF16),
            "mask_s": sb("mask_s", [P, P], BF16), "mask_t": sb("mask_t", [P, P], BF16),
            "neg_half": sb("neg_half", [P, NT]), "experts": sb("experts", [P, NT, E]),
        }
        t["x_loaded"] = c.enter_context(nc.semaphore("x_loaded"))
        constants(nc, c, t)
        a = {k.removeprefix("L0_attn_a_"): v for k, v in w.items() if "attn_a" in k}
        with ExitStack() as ca:
            sa = lambda n, s, d=F32: ca.enter_context(nc.sbuf_tensor(n, s, d))
            t["wf"], t["bf"] = sa("wf", [P, 3, NC, DL]), sa("bf", [P, 3])
            t["wo_a"], t["bo_a"] = sa("wo_a", [P, D]), sa("bo_a", [P, D])
            t["v"] = sa("v_all", [P, NQ, NB, QUAD * HDA])
            t["att"] = sa("att", [P, NQ * NB * QUAD, HDA])
            t["q_parts"] = nc.dram_tensor("q_parts", (B * HA, 2 * PARTS - 1, HDA, T), BF16, kind="Internal").ap()
            t["k_parts"] = nc.dram_tensor("k_parts", (B * HA, PARTS, HDA, T), BF16, kind="Internal").ap()
            fold_weights(nc, t, a)
            project_a(nc, t)
            attention_a(nc, t)
            output_a(nc, t)
        if stop > 1:
            rest_of_layers(nc, t, w, stop)
        stored = c.enter_context(nc.semaphore("stored"))
        with nc.Block() as block:
            @block.sync
            def _(sp):
                sp.dma_start(out.rearrange("b (i p) d -> p (b i) d", p=P), t["x"][:, :, :]).then_inc(stored, 16)
                sp.wait_ge(stored, 16)


_OUT = (B, T, D)


def kernel(**inputs):
    import numpy as np
    import concourse.bacc as bacc
    from concourse.bass_utils import run_bass_kernel_spmd

    nc = bacc.Bacc("TRN2", target_bir_lowering=False, num_devices=1)
    arrays = {name: np.ascontiguousarray(a) for name, a in inputs.items()}
    args = {name: nc.dram_tensor("in_" + name, a.shape, mybir.dt.from_np(a.dtype), kind="ExternalInput").ap()
            for name, a in arrays.items()}
    out = nc.dram_tensor("out_x", _OUT, F32, kind="ExternalOutput").ap()
    build(nc, out=out, **args)
    r = run_bass_kernel_spmd(nc, [{"in_" + name: a for name, a in arrays.items()}], core_ids=[0])
    return r.results[0]["out_x"]
```

```python
from contextlib import ExitStack

import concourse.bass as bass
from concourse import mybir

P = 128
F32 = mybir.dt.float32
BF16 = mybir.dt.bfloat16
I32 = mybir.dt.int32
U32 = mybir.dt.uint32
ALU = mybir.AluOpType
ACT = mybir.ActivationFunctionType
AX = mybir.AxisListType

B, T, D = 2, 1024, 256
TOK = B * T
NT = TOK // P
NC = D // P
CH = 512
NCH = TOK // CH
TPC = CH // P
EPS = 1e-5

HA = 16
DL = 128
HDA = DL // HA
QUAD = 4
NQ = B * HA // QUAD
QPB = NQ // B
PARTS = 3
COMBOS = PARTS * PARTS
KR = COMBOS * HDA
KM = KR + PARTS
NB = T // P
BIG = 1e30
MAGIC = 1.5 * 2 ** 23


def link_on(eng, sem, start=0):
    count = [start]

    def link(ins):
        count[0] = count[0] + 1
        ins.then_inc(sem, 1)
        eng.wait_ge(sem, count[0])

    return link


def constants(nc, ctx, tiles):
    ident, identb, mask_s, mask_t = tiles["ident"], tiles["identb"], tiles["mask_s"], tiles["mask_t"]
    with ExitStack() as c:
        cleared = c.enter_context(nc.semaphore("const_cleared"))
        made = c.enter_context(nc.semaphore("const_made"))
        block = c.enter_context(nc.Block())

        @block.gpsimd
        def _(pool):
            nc.gpsimd.memset(ident[:, :], 0.0).then_inc(cleared, 1)
            nc.gpsimd.memset(identb[:, :], 0.0).then_inc(cleared, 1)
            nc.gpsimd.memset(mask_s[:, :], 0.0).then_inc(cleared, 1)
            nc.gpsimd.memset(mask_t[:, :], 0.0).then_inc(cleared, 1)
            nc.gpsimd.memset(tiles["neg_half"][:, :], -0.5).then_inc(made, 1)
            pool.wait_ge(cleared, 4)
            for m in (ident, identb):
                nc.gpsimd.affine_select(out=m[:, :], in_=m[:, :], compare_op=ALU.not_equal, fill=1.0, base=0,
                                        pattern=[[-1, P]], channel_multiplier=1).then_inc(made, 1)
            nc.gpsimd.affine_select(out=mask_s[:, :], in_=mask_s[:, :], compare_op=ALU.is_ge, fill=-BIG, base=0,
                                    pattern=[[-1, P]], channel_multiplier=1).then_inc(made, 1)
            nc.gpsimd.affine_select(out=mask_t[:, :], in_=mask_t[:, :], compare_op=ALU.is_ge, fill=-BIG, base=0,
                                    pattern=[[1, P]], channel_multiplier=-1).then_inc(made, 1)
            nc.gpsimd.iota(tiles["experts"][:, :, :], [[0, NT], [1, E]], base=E, channel_multiplier=0,
                           allow_small_or_imprecise_dtypes=True).then_inc(made, 1)
            for name, value in (("restart", 1.0), ("ones_e", 1.0), ("ones", 1.0), ("before_me", 1.0), ("zeros", 0.0),
                                ("one_row", 1.0)):
                whole = tiles[name][:, :, :] if name == "restart" else tiles[name][:, :]
                nc.gpsimd.memset(whole, value).then_inc(cleared, 1)
            nc.gpsimd.iota(tiles["tile_no"][:, :, :], [[1, TILES], [0, E]], base=0, channel_multiplier=0,
                           allow_small_or_imprecise_dtypes=True).then_inc(made, 1)
            pool.wait_ge(cleared, 10)
            nc.gpsimd.memset(tiles["restart"][:, :, 0:1], 0.0).then_inc(made, 1)
            nc.gpsimd.affine_select(out=tiles["before_me"][:, :], in_=tiles["before_me"][:, :], compare_op=ALU.is_gt,
                                    fill=0.0, base=0, pattern=[[1, P]], channel_multiplier=-1).then_inc(made, 1)
            pool.wait_ge(made, 9)


def norm_statistics(nc, dve, pool_pow, x_sb, s, sem):
    st, small = s["st"], s["small"]
    mean, rstd, veps, r0, dif, cvs, tmp = (small[:, k, :] for k in range(7))
    with dve.Fori(0, NT) as i:
        nc.vector.bn_stats(st[:, bass.ds(i, 1), :], x_sb[:, bass.ds(i, 1), :]).then_inc(sem["stats"], 1)
    dve.wait_ge(sem["stats"], NT)
    link = link_on(dve, sem["dve_chain"])
    nc.vector.tensor_tensor(tmp, st[:, :, 1], st[:, :, 4], ALU.add)
    nc.vector.tensor_tensor(dif, st[:, :, 1], st[:, :, 4], ALU.subtract)
    link(nc.vector.tensor_tensor(cvs, st[:, :, 2], st[:, :, 5], ALU.add))
    nc.vector.tensor_scalar(mean, tmp, 0.5, None, ALU.mult)
    nc.vector.tensor_scalar(cvs, cvs, 1.0 / D, EPS, ALU.mult, ALU.add)
    link(nc.vector.tensor_tensor(dif, dif, dif, ALU.mult))
    nc.vector.scalar_tensor_tensor(veps, dif, 0.25, cvs, ALU.mult, ALU.add).then_inc(sem["veps"], 1)
    dve.wait_ge(sem["veps"], 1)
    dve.wait_ge(sem["pow"], 1)
    link(nc.vector.tensor_tensor(tmp, r0, r0, ALU.mult))
    link(nc.vector.tensor_tensor(tmp, tmp, veps, ALU.mult))
    link(nc.vector.tensor_scalar(tmp, tmp, -0.5, 1.5, ALU.mult, ALU.add))
    link(nc.vector.tensor_tensor(rstd, r0, tmp, ALU.mult))
    return mean, rstd


def fold_weights(nc, t, w):
    x_sb, ident = t["x"], t["ident"]
    with ExitStack() as c:
        sb = lambda n, s, d=F32: c.enter_context(nc.sbuf_tensor(n, s, d))
        sem = lambda n: c.enter_context(nc.semaphore(n))
        w1 = {k: sb(f"w1_{k}", [P, NC, D]) for k in "qkv"}
        w1t = {k: sb(f"w1t_{k}", [P, NC, D]) for k in "qkv"}
        w2 = {k: sb(f"w2_{k}", [P, NC, DL]) for k in "qkv"}
        bcol = sb("bcol", [P, 3, NC])
        blcol = sb("blcol", [P, 3, 1])
        tp = c.enter_context(nc.psum_tensor("fold_tp", [P, 3, NC, D], F32))
        fp = c.enter_context(nc.psum_tensor("fold_fp", [P, 3, 512], F32))
        loaded = {k: sem(f"fold_loaded_{k}") for k in "qkv"}
        bias_in = sem("fold_bias_in")
        turned, turned_out, folded, out = sem("fold_turned"), sem("fold_turned_out"), sem("fold_done"), sem("fold_out")
        block = c.enter_context(nc.Block())

        @block.sync
        def _(sp):
            for k in "qkv":
                sp.dma_start(w1[k][:, :, :], w[f"w{k}"].rearrange("(c p) n -> p c n", p=P)).then_inc(loaded[k], 16)
                sp.dma_start(w2[k][:, :, :], w[f"w{k}l"].rearrange("(c p) n -> p c n", p=P)).then_inc(loaded[k], 16)
            sp.dma_start(x_sb[:, :, :], w["x"].rearrange("b (i p) d -> p (b i) d", p=P)).then_inc(t["x_loaded"], 16)
            sp.dma_start(t["wo_a"][:, :], w["wo"]).then_inc(t["x_loaded"], 16)
            sp.dma_start(t["bo_a"][:, :], w["bo"].rearrange("(o n) -> o n", o=1).partition_broadcast(P)
                         ).then_inc(t["x_loaded"], 16)

        @block.scalar
        def _(act):
            for i, k in enumerate("qkv"):
                act.dma_start(bcol[:, i, :], w[f"b{k}"].rearrange("(c p) -> p c", p=P),
                              allow_slow_non_contiguous=True).then_inc(bias_in, 16)
                act.dma_start(blcol[:, i, :], w[f"b{k}l"].rearrange("(p o) -> p o", o=1)).then_inc(bias_in, 16)

        @block.tensor
        def _(pe):
            for i, k in enumerate("qkv"):
                pe.wait_ge(loaded[k], 32)
                for m in range(NC):
                    for n in range(NC):
                        ins = nc.tensor.transpose(tp[:, i, n, m * P:(m + 1) * P], w1[k][:, m, n * P:(n + 1) * P],
                                                  ident[:, :])
                ins.then_inc(turned, 1)
            pe.wait_ge(bias_in, 96)
            for i, k in enumerate("qkv"):
                pe.wait_ge(turned_out, i + 1)
                for m in range(NC):
                    for n in range(NC):
                        nc.tensor.matmul(fp[:, i, m * DL:(m + 1) * DL], w1t[k][:, n, m * P:(m + 1) * P],
                                         w2[k][:, n, :], start=n == 0, stop=n == NC - 1)
                for n in range(NC):
                    ins = nc.tensor.matmul(fp[:, i, NC * DL:NC * DL + 1], w2[k][:, n, :], bcol[:, i, n:n + 1],
                                           start=n == 0, stop=n == NC - 1)
                ins.then_inc(folded, 1)

        @block.vector
        def _(dve):
            for i, k in enumerate("qkv"):
                dve.wait_ge(turned, i + 1)
                nc.vector.tensor_copy(w1t[k][:, :, :], tp[:, i, :, :]).then_inc(turned_out, 1)
            for i, k in enumerate("qkv"):
                dve.wait_ge(folded, i + 1)
                nc.vector.tensor_copy(t["wf"][:, i, :, :], fp[:, i, 0:NC * DL].rearrange("p (c n) -> p c n", c=NC)
                                      ).then_inc(out, 1)
                nc.vector.tensor_tensor(t["bf"][:, i:i + 1], fp[:, i, NC * DL:NC * DL + 1], blcol[:, i, :],
                                        ALU.add).then_inc(out, 1)
            dve.wait_ge(out, 6)


def project_a(nc, t):
    x_sb, ident, wf, bf = t["x"], t["ident"], t["wf"], t["bf"]
    qs, ks = t["q_parts"], t["k_parts"]
    with ExitStack() as c:
        sb = lambda n, s, d=F32: c.enter_context(nc.sbuf_tensor(n, s, d))
        sem = lambda n: c.enter_context(nc.semaphore(n))
        s = {"st": sb("pa_st", [P, NT, 6]), "small": sb("pa_small", [P, 7, NT])}
        xn = sb("pa_xn", [P, 2 * TPC, D])
        xT = sb("pa_xT", [P, 2, NC, CH])
        rest = sb("pa_rest", [P, 2, CH])
        parts = sb("pa_parts", [P, 2, 2, PARTS, CH], BF16)
        vT = sb("pa_vT", [P, CH])
        xt_ps = c.enter_context(nc.psum_tensor("pa_xt", [P, NC, CH], F32))
        qk_ps = c.enter_context(nc.psum_tensor("pa_qk", [P, 2, CH], F32))
        v_ps = c.enter_context(nc.psum_tensor("pa_v", [P, CH], F32))
        vt_ps = c.enter_context(nc.psum_tensor("pa_vt", [P, CH], F32))
        ns = {k: sem(f"pa_{k}") for k in ("stats", "dve_chain", "veps", "pow")}
        xn_ready, xt_done, xT_ready = sem("pa_xn_ready"), sem("pa_xt_done"), sem("pa_xT_ready")
        qk_done, qk_free = sem("pa_qk_done"), sem("pa_qk_free")
        high, mid, low = sem("pa_high"), sem("pa_mid"), sem("pa_low")
        v_done, vT_ready, vt_done, v_out = sem("pa_v_done"), sem("pa_vT_ready"), sem("pa_vt_done"), sem("pa_v_out")
        saved = [sem("pa_saved0"), sem("pa_saved1")]
        block = c.enter_context(nc.Block())

        @block.gpsimd
        def _(pool):
            pool.wait_ge(ns["veps"], 1)
            nc.gpsimd.tensor_tensor(s["small"][:, 3, :], s["small"][:, 2, :], t["neg_half"][:, :], ALU.pow
                                    ).then_inc(ns["pow"], 1)

        @block.vector
        def _(dve):
            dve.wait_ge(t["x_loaded"], 48)
            mean, rstd = norm_statistics(nc, dve, None, x_sb, s, ns)
            for j in range(NCH):
                u = j % 2
                for k in range(TPC):
                    i = j * TPC + k
                    if j >= 2:
                        dve.wait_ge(xt_done, j - 1)
                    nc.vector.tensor_scalar(xn[:, u * TPC + k, :], x_sb[:, i, :], mean[:, i:i + 1], rstd[:, i:i + 1],
                                            ALU.subtract, ALU.mult).then_inc(xn_ready, 1)
                for g in range(2):
                    n = 2 * j + g
                    dve.wait_ge(high, n + 1)
                    if n >= 2:
                        dve.wait_ge(low, n - 1)
                    nc.vector.scalar_tensor_tensor(rest[:, g, :], qk_ps[:, g, :], bf[:, g:g + 1],
                                                   parts[:, u, g, 0, :], ALU.add, ALU.subtract).then_inc(qk_free, 1)
                for g in range(2):
                    n = 2 * j + g
                    dve.wait_ge(mid, n + 1)
                    nc.vector.tensor_tensor(parts[:, u, g, 2, :], rest[:, g, :], parts[:, u, g, 1, :],
                                            ALU.subtract).then_inc(low, 1)
                dve.wait_ge(vt_done, j + 1)
                b, k0 = j * TPC // NB, j * TPC % NB
                nc.vector.tensor_copy(t["v"][:, b * QPB:(b + 1) * QPB, k0:k0 + TPC, :],
                                      vt_ps[:, :].rearrange("p (i q n) -> p q i n", i=TPC, q=QPB)).then_inc(v_out, 1)

        @block.tensor
        def _(pe):
            for j in range(NCH):
                u = j % 2
                for k in range(TPC):
                    pe.wait_ge(xn_ready, j * TPC + k + 1)
                    if j >= 1:
                        pe.wait_ge(xT_ready, 2 * j)
                    for m in range(NC):
                        ins = nc.tensor.transpose(xt_ps[:, m, k * P:(k + 1) * P], xn[:, u * TPC + k, m * P:(m + 1) * P],
                                                  ident[:, :])
                ins.then_inc(xt_done, 1)
                pe.wait_ge(xT_ready, 2 * j + 2)
                if j >= 1:
                    pe.wait_ge(qk_free, 2 * j)
                    pe.wait_ge(vT_ready, j)
                for g in range(3):
                    dst = v_ps[:, :] if g == 2 else qk_ps[:, g, :]
                    for m in range(NC):
                        ins = nc.tensor.matmul(dst, wf[:, g, m, :], xT[:, u, m, :], start=m == 0, stop=m == NC - 1)
                    ins.then_inc(v_done if g == 2 else qk_done, 1)
                pe.wait_ge(vT_ready, j + 1)
                if j >= 1:
                    pe.wait_ge(v_out, j)
                for k in range(TPC):
                    ins = nc.tensor.transpose(vt_ps[:, k * P:(k + 1) * P], vT[:, k * P:(k + 1) * P], ident[:, :])
                ins.then_inc(vt_done, 1)

        @block.scalar
        def _(act):
            for j in range(NCH):
                u = j % 2
                act.wait_ge(xt_done, j + 1)
                if j >= 2:
                    act.wait_ge(v_done, j - 1)
                for m in range(NC):
                    nc.scalar.activation(xT[:, u, m, :], xt_ps[:, m, :], ACT.Copy).then_inc(xT_ready, 1)
                for g in range(2):
                    act.wait_ge(qk_done, 2 * j + g + 1)
                    if j >= 2:
                        act.wait_ge(saved[u], 16 * (5 + 3) * (j // 2))
                    nc.scalar.activation(parts[:, u, g, 0, :], qk_ps[:, g, :], ACT.Identity,
                                         bias=bf[:, g:g + 1]).then_inc(high, 1)
                act.wait_ge(v_done, j + 1)
                if j >= 1:
                    act.wait_ge(vt_done, j)
                nc.scalar.activation(vT[:, :], v_ps[:, :], ACT.Identity, bias=bf[:, 2:3]).then_inc(vT_ready, 1)
                for g in range(2):
                    act.wait_ge(qk_free, 2 * j + g + 1)
                    nc.scalar.activation(parts[:, u, g, 1, :], rest[:, g, :], ACT.Copy).then_inc(mid, 1)

        @block.sync
        def _(sp):
            for j in range(NCH):
                u, b, t0 = j % 2, j * CH // T, j * CH % T
                for g, (dst, n) in enumerate(((qs, 5), (ks, 3))):
                    sp.wait_ge(mid, 2 * j + g + 1)
                    sp.wait_ge(low, 2 * j + g + 1)
                    for r in range(n):
                        sp.dma_start(dst[b * HA:(b + 1) * HA, r, :, t0:t0 + CH], parts[:, u, g, r % PARTS, :]).then_inc(saved[u], 16)
            for u in range(2):
                sp.wait_ge(saved[u], 16 * 8 * NCH // 2)


PIECES1 = [(tb, s0, min(s0 + CH, (tb + 1) * P)) for tb in range(NB) for s0 in range(0, (tb + 1) * P, CH)]
GROUPS2 = [(c, sb) for c in range(T // CH) for sb in range((c + 1) * CH // P)]
N1 = QUAD * len(PIECES1)
NG = len(GROUPS2)
N2 = QUAD * NG
FIRST_GROUPS = NG - 2
RS = 3


def share(g):
    per = -(-N1 // FIRST_GROUPS)
    return range(min(g * per, N1), min((g + 1) * per, N1)) if g < FIRST_GROUPS else range(0)


def piece1(n):
    h, k = divmod(n, len(PIECES1))
    tb, s0, s1 = PIECES1[k]
    col = tb if s0 == 0 else NB + tb - CH // P
    return h, tb, s0, s1, col


def attention_a(nc, t):
    qs, ks, v_all, identb, ident = t["q_parts"], t["k_parts"], t["v"], t["identb"], t["ident"]
    att = t["att"]
    NM = NB + NB - CH // P
    with ExitStack() as c:
        sb = lambda n, s, d=F32: c.enter_context(nc.sbuf_tensor(n, s, d))
        sem = lambda n: c.enter_context(nc.semaphore(n))
        qst = sb("qst", [KM, 2, QUAD, T], BF16)
        kst = sb("kst", [KM, 2, QUAD, T], BF16)
        vq = sb("vq", [P, 2, NB, QUAD, 32])
        pt = sb("pt", [P, RS, QUAD, CH])
        mx = sb("mx", [P, QUAD, NM])
        mrest = sb("mrest", [P, QUAD, NB])
        mparts = sb("mparts", [P, PARTS, QUAD, NB], BF16)
        mrow = sb("mrow", [PARTS * QUAD * NB, P], BF16)
        oT = sb("oT", [P, CH])
        rden = sb("rden", [P, TPC, QUAD])
        s1 = [c.enter_context(nc.psum_tensor(f"s1_{i}", [P, CH], F32)) for i in range(RS)]
        st = [c.enter_context(nc.psum_tensor(f"st_{i}", [P, CH], F32)) for i in range(RS)]
        o_ps = c.enter_context(nc.psum_tensor("o_ps", [P, CH], F32))
        tr = c.enter_context(nc.psum_tensor("tr", [P, CH], F32))
        rows_set, v_set, bias_added = sem("aa_rows_set"), sem("aa_v_set"), sem("aa_bias_added")
        stack = [sem("aa_stack0"), sem("aa_stack1")]
        s1_done, s1_used = sem("aa_s1_done"), sem("aa_s1_used")
        max_chain, rden_ready = sem("aa_max_chain"), sem("aa_rden_ready")
        mparts_ready, mt_done, mrow_ready = sem("aa_mparts"), sem("aa_mt_done"), sem("aa_mrow_ready")
        mrow_in = [sem("aa_mrow_in0"), sem("aa_mrow_in1")]
        st_done, exp_done, av_done = sem("aa_st_done"), sem("aa_exp_done"), sem("aa_av_done")
        v_ready, oT_ready, ot_done, norm_done = (sem("aa_v_ready"), sem("aa_oT_ready"), sem("aa_ot_done"),
                                                 sem("aa_norm_done"))
        block = c.enter_context(nc.Block())
        STACK = 16 * 2 * PARTS
        MROW = 16 * PARTS

        LINKS = 4

        def quads(eng, body):
            body(0, 0, 0, True, False)
            with eng.Fori(0, NQ // 2 - 1) as i:
                body(i * 2 + 1, i, 1, False, False)
                body(i * 2 + 2, i + 1, 0, False, False)
            body(NQ - 1, NQ // 2 - 1, 1, False, True)

        @block.sync
        def _(sp):
            def load(q, u):
                for r in range(PARTS):
                    sp.dma_start(qst[r * PARTS * HDA:(r + 1) * PARTS * HDA, u, :, :],
                                 qs[bass.ds(q * QUAD, QUAD), r:r + PARTS, :, :].rearrange("h r d t -> (r d) h t")
                                 ).then_inc(stack[u], 16)
                    sp.dma_start(kst[r * PARTS * HDA:(r + 1) * PARTS * HDA, u, :, :],
                                 ks[bass.ds(q * QUAD, QUAD), :, :, :].rearrange("h r d t -> (r d) h t")
                                 ).then_inc(stack[u], 16)

            def max_rows(q, u):
                sp.wait_ge(mrow_ready, q + 1)
                n = QUAD * NB
                for r in range(PARTS):
                    sp.dma_start(qst[KR + r:KR + r + 1, u, :, :].rearrange("o h (k p) -> o (h k) p", p=P),
                                 mrow[r * n:(r + 1) * n, :]).then_inc(mrow_in[u], 16)

            def step(q, u):
                max_rows(q + 1, 1 - u)
                sp.wait_ge(st_done, (q + 1) * N2)
                load(q + 2, u)

            sp.wait_ge(rows_set, 2)
            load(0, 0)
            load(1, 1)
            max_rows(0, 0)
            with sp.Fori(0, NQ // 2 - 1) as i:
                step(i * 2, 0)
                step(i * 2 + 1, 1)
            max_rows(NQ - 1, 1)
            for u in range(2):
                sp.wait_ge(mrow_in[u], MROW * NQ // 2)
                sp.wait_ge(stack[u], STACK * NQ // 2)

        @block.gpsimd
        def _(pool):
            nc.gpsimd.memset(kst[64:KM, :, :, :], 1.0).then_inc(rows_set, 1)
            nc.gpsimd.memset(qst[64:KM, :, :, :], 0.0).then_inc(rows_set, 1)
            pool.wait_ge(rows_set, 2)
            nc.gpsimd.memset(vq[:, :, :, :, :], 0.0).then_inc(v_set, 1)
            pool.wait_ge(v_set, 1)
            nc.gpsimd.memset(vq[:, :, :, :, HDA:HDA + 1], 1.0).then_inc(v_set, 1)
            pool.wait_ge(v_set, 2)

            def copy_v(q, u):
                src = v_all[:, q, :, :] if isinstance(q, int) else v_all[:, bass.ds(q, 1), :, :]
                src = src.rearrange("p (o k) (h d) -> p (o k) h d" if isinstance(q, int) else
                                    "p o k (h d) -> p (o k) h d", h=QUAD, **({"o": 1} if isinstance(q, int) else {}))
                nc.gpsimd.tensor_copy(vq[:, u, :, :, 0:HDA], src).then_inc(v_ready, 1)

            copy_v(0, 0)
            copy_v(1, 1)
            for j in range(TILES):
                pool.dma_start(t["x_sorted"][j * P:(j + 1) * P, :], t["zeros"][:, :]
                               ).then_inc(t["x_sorted_cleared"], 16)
            with pool.Fori(0, NT) as i:
                xs = t["x"][:, bass.ds(i, 1), :]
                nc.gpsimd.tensor_tensor(xs, xs, t["bo_a"][:, :].rearrange("p (o n) -> p o n", o=1), ALU.add
                                        ).then_inc(bias_added, 1)
            with pool.Fori(0, NQ // 2 - 1) as i:
                for u in range(2):
                    pool.wait_ge(av_done, (i * 2 + 1 + u) * NG)
                    copy_v(i * 2 + 2 + u, u)
            pool.wait_ge(bias_added, NT)

        @block.tensor
        def _(pe):
            def scores(q, u, n):
                h, tb, k0, k1, _col = piece1(n)
                if not (isinstance(q, int) and q == 0 and n < RS):
                    pe.wait_ge(s1_used, q * N1 + (n - RS + 1))
                diagonal = k1 == (tb + 1) * P
                ins = nc.tensor.matmul(s1[n % RS][:, 0:k1 - k0], qst[0:KR, u, h, tb * P:(tb + 1) * P],
                                       kst[0:KR, u, h, k0:k1], start=True, stop=not diagonal)
                if diagonal:
                    ins = nc.tensor.matmul(s1[n % RS][:, k1 - k0 - P:k1 - k0], identb[:, :], t["mask_s"][:, :],
                                           start=False, stop=True)
                ins.then_inc(s1_done, 1)

            def scores_t(q, u, g, h):
                c_, kb = GROUPS2[g]
                t0 = max(c_ * CH, kb * P)
                w = (c_ + 1) * CH - t0
                n = g * QUAD + h
                if not (isinstance(q, int) and q == 0 and n < RS):
                    pe.wait_ge(exp_done, q * N2 + (n - RS + 1))
                diagonal = kb * P >= c_ * CH
                ins = nc.tensor.matmul(st[n % RS][:, 0:w], kst[:, u, h, kb * P:(kb + 1) * P],
                                       qst[:, u, h, t0:t0 + w], start=True, stop=not diagonal)
                if diagonal:
                    ins = nc.tensor.matmul(st[n % RS][:, 0:P], identb[:, :], t["mask_t"][:, :],
                                           start=False, stop=True)
                ins.then_inc(st_done, 1)

            def values(q, u, g):
                c_, kb = GROUPS2[g]
                w = (c_ + 1) * CH - max(c_ * CH, kb * P)
                pe.wait_ge(exp_done, q * N2 + (g + 1) * QUAD)
                if kb == 0:
                    pe.wait_ge(v_ready, q + 1)
                    if not (isinstance(q, int) and q == 0 and c_ == 0):
                        pe.wait_ge(oT_ready, q * 2 + c_)
                last = kb == (c_ + 1) * CH // P - 1
                for h in range(QUAD):
                    ins = nc.tensor.matmul(o_ps[32 * h:32 * h + 32, CH - w:CH], vq[:, u, kb, h, :],
                                           pt[:, g % RS, h, 0:w], start=kb == 0, stop=last, skip_group_check=True)
                ins.then_inc(av_done, 1)

            def turn_output(q, c_):
                pe.wait_ge(oT_ready, q * 2 + (c_ + 1))
                for k in range(TPC):
                    ins = nc.tensor.transpose(tr[:, k * P:(k + 1) * P], oT[:, k * P:(k + 1) * P], ident[:, :])
                ins.then_inc(ot_done, 1)

            def turn_maxima(q):
                pe.wait_ge(mparts_ready, q + 1)
                n = PARTS * QUAD * NB
                nc.tensor.transpose(tr[0:n, 0:P // 2].bitcast(BF16),
                                    mparts[:, :, :, :].rearrange("p r h k -> p (r h k)"), identb[:, :]
                                    ).then_inc(mt_done, 1)

            def quad(q, k, u, first, last):
                pe.wait_ge(mrow_in[u], (k + 1) * MROW)
                if not last:
                    pe.wait_ge(stack[1 - u], (k + u + 1) * STACK)
                for g in range(NG):
                    todo = [] if last else list(share(g))
                    per = -(-len(todo) // QUAD)
                    for h in range(QUAD):
                        scores_t(q, u, g, h)
                        for n in todo[h * per:(h + 1) * per]:
                            scores(q + 1, 1 - u, n)
                    if g > 0:
                        values(q, u, g - 1)
                    elif not first:
                        values(q - 1, 1 - u, NG - 1)
                    if g == 1 and not first:
                        pe.wait_ge(mrow_ready, q + 1)
                        turn_output(q - 1, 1)
                    if g == 5:
                        if first:
                            pe.wait_ge(mrow_ready, 1)
                        else:
                            pe.wait_ge(norm_done, q * 2)
                        turn_output(q, 0)
                    if g == NG - 2 and not last:
                        pe.wait_ge(norm_done, q * 2 + 1)
                        turn_maxima(q + 1)
                if last:
                    values(q, u, NG - 1)
                    pe.wait_ge(norm_done, q * 2 + 1)
                    turn_output(q, 1)

            pe.wait_ge(stack[0], STACK)
            for n in range(N1):
                scores(0, 0, n)
            turn_maxima(0)
            quads(pe, quad)

        @block.scalar
        def _(act):
            nc.scalar.preload_act_table(ACT.Exp)

            def move_maxima(q, k, u):
                act.wait_ge(mt_done, q + 1)
                if not (isinstance(q, int) and q == 0):
                    act.wait_ge(mrow_in[1 - u], (k + u) * MROW)
                n = PARTS * QUAD * NB
                nc.scalar.activation(mrow[:, :], tr[0:n, 0:P // 2].bitcast(BF16), ACT.Copy).then_inc(mrow_ready, 1)

            def move_output(q, c_):
                act.wait_ge(av_done, q * NG + (NG if c_ else CH // P))
                if not (isinstance(q, int) and q == 0 and c_ == 0):
                    act.wait_ge(ot_done, q * 2 + c_)
                nc.scalar.activation(oT[:, :], o_ps[:, :], ACT.Copy).then_inc(oT_ready, 1)

            def quad(q, k, u, first, last):
                for g in range(NG):
                    c_, kb = GROUPS2[g]
                    w = (c_ + 1) * CH - max(c_ * CH, kb * P)
                    if not (first and g < RS):
                        act.wait_ge(av_done, q * NG + (g - RS + 1))
                    for h in range(QUAD):
                        n = g * QUAD + h
                        act.wait_ge(st_done, q * N2 + (n + 1))
                        nc.scalar.activation(pt[:, g % RS, h, 0:w], st[n % RS][:, 0:w], ACT.Exp,
                                             scale=float(HDA) ** -0.5).then_inc(exp_done, 1)
                    if g == 0 and not first:
                        move_output(q - 1, 1)
                    if g == CH // P:
                        move_output(q, 0)
                    if g == NG - 2 and not last:
                        move_maxima(q + 1, k + u, 1 - u)
                if last:
                    move_output(q, 1)

            move_maxima(0, 0, 0)
            quads(act, quad)

        @block.vector
        def _(dve):
            def maximum(q, n):
                h, tb, k0, k1, col = piece1(n)
                dve.wait_ge(s1_done, q * N1 + (n + 1))
                nc.vector.reduce_max(mx[:, h, col:col + 1], s1[n % RS][:, 0:k1 - k0], AX.X).then_inc(s1_used, 1)

            def split_maxima(q):
                dve.wait_ge(s1_used, q * N1 + N1)
                link = link_on(dve, max_chain, q * LINKS)
                two = CH // P
                link(nc.vector.tensor_tensor(mx[:, :, two:NB], mx[:, :, two:NB], mx[:, :, NB:NM], ALU.max))
                if not (isinstance(q, int) and q == 0):
                    dve.wait_ge(mt_done, q)
                link(nc.vector.tensor_scalar(mparts[:, 0, :, :], mx[:, :, 0:NB], -1.0, None, ALU.mult))
                link(nc.vector.scalar_tensor_tensor(mrest[:, :, :], mx[:, :, 0:NB], -1.0, mparts[:, 0, :, :],
                                                    ALU.mult, ALU.subtract))
                link(nc.vector.tensor_copy(mparts[:, 1, :, :], mrest[:, :, :]))
                nc.vector.tensor_tensor(mparts[:, 2, :, :], mrest[:, :, :], mparts[:, 1, :, :], ALU.subtract
                                        ).then_inc(mparts_ready, 1)

            def normalise(q, c_):
                dve.wait_ge(ot_done, q * 2 + (c_ + 1))
                o = tr[:, :].rearrange("p (k h n) -> p k h n", k=TPC, h=QUAD)
                nc.vector.reciprocal(rden[:, :, :], o[:, :, :, HDA]).then_inc(rden_ready, 1)
                dve.wait_ge(rden_ready, q * 2 + (c_ + 1))
                dst = att[:, bass.ds((q * 2 + c_) * TPC * QUAD, TPC * QUAD), :]
                nc.vector.tensor_tensor(dst, o[:, :, :, 0:HDA].rearrange("p k h d -> p (k h) d"),
                                        rden[:, :, :].rearrange("p k (h o) -> p (k h) o", o=1)
                                        .broadcast_to([P, TPC * QUAD, HDA]), ALU.mult).then_inc(norm_done, 1)

            def quad(q, k, u, first, last):
                for g in range(NG):
                    if not last:
                        for n in share(g):
                            maximum(q + 1, n)
                    if g == 1 and not first:
                        normalise(q - 1, 1)
                    if g == 5:
                        normalise(q, 0)
                    if g == FIRST_GROUPS and not last:
                        split_maxima(q + 1)
                if last:
                    normalise(q, 1)

            for n in range(N1):
                maximum(0, n)
            split_maxima(0)
            quads(dve, quad)
            dve.wait_ge(norm_done, 2 * NQ)


def output_a(nc, t):
    x_sb, ident, att = t["x"], t["ident"], t["att"]
    with ExitStack() as c:
        sb = lambda n, s, d=F32: c.enter_context(nc.sbuf_tensor(n, s, d))
        sem = lambda n: c.enter_context(nc.semaphore(n))
        a = sb("oa_a", [P, 2, DL])
        aT = sb("oa_aT", [P, 2, DL])
        tp = [c.enter_context(nc.psum_tensor(f"oa_tp{i}", [P, CH], F32)) for i in range(2)]
        op = [c.enter_context(nc.psum_tensor(f"oa_op{i}", [P, CH], F32)) for i in range(2)]
        picked, turned, ready, done, added = (sem("oa_picked"), sem("oa_turned"), sem("oa_ready"), sem("oa_done"),
                                              sem("oa_added"))
        block = c.enter_context(nc.Block())
        view = att[:, :, :].rearrange("p (b g c k h) d -> p b c k g (h d)", b=B, g=QPB, c=T // CH, k=TPC)

        @block.gpsimd
        def _(pool):
            for i in range(NT):
                b, r = divmod(i, NB)
                if i >= 2:
                    pool.wait_ge(turned, i - 1)
                nc.gpsimd.tensor_copy(a[:, i % 2, :].rearrange("p (g n) -> p g n", g=QPB),
                                      view[:, b, r // TPC, r % TPC, :, :]).then_inc(picked, 1)

        @block.tensor
        def _(pe):
            def product(i):
                pe.wait_ge(ready, i + 1)
                if i >= 2:
                    pe.wait_ge(added, i - 1)
                nc.tensor.matmul(op[i % 2][:, 0:D], aT[:, i % 2, :], t["wo_a"][:, :], start=True, stop=True
                                 ).then_inc(done, 1)
            for i in range(NT):
                pe.wait_ge(picked, i + 1)
                if i >= 2:
                    pe.wait_ge(ready, i - 1)
                nc.tensor.transpose(tp[i % 2][:, 0:P], a[:, i % 2, :], ident[:, :]).then_inc(turned, 1)
                if i:
                    product(i - 1)
            product(NT - 1)

        @block.scalar
        def _(act):
            for i in range(NT):
                act.wait_ge(turned, i + 1)
                if i >= 2:
                    act.wait_ge(done, i - 1)
                nc.scalar.activation(aT[:, i % 2, :], tp[i % 2][:, 0:P], ACT.Copy).then_inc(ready, 1)

        @block.vector
        def _(dve):
            for i in range(NT):
                dve.wait_ge(done, i + 1)
                nc.vector.tensor_tensor(x_sb[:, i, :], op[i % 2][:, 0:D], x_sb[:, i, :], ALU.add).then_inc(added, 1)
            dve.wait_ge(added, NT)


E, SH, F = 16, 2, 128
NE = SH + E


SLOTS = 2 * TOK
TILES = (SLOTS + E * (P - 1)) // P
XIN = 4
GIN = 4


def expert_layer(nc, t, w, tag, load_weights):
    x_sb, ident, wt = t["x"], t["ident"], t["expert_w"]
    up_r, down_r, bias_up, bias_down = wt["up"], wt["down"], wt["bias_up"], wt["bias_down"]
    semaphores = []
    with ExitStack() as c:
        sb = lambda n, s, d=F32: c.enter_context(nc.sbuf_tensor(tag + n, s, d))

        def sem(n):
            semaphores.append(nc.alloc_semaphore(tag + n))
            return semaphores[-1]

        s = {"st": sb("st", [P, NT, 6]), "small": sb("small", [P, 7, NT])}
        xn, xT = sb("xn", [P, NT, D]), sb("xT", [P, NC, TOK])
        lgT = sb("lgT", [E, 2, CH])
        aff, key, second = (sb(n, [P, NT, E]) for n in ("aff", "key", "second"))
        one = [sb("one0", [P, NT, E]), sb("one1", [P, NT, E])]
        chosen = sb("chosen", [P, E, NT], BF16)
        top, idx, den = sb("top", [P, 2, NT]), sb("idx", [P, NT]), sb("den", [P, NT])
        before, total = sb("before", [P, E, NT]), sb("total", [P, E, NT])
        tiles_of, tiles_to = sb("tiles_of", [P, E]), sb("tiles_to", [P, E])
        ended = sb("ended", [1, TILES, E])
        expert_of, expert_id = sb("expert_of", [1, TILES]), sb("expert_id", [1, TILES], I32)
        placef, place = sb("placef", [P, 2, NT]), sb("place", [P, 2, NT], U32)
        gel, y = sb("gel", [P, 2, CH]), sb("y", [P, 2, SH, CH])
        xin, xsT = sb("xin", [P, XIN, D]), sb("xsT", [P, 2, NC, P])
        hg, yr, yT, yo = sb("hg", [P, 2, F]), sb("yr", [P, 2, F]), sb("yT", [P, 2, P]), sb("yo", [P, XIN, D])
        back = sb("back", [P, GIN, 2, D])
        bank = [c.enter_context(nc.psum_tensor(tag + f"bank{i}", [P, CH], F32)) for i in range(8)]

        ns = {k: sem(k) for k in ("stats", "dve_chain", "veps", "pow")}
        xn_ready, xt_done, xT_ready = sem("xn_ready"), sem("xt_done"), sem("xT_ready")
        lg_done, lg_out, lg_turned, exp_done = sem("lg_done"), sem("lg_out"), sem("lg_turned"), sem("exp_done")
        chain, chosen_ready, counted, counts_used, place_ready = (sem("chain"), sem("chosen"), sem("counted"),
                                                                  sem("counts_used"), sem("place"))
        scattered = sem("scattered")
        gu_done, gel_ready, y_ready, sh_done, sh_added = (sem("gu"), sem("gel"), sem("y"), sem("sh_done"),
                                                          sem("sh_added"))
        x_in = [sem(f"x_in{i}") for i in range(XIN)]
        y_out = [sem(f"y_out{i}") for i in range(XIN)]
        t1_done, t1_out, u_done, hg_ready, yr_ready, t2_done, t2_out, d_done, yo_ready = (
            sem(n) for n in ("t1_done", "t1_out", "u_done", "hg_ready", "yr_ready", "t2_done", "t2_out",
                             "d_done", "yo_ready"))
        kept = sem("kept")
        g_in = [sem(f"g_in{i}") for i in range(GIN)]
        joined = sem("joined")
        block = c.enter_context(nc.Block())

        def steps(eng, step, ahead):
            for j in range(2 * XIN):
                step(j, j % XIN, j // XIN)
            with eng.Fori(2, TILES // XIN) as r:
                for m in range(XIN):
                    step(r * XIN + m, m, r)
            for j in range(TILES // XIN * XIN, TILES + ahead):
                step(j, j % XIN, j // XIN)

        def round_of(m, r, back):
            return r if m >= back else r - 1

        def live(j, first=0):
            return not isinstance(j, int) or first <= j < TILES

        @block.sync
        def _(sp):
            if load_weights:
                sp.dma_start(wt["wa"][:, :, :], w["wa"].rearrange("(c p) e -> p c e", p=P)).then_inc(wt["wa_loaded"], 16)
                for e in range(SH):
                    for a, name in enumerate(("sg", "sw1")):
                        sp.dma_start(wt["up_s"][:, e, a, :, :], w[name][e].rearrange("(c p) f -> p c f", p=P)
                                     ).then_inc(wt["s_loaded"], 16)
                    sp.dma_start(wt["down_s"][:, e, :], w["sw2"][e]).then_inc(wt["s_loaded"], 16)
                for a, name in enumerate(("sgb", "sb1")):
                    sp.dma_start(wt["bias_s"][:, a, :], w[name].rearrange("e f -> f e"),
                                 allow_slow_non_contiguous=True).then_inc(wt["s_loaded"], 16)
                for e in range(SH):
                    sp.dma_start(wt["bias2_s"][:, e, :], w["sb2"][e:e + 1, :].partition_broadcast(P)
                                 ).then_inc(wt["s_loaded"], 16)
                for a, name in enumerate(("rg", "rw1")):
                    for m in range(NC):
                        sp.dma_start(up_r[:, :, m, a, :], w[name][:, m * P:(m + 1) * P, :].rearrange("e p f -> p e f")
                                     ).then_inc(wt["r_loaded"], 16)
                sp.dma_start(down_r[:, :, :], w["rw2"].rearrange("e f d -> f e d")).then_inc(wt["r_loaded"], 16)
                for a, name in enumerate(("rgb", "rb1")):
                    sp.dma_start(bias_up[:, :, a, :], w[name].rearrange("(o e) f -> o e f", o=1)
                                 ).then_inc(wt["r_loaded"], 16)
                sp.dma_start(bias_down[:, :, :], w["rb2"].rearrange("(o e) d -> o e d", o=1)).then_inc(wt["r_loaded"], 16)

            sp.wait_ge(scattered, 16 * 2 * NT)

            def step(j, m, r):
                if not (isinstance(j, int) and j < XIN):
                    sp.wait_ge(t1_done, j - (XIN - 1))
                sp.dma_start(xin[:, m, :], t["x_sorted"][bass.ds(j * P, P), :]).then_inc(x_in[m], 16)
            steps(sp, step, 0)
            for m in range(XIN):
                sp.wait_ge(y_out[m], 16 * len(range(m, TILES, XIN)))

        @block.gpsimd
        def _(pool):
            pool.wait_ge(ns["veps"], 1)
            nc.gpsimd.tensor_tensor(s["small"][:, 3, :], s["small"][:, 2, :], t["neg_half"][:, :], ALU.pow
                                    ).then_inc(ns["pow"], 1)
            pool.wait_ge(place_ready, 1)
            if load_weights:
                pool.wait_ge(t["x_sorted_cleared"], 16 * TILES)
            for i in range(NT):
                for r in range(2):
                    nc.gpsimd.indirect_dma_start(t["x_sorted"], bass.IndirectOffsetOnAxis(ap=place[:, r, i:i + 1], axis=0),
                                                 xn[:, i, :], None).then_inc(scattered, 16)
            for i in range(NT):
                pool.wait_ge(sh_added, i // 2 + 1)
                nc.gpsimd.tensor_tensor(x_sb[:, i, :], x_sb[:, i, :], xn[:, i, :], ALU.add).then_inc(kept, 1)
            for e in range(SH):
                for i in range(NT):
                    pool.wait_ge(kept, e * NT + i + 1)
                    nc.gpsimd.tensor_tensor(x_sb[:, i, :], x_sb[:, i, :], wt["bias2_s"][:, e, :], ALU.add
                                            ).then_inc(kept, 1)
            for m in range(XIN):
                pool.wait_ge(y_out[m], 16 * len(range(m, TILES, XIN)))
            for i in range(NT):
                if i >= GIN:
                    pool.wait_ge(joined, i - GIN + 1)
                for r in range(2):
                    nc.gpsimd.indirect_dma_start(back[:, i % GIN, r, :], None, t["y_sorted"],
                                                 bass.IndirectOffsetOnAxis(ap=place[:, r, i:i + 1], axis=0)
                                                 ).then_inc(g_in[i % GIN], 16)

        @block.vector
        def _(dve):
            mean, rstd = norm_statistics(nc, dve, None, x_sb, s, ns)
            for i in range(NT):
                nc.vector.tensor_scalar(xn[:, i, :], x_sb[:, i, :], mean[:, i:i + 1], rstd[:, i:i + 1],
                                        ALU.subtract, ALU.mult).then_inc(xn_ready, 1)
            link = link_on(dve, chain)
            wide = lambda a: a.rearrange("p (i o) -> p i o", o=1).broadcast_to([P, NT, E])
            dve.wait_ge(exp_done, 1)
            link(nc.vector.tensor_scalar(aff[:, :, :], aff[:, :, :], 1.0, None, ALU.add))
            link(nc.vector.reciprocal(aff[:, :, :], aff[:, :, :]))
            src = aff
            for r in range(2):
                link(nc.vector.tensor_reduce(top[:, r, :], src[:, :, :], AX.X, ALU.max))
                link(nc.vector.tensor_tensor(key[:, :, :], src[:, :, :], wide(top[:, r, :]), ALU.is_equal))
                link(nc.vector.scalar_tensor_tensor(key[:, :, :], key[:, :, :], -float(E), t["experts"][:, :, :],
                                                    ALU.mult, ALU.add))
                link(nc.vector.tensor_reduce(idx[:, :], key[:, :, :], AX.X, ALU.min))
                link(nc.vector.tensor_tensor(one[r][:, :, :], key[:, :, :], wide(idx[:, :]), ALU.is_equal))
                if r == 0:
                    link(nc.vector.scalar_tensor_tensor(second[:, :, :], one[0][:, :, :], -4.0, aff[:, :, :],
                                                        ALU.mult, ALU.add))
                    src = second
            nc.vector.tensor_tensor(chosen[:, :, :].rearrange("p e i -> p i e"), one[0][:, :, :], one[1][:, :, :],
                                    ALU.add).then_inc(chosen_ready, 1)
            link(nc.vector.tensor_tensor(den[:, :], top[:, 0, :], top[:, 1, :], ALU.add))
            link(nc.vector.reciprocal(den[:, :], den[:, :]))
            for r in range(2):
                link(nc.vector.tensor_tensor(top[:, r, :], top[:, r, :], den[:, :], ALU.mult))
            dve.wait_ge(counted, 1)
            cnt = bank[7][:, :].rearrange("p (k e i) -> p k e i", k=2, e=E)
            link(nc.vector.tensor_copy(total[:, :, :], cnt[:, 1, :, :]))
            flat = lambda a: a[:, :, :].rearrange("p e i -> p (e i)")
            link(nc.vector.tensor_tensor_scan(flat(before), flat(t["restart"]), flat(total), 0.0, ALU.mult, ALU.add))
            link(nc.vector.tensor_scalar(tiles_of[:, :], before[:, :, NT - 1], 1.0 / P, (P - 1 - 63.75) / P,
                                         ALU.mult, ALU.add))
            link(nc.vector.tensor_scalar(tiles_of[:, :], tiles_of[:, :], MAGIC, -MAGIC, ALU.add, ALU.add))
            link(nc.vector.tensor_tensor_scan(tiles_to[:, :], t["ones_e"][:, :], tiles_of[:, :], 0.0, ALU.mult,
                                              ALU.add))
            link(nc.vector.tensor_tensor(before[:, :, :], before[:, :, :], total[:, :, :], ALU.subtract))
            link(nc.vector.tensor_tensor(before[:, :, :], cnt[:, 0, :, :], before[:, :, :], ALU.add))
            nc.vector.tensor_tensor(ended[:, :, :], tiles_to[0:1, :].rearrange("p (o e) -> p o e", o=1)
                                    .broadcast_to([1, TILES, E]), t["tile_no"][:, :, :], ALU.is_le)
            link(nc.vector.tensor_tensor(tiles_of[:, :], tiles_to[:, :], tiles_of[:, :], ALU.subtract))
            link(nc.vector.scalar_tensor_tensor(before[:, :, :], tiles_of[:, :].rearrange("p (e o) -> p e o", o=1)
                                                .broadcast_to([P, E, NT]), float(P), before[:, :, :],
                                                ALU.mult, ALU.add))
            for r in range(2):
                link(nc.vector.tensor_tensor(key[:, :, :], one[r][:, :, :], before[:, :, :].rearrange("p e i -> p i e"),
                                             ALU.mult))
                link(nc.vector.tensor_reduce(placef[:, r, :], key[:, :, :], AX.X, ALU.add))
            nc.vector.tensor_copy(place[:, :, :], placef[:, :, :]).then_inc(place_ready, 1)
            link(nc.vector.tensor_reduce(expert_of[:, :], ended[:, :, :], AX.X, ALU.add))
            nc.vector.tensor_scalar(expert_id[:, :], expert_of[:, :], float(E - 1), None, ALU.min
                                    ).then_inc(place_ready, 1)

            def add_shared(j):
                for k in range(TPC // 2):
                    i = j * TPC + 2 * k
                    dve.wait_ge(sh_done, i // 2 + 1)
                    xs = x_sb[:, i:i + 2, :]
                    nc.vector.tensor_tensor(xs, bank[4 + k][:, :].rearrange("p (i d) -> p i d", i=2), xs, ALU.add
                                            ).then_inc(sh_added, 1)

            for j in range(NCH):
                for e in range(SH):
                    dve.wait_ge(gel_ready, j * SH + e + 1)
                    if j >= 2:
                        dve.wait_ge(sh_done, (j - 1) * TPC // 2)
                    nc.vector.scalar_tensor_tensor(y[:, j % 2, e, :], bank[2 * e + 1][:, :], wt["bias_s"][:, 1, e:e + 1],
                                                   gel[:, e, :], ALU.add, ALU.mult).then_inc(y_ready, 1)
                if j:
                    add_shared(j - 1)
            add_shared(NCH - 1)

            def step(j, m, r):
                a, d = j - 1, j - 3
                if live(d):
                    dve.wait_ge(d_done, d + 1)
                    if not (isinstance(d, int) and d < XIN):
                        dve.wait_ge(y_out[(m - 3) % XIN], round_of(m, r, 3) * 16)
                    nc.vector.tensor_copy(yo[:, (m - 3) % XIN, :], bank[6 + (m - 3) % 2][:, 0:D]).then_inc(yo_ready, 1)
                if live(a):
                    dve.wait_ge(hg_ready, a + 1)
                    if not (isinstance(a, int) and a < 2):
                        dve.wait_ge(t2_done, a - 1)
                    nc.vector.tensor_tensor(yr[:, (m - 1) % 2, :], hg[:, (m - 1) % 2, :],
                                            bank[2 + (m - 1) % 2][:, F:2 * F], ALU.mult).then_inc(yr_ready, 1)
            steps(dve, step, 3)

            dve.wait_ge(kept, (1 + SH) * NT)
            for i in range(NT):
                dve.wait_ge(g_in[i % GIN], 32 * (i // GIN + 1))
                link(nc.vector.scalar_tensor_tensor(x_sb[:, i, :], back[:, i % GIN, 0, :], top[:, 0, i:i + 1],
                                                    x_sb[:, i, :], ALU.mult, ALU.add))
                nc.vector.scalar_tensor_tensor(x_sb[:, i, :], back[:, i % GIN, 1, :], top[:, 1, i:i + 1],
                                               x_sb[:, i, :], ALU.mult, ALU.add).then_inc(joined, 1)
            dve.wait_ge(joined, NT)

        @block.tensor
        def _(pe):
            for j in range(NCH):
                for k in range(TPC):
                    i = j * TPC + k
                    pe.wait_ge(xn_ready, i + 1)
                    if j >= 2:
                        pe.wait_ge(xT_ready, NC * (j - 1))
                    for m in range(NC):
                        ins = nc.tensor.transpose(bank[j % 2 * NC + m][:, k * P:(k + 1) * P],
                                                  xn[:, i, m * P:(m + 1) * P], ident[:, :])
                ins.then_inc(xt_done, 1)
                pe.wait_ge(xT_ready, NC * (j + 1))
                if j == 0:
                    pe.wait_ge(wt["wa_loaded"], 16)
                if j >= 2:
                    pe.wait_ge(lg_out, j - 1)
                for m in range(NC):
                    ins = nc.tensor.matmul(bank[4 + j % 2][0:E, :], wt["wa"][:, m, :], xT[:, m, j * CH:(j + 1) * CH],
                                           start=m == 0, stop=m == NC - 1)
                ins.then_inc(lg_done, 1)
                pe.wait_ge(lg_out, j + 1)
                for k in range(TPC):
                    i = j * TPC + k
                    ins = nc.tensor.transpose(bank[6][:, i * E:(i + 1) * E], lgT[:, j % 2, k * P:(k + 1) * P],
                                              ident[0:E, 0:E])
                ins.then_inc(lg_turned, 1)

            def shared_up(j):
                for e in range(SH):
                    if j:
                        pe.wait_ge(y_ready, (j - 1) * SH + e + 1)
                    for a in range(2):
                        for m in range(NC):
                            ins = nc.tensor.matmul(bank[2 * e + a][:, :], wt["up_s"][:, e, a, m, :],
                                                   xT[:, m, j * CH:(j + 1) * CH], start=m == 0, stop=m == NC - 1)
                    ins.then_inc(gu_done, 1)

            def shared_down(j):
                pe.wait_ge(y_ready, SH * (j + 1))
                for k in range(TPC):
                    if j:
                        pe.wait_ge(sh_added, (j - 1) * TPC // 2 + k // 2 + 1)
                    for e in range(SH):
                        ins = nc.tensor.matmul(bank[4 + k // 2][:, k % 2 * D:(k % 2 + 1) * D],
                                               y[:, j % 2, e, k * P:(k + 1) * P], wt["down_s"][:, e, :],
                                               start=e == 0, stop=e == SH - 1)
                    if k % 2:
                        ins.then_inc(sh_done, 1)

            if load_weights:
                pe.wait_ge(wt["s_loaded"], 16 * (3 * SH + 2 + SH))
            shared_up(0)
            pe.wait_ge(chosen_ready, 1)
            ch = chosen[:, :, :].rearrange("p e i -> p (e i)")
            nc.tensor.matmul(bank[7][:, 0:NT * E], t["before_me"][:, :], ch, start=True, stop=True)
            nc.tensor.matmul(bank[7][:, NT * E:2 * NT * E], t["ones"][:, :], ch, start=True, stop=True
                             ).then_inc(counted, 1)
            for j in range(1, NCH):
                shared_up(j)
                shared_down(j - 1)
            shared_down(NCH - 1)

            pe.wait_ge(place_ready, 2)
            if load_weights:
                pe.wait_ge(wt["r_loaded"], 16 * 8)
            pe.wait_ge(y_ready, SH * NCH)
            pe.wait_ge(sh_added, NT // 2)

            number = [pe.alloc_register(f"{tag}expert{m}") for m in range(XIN)]

            def step(j, m, r):
                a, b, d = j - 1, j - 2, j - 3
                if live(j):
                    pe.load(number[m], expert_id[0:1, bass.ds(j, 1)])
                    pe.wait_ge(x_in[m], r * 16 + 16)
                    if not (isinstance(j, int) and j < 2):
                        pe.wait_ge(t1_out, j - 1)
                    for n in range(NC):
                        ins = nc.tensor.transpose(bank[m % 2][:, n * P:(n + 1) * P], xin[:, m, n * P:(n + 1) * P],
                                                  ident[:, :])
                    ins.then_inc(t1_done, 1)
                if live(a):
                    pe.wait_ge(t1_out, a + 1)
                    if not (isinstance(a, int) and a < 2):
                        pe.wait_ge(yr_ready, a - 1)
                    e = pe.snap(number[(m - 1) % XIN], min_val=0, max_val=E - 1)
                    u = (m - 1) % 2
                    nc.tensor.matmul(bank[2 + u][:, 0:2 * F], t["one_row"][:, :],
                                     bias_up[:, bass.ds(e, 1), :, :].rearrange("p o a f -> p (o a f)"),
                                     start=True, stop=False)
                    for n in range(NC):
                        ins = nc.tensor.matmul(bank[2 + u][:, 0:2 * F], xsT[:, u, n, :],
                                               up_r[:, bass.ds(e, 1), n, :, :].rearrange("p o a f -> p (o a f)"),
                                               start=False, stop=n == NC - 1)
                    ins.then_inc(u_done, 1)
                if live(b):
                    pe.wait_ge(yr_ready, b + 1)
                    if not (isinstance(b, int) and b < 2):
                        pe.wait_ge(t2_out, b - 1)
                    nc.tensor.transpose(bank[4 + m % 2][:, 0:P], yr[:, m % 2, :], ident[:, :]).then_inc(t2_done, 1)
                if live(d):
                    pe.wait_ge(t2_out, d + 1)
                    if not (isinstance(d, int) and d < 2):
                        pe.wait_ge(yo_ready, d - 1)
                    e = pe.snap(number[(m - 3) % XIN], min_val=0, max_val=E - 1)
                    u = (m - 3) % 2
                    nc.tensor.matmul(bank[6 + u][:, 0:D], t["one_row"][:, :],
                                     bias_down[:, bass.ds(e, 1), :].rearrange("p o d -> p (o d)"), start=True,
                                     stop=False)
                    nc.tensor.matmul(bank[6 + u][:, 0:D], yT[:, u, :],
                                     down_r[:, bass.ds(e, 1), :].rearrange("p o d -> p (o d)"), start=False, stop=True
                                     ).then_inc(d_done, 1)
            steps(pe, step, 3)


        @block.scalar
        def _(act):
            nc.scalar.preload_act_table(ACT.Exp)
            for j in range(NCH):
                act.wait_ge(xt_done, j + 1)
                for m in range(NC):
                    nc.scalar.activation(xT[:, m, j * CH:(j + 1) * CH], bank[j % 2 * NC + m][:, :], ACT.Copy
                                         ).then_inc(xT_ready, 1)
                act.wait_ge(lg_done, j + 1)
                if j >= 2:
                    act.wait_ge(lg_turned, j - 1)
                nc.scalar.activation(lgT[:, j % 2, :], bank[4 + j % 2][0:E, :], ACT.Copy).then_inc(lg_out, 1)
            act.wait_ge(lg_turned, NCH)
            nc.scalar.activation(aff[:, :, :], bank[6][:, 0:NT * E].rearrange("p (i e) -> p i e", e=E), ACT.Exp,
                                 scale=-1.0).then_inc(exp_done, 1)
            nc.scalar.preload_act_table(ACT.Gelu)
            if load_weights:
                act.wait_ge(wt["s_loaded"], 16 * (3 * SH + 2 + SH))
            for j in range(NCH):
                for e in range(SH):
                    n = j * SH + e
                    act.wait_ge(gu_done, n + 1)
                    if j:
                        act.wait_ge(y_ready, n - 1)
                    nc.scalar.activation(gel[:, e, :], bank[2 * e][:, :], ACT.Gelu, bias=wt["bias_s"][:, 0, e:e + 1]
                                         ).then_inc(gel_ready, 1)

            def step(j, m, r):
                a, b, o = j - 1, j - 2, j - XIN
                if live(o):
                    act.wait_ge(yo_ready, o + 1)
                    act.dma_start(t["y_sorted"][bass.ds(o * P, P), :], yo[:, m, :]).then_inc(y_out[m], 16)
                if live(j):
                    act.wait_ge(t1_done, j + 1)
                    if not (isinstance(j, int) and j < 2):
                        act.wait_ge(u_done, j - 1)
                    nc.scalar.activation(xsT[:, m % 2, :, :], bank[m % 2][:, 0:D].rearrange("p (c n) -> p c n", c=NC),
                                         ACT.Copy).then_inc(t1_out, 1)
                if live(a):
                    u = (m - 1) % 2
                    act.wait_ge(u_done, a + 1)
                    if not (isinstance(a, int) and a < 2):
                        act.wait_ge(yr_ready, a - 1)
                    nc.scalar.activation(hg[:, u, :], bank[2 + u][:, 0:F], ACT.Gelu).then_inc(hg_ready, 1)
                if live(b):
                    act.wait_ge(t2_done, b + 1)
                    if not (isinstance(b, int) and b < 2):
                        act.wait_ge(d_done, b - 1)
                    nc.scalar.activation(yT[:, m % 2, :], bank[4 + m % 2][:, 0:P], ACT.Copy).then_inc(t2_out, 1)
            steps(act, step, XIN)

    nc.all_engine_barrier()
    nc.clear_and_free_semaphores(semaphores)
    nc.all_engine_barrier()


HB = 16
HDB = D // HB
TWO_PI = 6.283185307179586
PI_IN = 3.1415925
C1 = 6.28125
C2 = 1.9350051879882812e-3
C3 = TWO_PI - C1 - C2


def rotation_tables(nc, t, w):
    ident = t["ident"]
    with ExitStack() as c:
        sb = lambda n, s, d=F32: c.enter_context(nc.sbuf_tensor("rt_" + n, s, d))
        sem = lambda n: c.enter_context(nc.semaphore("rt_" + n))
        H2 = HDB // 2
        freq, pos = sb("freq", [P, H2]), sb("pos", [P, NB])
        angle, turns, red = sb("angle", [P, NB, H2]), sb("turns", [P, 2, NB, H2]), sb("red", [P, 2, NB, H2])
        raw = {k: sb("raw_" + k, [P, NC, D]) for k in "qkvo"}
        tp = [c.enter_context(nc.psum_tensor(f"rt_tp{i}", [P, NC, D], F32)) for i in range(4)]
        loaded, w_loaded, pos_ready, chain, reduced, turned, copied, made = (
            sem("loaded"), sem("w_loaded"), sem("pos"), sem("chain"), sem("reduced"), sem("turned"), sem("copied"),
            sem("made"))
        block = c.enter_context(nc.Block())

        @block.sync
        def _(sp):
            sp.dma_start(freq[:, :], w["inv_freq"].rearrange("(o n) -> o n", o=1).partition_broadcast(P)
                         ).then_inc(loaded, 16)
            for k in "qkvo":
                sp.dma_start(raw[k][:, :, :], w["w" + k].rearrange("(c p) n -> p c n", p=P)).then_inc(w_loaded, 16)
            sp.wait_ge(w_loaded, 64)

        @block.gpsimd
        def _(pool):
            nc.gpsimd.iota(pos[:, :], [[P, NB]], base=0, channel_multiplier=1,
                           allow_small_or_imprecise_dtypes=True).then_inc(pos_ready, 1)

        @block.vector
        def _(dve):
            link = link_on(dve, chain)
            dve.wait_ge(loaded, 16)
            dve.wait_ge(pos_ready, 1)
            link(nc.vector.tensor_tensor(
                angle[:, :, :], pos[:, :].rearrange("p (k o) -> p k o", o=1).broadcast_to([P, NB, H2]),
                freq[:, :].rearrange("p (o n) -> p o n", o=1).broadcast_to([P, NB, H2]), ALU.mult))
            for r in range(2):
                tr, rd = turns[:, r, :, :], red[:, r, :, :]
                link(nc.vector.tensor_scalar(tr, angle[:, :, :], 1.0 / TWO_PI, 0.25 * r, ALU.mult, ALU.add))
                link(nc.vector.tensor_scalar(tr, tr, MAGIC, -MAGIC, ALU.add, ALU.add))
                link(nc.vector.scalar_tensor_tensor(rd, tr, -C1, angle[:, :, :], ALU.mult, ALU.add))
                link(nc.vector.scalar_tensor_tensor(rd, tr, -C2, rd, ALU.mult, ALU.add))
                link(nc.vector.scalar_tensor_tensor(rd, tr, -C3, rd, ALU.mult, ALU.add))
                if r:
                    link(nc.vector.tensor_scalar(rd, rd, TWO_PI / 4, None, ALU.add))
                nc.vector.tensor_scalar(rd, rd, PI_IN, -PI_IN, ALU.min, ALU.max).then_inc(reduced, 1)
            for i, k in enumerate("qkvo"):
                dve.wait_ge(turned, i + 1)
                dst = {"q": t["wqk"][:, :, 0:D], "k": t["wqk"][:, :, D:2 * D], "v": t["wv"][:, :, :],
                       "o": t["wo_b"][:, :, :]}[k]
                nc.vector.tensor_copy(dst, tp[i][:, :, :]).then_inc(copied, 1)
            dve.wait_ge(copied, 4)

        @block.scalar
        def _(act):
            for r in range(2):
                act.wait_ge(reduced, r + 1)
                nc.scalar.activation((t["sin"], t["cos"])[r][:, :, :], red[:, r, :, :], ACT.Sin).then_inc(made, 1)
            act.wait_ge(made, 2)

        @block.tensor
        def _(pe):
            pe.wait_ge(w_loaded, 64)
            for i, k in enumerate("qkvo"):
                for m in range(NC):
                    for n in range(NC):
                        ins = nc.tensor.transpose(tp[i][:, n, m * P:(m + 1) * P], raw[k][:, m, n * P:(n + 1) * P],
                                                  ident[:, :])
                ins.then_inc(turned, 1)


def attention_b(nc, t):
    x_sb, ident = t["x"], t["ident"]
    H2 = HDB // 2
    with ExitStack() as c:
        sb = lambda n, s, d=F32: c.enter_context(nc.sbuf_tensor("ab_" + n, s, d))
        sem = lambda n: c.enter_context(nc.semaphore("ab_" + n))
        s = {"st": sb("st", [P, NT, 6]), "small": sb("small", [P, 7, NT])}
        xn, xT = sb("xn", [P, 2, D]), sb("xT", [P, 2, NC, P])
        rot = sb("rot", [P, 2 * HB, HDB])
        cr = sb("cr", [P, 4, 2 * HB, H2])
        v = sb("v", [P, HB, HDB])
        prod = sb("prod", [P, HB, HB, HDB])
        sc, ex = sb("sc", [P, HB, HB]), sb("ex", [P, HB, HB])
        mx, dn = sb("mx", [P, HB]), sb("dn", [P, HB])
        o, oT = sb("o", [P, D]), sb("oT", [P, NC, P])
        ps = lambda n: c.enter_context(nc.psum_tensor("ab_" + n, [P, CH], F32))
        xt_ps = [ps("xt0"), ps("xt1")]
        qk_ps, v_ps, ot_ps, y_ps = [ps("qk0"), ps("qk1")], [ps("v0"), ps("v1")], ps("ot"), ps("y")
        ns = {k: sem(k) for k in ("stats", "dve_chain", "veps", "pow")}
        xn_ready, xt_done, xT_ready, qkv_done, qkv_used = (sem("xn_ready"), sem("xt_done"), sem("xT_ready"),
                                                           sem("qkv_done"), sem("qkv_used"))
        chain, sc_ready, ex_ready, o_ready, ot_done, oT_ready, y_done, added = (
            sem("chain"), sem("sc"), sem("ex"), sem("o"), sem("otd"), sem("oTr"), sem("y"), sem("added"))
        block = c.enter_context(nc.Block())

        @block.gpsimd
        def _(pool):
            pool.wait_ge(ns["veps"], 1)
            nc.gpsimd.tensor_tensor(s["small"][:, 3, :], s["small"][:, 2, :], t["neg_half"][:, :], ALU.pow
                                    ).then_inc(ns["pow"], 1)

        @block.vector
        def _(dve):
            mean, rstd = norm_statistics(nc, dve, None, x_sb, s, ns)

            def norm(i):
                if i >= 2:
                    dve.wait_ge(xt_done, i - 1)
                nc.vector.tensor_scalar(xn[:, i % 2, :], x_sb[:, i, :], mean[:, i:i + 1], rstd[:, i:i + 1],
                                        ALU.subtract, ALU.mult).then_inc(xn_ready, 1)

            link = link_on(dve, chain)
            norm(0)
            for i in range(NT):
                if i + 1 < NT:
                    norm(i + 1)
                dve.wait_ge(qkv_done, i + 1)
                qk = qk_ps[i % 2][:, :].rearrange("p (h n e) -> p h n e", n=H2, e=2)
                cos = t["cos"][:, i % NB:i % NB + 1, :].broadcast_to([P, 2 * HB, H2])
                sin = t["sin"][:, i % NB:i % NB + 1, :].broadcast_to([P, 2 * HB, H2])
                nc.vector.tensor_tensor(cr[:, 0, :, :], qk[:, :, :, 0], cos, ALU.mult)
                nc.vector.tensor_tensor(cr[:, 1, :, :], qk[:, :, :, 1], sin, ALU.mult)
                nc.vector.tensor_tensor(cr[:, 2, :, :], qk[:, :, :, 0], sin, ALU.mult)
                nc.vector.tensor_copy(v[:, :, :], v_ps[i % 2][:, 0:D].rearrange("p (h n) -> p h n", h=HB))
                link(nc.vector.tensor_tensor(cr[:, 3, :, :], qk[:, :, :, 1], cos, ALU.mult))
                nc.vector.tensor_tensor(rot[:, :, 0:H2], cr[:, 0, :, :], cr[:, 1, :, :], ALU.subtract
                                        ).then_inc(qkv_used, 1)
                link(nc.vector.tensor_tensor(rot[:, :, H2:HDB], cr[:, 2, :, :], cr[:, 3, :, :], ALU.add))
                bq = rot[:, 0:HB, :].rearrange("p h (o n) -> p h o n", o=1).broadcast_to([P, HB, HB, HDB])
                bk = rot[:, HB:2 * HB, :].rearrange("p (o h) n -> p o h n", o=1).broadcast_to([P, HB, HB, HDB])
                link(nc.vector.tensor_tensor(prod[:, :, :, :], bq, bk, ALU.mult))
                link(nc.vector.tensor_reduce(sc[:, :, :], prod[:, :, :, :], AX.X, ALU.add))
                link(nc.vector.tensor_reduce(mx[:, :], sc[:, :, :], AX.X, ALU.max))
                wide = lambda a, n: a.rearrange("p (h o) -> p h o", o=1).broadcast_to([P, HB, n])
                nc.vector.tensor_tensor(sc[:, :, :], sc[:, :, :], wide(mx[:, :], HB), ALU.subtract
                                        ).then_inc(sc_ready, 1)
                dve.wait_ge(ex_ready, i + 1)
                link(nc.vector.tensor_reduce(dn[:, :], ex[:, :, :], AX.X, ALU.add))
                bp = ex[:, :, :].rearrange("p h (o t) -> p h o t", o=1).broadcast_to([P, HB, HDB, HB])
                bv = v[:, :, :].rearrange("p (o t) n -> p o n t", o=1).broadcast_to([P, HB, HDB, HB])
                link(nc.vector.tensor_tensor(prod[:, :, :, :], bp, bv, ALU.mult))
                link(nc.vector.reciprocal(dn[:, :], dn[:, :]))
                oh = o[:, :].rearrange("p (h n) -> p h n", h=HB)
                if i:
                    dve.wait_ge(ot_done, i)
                link(nc.vector.tensor_reduce(oh, prod[:, :, :, :], AX.X, ALU.add))
                nc.vector.tensor_tensor(oh, oh, wide(dn[:, :], HDB), ALU.mult).then_inc(o_ready, 1)
                if i:
                    dve.wait_ge(y_done, i)
                    nc.vector.tensor_tensor(x_sb[:, i - 1, :], y_ps[:, 0:D], x_sb[:, i - 1, :], ALU.add
                                            ).then_inc(added, 1)
            dve.wait_ge(y_done, NT)
            nc.vector.tensor_tensor(x_sb[:, NT - 1, :], y_ps[:, 0:D], x_sb[:, NT - 1, :], ALU.add).then_inc(added, 1)
            dve.wait_ge(added, NT)

        @block.tensor
        def _(pe):
            def project(i):
                u = i % 2
                pe.wait_ge(xn_ready, i + 1)
                if i >= 2:
                    pe.wait_ge(xT_ready, i - 1)
                for m in range(NC):
                    ins = nc.tensor.transpose(xt_ps[u][:, m * P:(m + 1) * P], xn[:, u, m * P:(m + 1) * P], ident[:, :])
                ins.then_inc(xt_done, 1)
                pe.wait_ge(xT_ready, i + 1)
                if i >= 2:
                    pe.wait_ge(qkv_used, i - 1)
                for m in range(NC):
                    nc.tensor.matmul(qk_ps[u][:, :], xT[:, u, m, :], t["wqk"][:, m, :], start=m == 0, stop=m == NC - 1)
                for m in range(NC):
                    ins = nc.tensor.matmul(v_ps[u][:, 0:D], xT[:, u, m, :], t["wv"][:, m, :], start=m == 0,
                                           stop=m == NC - 1)
                ins.then_inc(qkv_done, 1)

            project(0)
            for i in range(NT):
                if i + 1 < NT:
                    project(i + 1)
                pe.wait_ge(o_ready, i + 1)
                if i:
                    pe.wait_ge(oT_ready, i)
                for m in range(NC):
                    ins = nc.tensor.transpose(ot_ps[:, m * P:(m + 1) * P], o[:, m * P:(m + 1) * P], ident[:, :])
                ins.then_inc(ot_done, 1)
                pe.wait_ge(oT_ready, i + 1)
                if i:
                    pe.wait_ge(added, i)
                for m in range(NC):
                    ins = nc.tensor.matmul(y_ps[:, 0:D], oT[:, m, :], t["wo_b"][:, m, :], start=m == 0, stop=m == NC - 1)
                ins.then_inc(y_done, 1)

        @block.scalar
        def _(act):
            nc.scalar.preload_act_table(ACT.Exp)

            def turn(i):
                act.wait_ge(xt_done, i + 1)
                if i >= 2:
                    act.wait_ge(qkv_done, i - 1)
                nc.scalar.activation(xT[:, i % 2, :, :], xt_ps[i % 2][:, 0:D].rearrange("p (c n) -> p c n", c=NC),
                                     ACT.Copy).then_inc(xT_ready, 1)
            turn(0)
            for i in range(NT):
                if i + 1 < NT:
                    turn(i + 1)
                act.wait_ge(sc_ready, i + 1)
                nc.scalar.activation(ex[:, :, :], sc[:, :, :], ACT.Exp, scale=float(HDB) ** -0.5).then_inc(ex_ready, 1)
                act.wait_ge(ot_done, i + 1)
                if i:
                    act.wait_ge(y_done, i)
                nc.scalar.activation(oT[:, :, :], ot_ps[:, 0:D].rearrange("p (c n) -> p c n", c=NC), ACT.Copy
                                     ).then_inc(oT_ready, 1)


def rest_of_layers(nc, t, w, stop):
    ffn = {k.removeprefix("L0_ffn_"): v for k, v in w.items() if "ffn" in k}
    b = {k.removeprefix("L0_attn_b_"): v for k, v in w.items() if "attn_b" in k}
    expert_layer(nc, t, ffn, "l2", True)
    if stop > 2:
        with ExitStack() as c:
            sb = lambda n, s, d=F32: c.enter_context(nc.sbuf_tensor(n, s, d))
            t["sin"], t["cos"] = sb("sin", [P, NB, HDB // 2]), sb("cos", [P, NB, HDB // 2])
            t["wqk"], t["wv"], t["wo_b"] = sb("wqk", [P, NC, 2 * D]), sb("wv", [P, NC, D]), sb("wo_b", [P, NC, D])
            rotation_tables(nc, t, b)
            attention_b(nc, t)
    if stop > 3:
        expert_layer(nc, t, ffn, "l4", False)


def build(nc, stop=9, out=None, **w):
    nc.disable_value_cache = True
    with ExitStack() as c:
        sb = lambda n, s, d=F32: c.enter_context(nc.sbuf_tensor(n, s, d))
        t = {
            "x": sb("x_sb", [P, NT, D]), "ident": sb("ident", [P, P]), "identb": sb("identb", [P, P], BF16),
            "mask_s": sb("mask_s", [P, P], BF16), "mask_t": sb("mask_t", [P, P], BF16),
            "neg_half": sb("neg_half", [P, NT]), "experts": sb("experts", [P, NT, E]),
            "restart": sb("restart", [P, E, NT]), "ones_e": sb("ones_e", [P, E]),
            "tile_no": sb("tile_no", [1, TILES, E]), "one_row": sb("one_row", [1, P]),
            "before_me": sb("before_me", [P, P], BF16), "ones": sb("ones", [P, P], BF16), "zeros": sb("zeros", [P, D]),
            "x_sorted": nc.dram_tensor("x_sorted", (TILES * P, D), F32, kind="Internal").ap(),
            "y_sorted": nc.dram_tensor("y_sorted", (TILES * P, D), F32, kind="Internal").ap(),
        }
        t["x_loaded"] = c.enter_context(nc.semaphore("x_loaded"))
        t["x_sorted_cleared"] = c.enter_context(nc.semaphore("x_sorted_cleared"))
        constants(nc, c, t)
        a = {k.removeprefix("L0_attn_a_"): v for k, v in w.items() if "attn_a" in k}
        with ExitStack() as ca:
            sa = lambda n, s, d=F32: ca.enter_context(nc.sbuf_tensor(n, s, d))
            t["wf"], t["bf"] = sa("wf", [P, 3, NC, DL]), sa("bf", [P, 3])
            t["wo_a"], t["bo_a"] = sa("wo_a", [P, D]), sa("bo_a", [P, D])
            t["v"] = sa("v_all", [P, NQ, NB, QUAD * HDA])
            t["att"] = sa("att", [P, NQ * NB * QUAD, HDA])
            t["q_parts"] = nc.dram_tensor("q_parts", (B * HA, 2 * PARTS - 1, HDA, T), BF16, kind="Internal").ap()
            t["k_parts"] = nc.dram_tensor("k_parts", (B * HA, PARTS, HDA, T), BF16, kind="Internal").ap()
            fold_weights(nc, t, a)
            project_a(nc, t)
            attention_a(nc, t)
            output_a(nc, t)
        if stop > 1:
            with ExitStack() as ce:
                se = lambda n, s, d=F32: ce.enter_context(nc.sbuf_tensor("ew_" + n, s, d))
                t["expert_w"] = {
                    "up": se("up", [P, E, NC, 2, F]), "down": se("down", [P, E, D]),
                    "bias_up": se("bias_up", [1, E, 2, F]), "bias_down": se("bias_down", [1, E, D]),
                    "up_s": se("up_s", [P, SH, 2, NC, F]), "down_s": se("down_s", [P, SH, D]),
                    "bias_s": se("bias_s", [P, 2, SH]), "bias2_s": se("bias2_s", [P, SH, D]),
                    "wa": se("wa", [P, NC, E]),
                    **{n: ce.enter_context(nc.semaphore("ew_" + n)) for n in ("wa_loaded", "s_loaded", "r_loaded")},
                }
                rest_of_layers(nc, t, w, stop)
        stored = c.enter_context(nc.semaphore("stored"))
        with nc.Block() as block:
            @block.sync
            def _(sp):
                sp.dma_start(out.rearrange("b (i p) d -> p (b i) d", p=P), t["x"][:, :, :]).then_inc(stored, 16)
                sp.wait_ge(stored, 16)


_OUT = (B, T, D)


def kernel(**inputs):
    import numpy as np
    import concourse.bacc as bacc
    from concourse.bass_utils import run_bass_kernel_spmd

    nc = bacc.Bacc("TRN2", target_bir_lowering=False, num_devices=1)
    arrays = {name: np.ascontiguousarray(a) for name, a in inputs.items()}
    args = {name: nc.dram_tensor("in_" + name, a.shape, mybir.dt.from_np(a.dtype), kind="ExternalInput").ap()
            for name, a in arrays.items()}
    out = nc.dram_tensor("out_x", _OUT, F32, kind="ExternalOutput").ap()
    build(nc, out=out, **args)
    r = run_bass_kernel_spmd(nc, [{"in_" + name: a for name, a in arrays.items()}], core_ids=[0])
    return r.results[0]["out_x"]
```

```python
from contextlib import ExitStack

import concourse.bass as bass
from concourse import mybir

P = 128
F32 = mybir.dt.float32
BF16 = mybir.dt.bfloat16
I32 = mybir.dt.int32
U32 = mybir.dt.uint32
ALU = mybir.AluOpType
ACT = mybir.ActivationFunctionType
AX = mybir.AxisListType

B, T, D = 2, 1024, 256
TOK = B * T
NT = TOK // P
NC = D // P
CH = 512
NCH = TOK // CH
TPC = CH // P
EPS = 1e-5

HA = 16
DL = 128
HDA = DL // HA
QUAD = 4
NQ = B * HA // QUAD
QPB = NQ // B
PARTS = 3
COMBOS = PARTS * PARTS
KR = COMBOS * HDA
KM = KR + PARTS
NB = T // P
BIG = 1e30
MAGIC = 1.5 * 2 ** 23


HB = 16
HP = 7
HDB = D // HB
TWO_PI = 6.283185307179586
PI_IN = 3.1415925
C1 = 6.28125
C2 = 1.9350051879882812e-3
C3 = TWO_PI - C1 - C2


def link_on(eng, sem, start=0):
    count = [start]

    def link(ins):
        count[0] = count[0] + 1
        ins.then_inc(sem, 1)
        eng.wait_ge(sem, count[0])

    return link


CONSTANTS = 9


def constants(nc, pool, tiles, cleared, made):
    ident, identb, mask_s, mask_t = tiles["ident"], tiles["identb"], tiles["mask_s"], tiles["mask_t"]
    nc.gpsimd.memset(ident[:, :], 0.0).then_inc(cleared, 1)
    nc.gpsimd.memset(identb[:, :], 0.0).then_inc(cleared, 1)
    nc.gpsimd.memset(mask_s[:, :], 0.0).then_inc(cleared, 1)
    nc.gpsimd.memset(mask_t[:, :], 0.0).then_inc(cleared, 1)
    nc.gpsimd.memset(tiles["neg_half"][:, :], -0.5).then_inc(made, 1)
    pool.wait_ge(cleared, 4)
    for m in (ident, identb):
        nc.gpsimd.affine_select(out=m[:, :], in_=m[:, :], compare_op=ALU.not_equal, fill=1.0, base=0,
                                pattern=[[-1, P]], channel_multiplier=1).then_inc(made, 1)
    nc.gpsimd.affine_select(out=mask_s[:, :], in_=mask_s[:, :], compare_op=ALU.is_ge, fill=-BIG, base=0,
                            pattern=[[-1, P]], channel_multiplier=1).then_inc(made, 1)
    nc.gpsimd.affine_select(out=mask_t[:, :], in_=mask_t[:, :], compare_op=ALU.is_ge, fill=-BIG, base=0,
                            pattern=[[1, P]], channel_multiplier=-1).then_inc(made, 1)
    nc.gpsimd.iota(tiles["experts"][:, :, :], [[0, NT], [1, E]], base=E, channel_multiplier=0,
                   allow_small_or_imprecise_dtypes=True).then_inc(made, 1)
    for name, value in (("restart", 1.0), ("ones_e", 1.0), ("ones", 1.0), ("before_me", 1.0), ("zeros", 0.0),
                        ("one_rows", 1.0)):
        whole = tiles[name][:, :, :] if name == "restart" else tiles[name][:, :]
        nc.gpsimd.memset(whole, value).then_inc(cleared, 1)
    nc.gpsimd.iota(tiles["tile_no"][:, :, :], [[1, TILES], [0, E]], base=0, channel_multiplier=0,
                   allow_small_or_imprecise_dtypes=True).then_inc(made, 1)
    pool.wait_ge(cleared, 10)
    nc.gpsimd.memset(tiles["restart"][:, :, 0:1], 0.0).then_inc(made, 1)
    nc.gpsimd.affine_select(out=tiles["before_me"][:, :], in_=tiles["before_me"][:, :], compare_op=ALU.is_gt,
                            fill=0.0, base=0, pattern=[[1, P]], channel_multiplier=-1).then_inc(made, 1)
    pool.wait_ge(made, CONSTANTS)


def tile_statistics(nc, t, i):
    return nc.vector.bn_stats(t["stats"][:, bass.ds(i, 1), :], t["x"][:, bass.ds(i, 1), :])


def norm_statistics(nc, dve, t, s, sem):
    st, small = t["stats"], s["small"]
    mean, rstd, veps, r0, dif, cvs, tmp = (small[:, k, :] for k in range(7))
    link = link_on(dve, sem["dve_chain"])
    nc.vector.tensor_tensor(tmp, st[:, :, 1], st[:, :, 4], ALU.add)
    nc.vector.tensor_tensor(dif, st[:, :, 1], st[:, :, 4], ALU.subtract)
    link(nc.vector.tensor_tensor(cvs, st[:, :, 2], st[:, :, 5], ALU.add))
    nc.vector.tensor_scalar(mean, tmp, 0.5, None, ALU.mult)
    nc.vector.tensor_scalar(cvs, cvs, 1.0 / D, EPS, ALU.mult, ALU.add)
    link(nc.vector.tensor_tensor(dif, dif, dif, ALU.mult))
    nc.vector.scalar_tensor_tensor(veps, dif, 0.25, cvs, ALU.mult, ALU.add).then_inc(sem["veps"], 1)
    dve.wait_ge(sem["veps"], 1)
    dve.wait_ge(sem["pow"], 1)
    link(nc.vector.tensor_tensor(tmp, r0, r0, ALU.mult))
    link(nc.vector.tensor_tensor(tmp, tmp, veps, ALU.mult))
    link(nc.vector.tensor_scalar(tmp, tmp, -0.5, 1.5, ALU.mult, ALU.add))
    link(nc.vector.tensor_tensor(rstd, r0, tmp, ALU.mult))
    return mean, rstd


def fold_weights(nc, t, w):
    x_sb, ident = t["x"], t["ident"]
    with ExitStack() as c:
        sb = lambda n, s, d=F32: c.enter_context(nc.sbuf_tensor(n, s, d))
        sem = lambda n: c.enter_context(nc.semaphore(n))
        w1 = {k: sb(f"w1_{k}", [P, NC, D]) for k in "qkv"}
        w1t = {k: sb(f"w1t_{k}", [P, NC, D]) for k in "qkv"}
        w2 = {k: sb(f"w2_{k}", [P, NC, DL]) for k in "qkv"}
        bcol = sb("bcol", [P, 3, NC])
        blcol = sb("blcol", [P, 3, 1])
        tp = c.enter_context(nc.psum_tensor("fold_tp", [P, 3, NC, D], F32))
        fp = c.enter_context(nc.psum_tensor("fold_fp", [P, 3, 512], F32))
        loaded = {k: sem(f"fold_loaded_{k}") for k in "qkv"}
        bias_in = sem("fold_bias_in")
        turned, turned_out, folded, out = sem("fold_turned"), sem("fold_turned_out"), sem("fold_done"), sem("fold_out")
        cleared, made, x_in, measured = (sem("const_cleared"), sem("const_made"),
                                         [sem(f"fold_x_in{j}") for j in range(NCH)], sem("fold_measured"))
        block = c.enter_context(nc.Block())

        @block.gpsimd
        def _(pool):
            constants(nc, pool, t, cleared, made)

        @block.sync
        def _(sp):
            for k in "qkv":
                sp.dma_start(w1[k][:, :, :], w[f"w{k}"].rearrange("(c p) n -> p c n", p=P)).then_inc(loaded[k], 16)
                sp.dma_start(w2[k][:, :, :], w[f"w{k}l"].rearrange("(c p) n -> p c n", p=P)).then_inc(loaded[k], 16)
            sp.dma_start(t["wo_a"][:, :], w["wo"]).then_inc(t["wo_loaded"], 16)
            sp.dma_start(t["bo_a"][:, :], w["bo"].rearrange("(o n) -> o n", o=1).partition_broadcast(P)
                         ).then_inc(t["wo_loaded"], 16)

        @block.scalar
        def _(act):
            for j in range(NCH):
                b, r = divmod(j * CH, T)
                act.dma_start(x_sb[:, j * TPC:(j + 1) * TPC, :], w["x"][b, r:r + CH, :]
                              .rearrange("(i p) d -> p i d", p=P)).then_inc(x_in[j], 16)
            for i, k in enumerate("qkv"):
                act.dma_start(bcol[:, i, :], w[f"b{k}"].rearrange("(c p) -> p c", p=P),
                              allow_slow_non_contiguous=True).then_inc(bias_in, 16)
                act.dma_start(blcol[:, i, :], w[f"b{k}l"].rearrange("(p o) -> p o", o=1)).then_inc(bias_in, 16)

        @block.tensor
        def _(pe):
            pe.wait_ge(made, CONSTANTS)
            for i, k in enumerate("qkv"):
                pe.wait_ge(loaded[k], 32)
                for m in range(NC):
                    for n in range(NC):
                        ins = nc.tensor.transpose(tp[:, i, n, m * P:(m + 1) * P], w1[k][:, m, n * P:(n + 1) * P],
                                                  ident[:, :])
                ins.then_inc(turned, 1)
            pe.wait_ge(bias_in, 96)
            for i, k in enumerate("qkv"):
                pe.wait_ge(turned_out, i + 1)
                for m in range(NC):
                    for n in range(NC):
                        nc.tensor.matmul(fp[:, i, m * DL:(m + 1) * DL], w1t[k][:, n, m * P:(m + 1) * P],
                                         w2[k][:, n, :], start=n == 0, stop=n == NC - 1)
                for n in range(NC):
                    ins = nc.tensor.matmul(fp[:, i, NC * DL:NC * DL + 1], w2[k][:, n, :], bcol[:, i, n:n + 1],
                                           start=n == 0, stop=n == NC - 1)
                ins.then_inc(folded, 1)

        @block.vector
        def _(dve):
            for j in range(NCH):
                dve.wait_ge(x_in[j], 16)
                for k in range(TPC):
                    tile_statistics(nc, t, j * TPC + k).then_inc(measured, 1)
            dve.wait_ge(measured, NT)
            for i, k in enumerate("qkv"):
                dve.wait_ge(turned, i + 1)
                nc.vector.tensor_copy(w1t[k][:, :, :], tp[:, i, :, :]).then_inc(turned_out, 1)
            for i, k in enumerate("qkv"):
                dve.wait_ge(folded, i + 1)
                nc.vector.tensor_copy(t["wf"][:, i, :, :], fp[:, i, 0:NC * DL].rearrange("p (c n) -> p c n", c=NC)
                                      ).then_inc(out, 1)
                nc.vector.tensor_tensor(t["bf"][:, i:i + 1], fp[:, i, NC * DL:NC * DL + 1], blcol[:, i, :],
                                        ALU.add).then_inc(out, 1)
            dve.wait_ge(out, 6)


def load_stack(sp, t, q, u):
    for r in range(PARTS):
        rows = slice(r * PARTS * HDA, (r + 1) * PARTS * HDA)
        sp.dma_start(t["qst"][rows, u, :, :],
                     t["q_parts"][bass.ds(q * QUAD, QUAD), r:r + PARTS, :, :].rearrange("h r d t -> (r d) h t")
                     ).then_inc(t["stack"][u], 16)
        sp.dma_start(t["kst"][rows, u, :, :],
                     t["k_parts"][bass.ds(q * QUAD, QUAD), :, :, :].rearrange("h r d t -> (r d) h t")
                     ).then_inc(t["stack"][u], 16)


def project_a(nc, t):
    x_sb, ident, wf, bf = t["x"], t["ident"], t["wf"], t["bf"]
    qs, ks = t["q_parts"], t["k_parts"]
    with ExitStack() as c:
        sb = lambda n, s, d=F32: c.enter_context(nc.sbuf_tensor(n, s, d))
        sem = lambda n: c.enter_context(nc.semaphore(n))
        s = {"small": sb("pa_small", [P, 7, NT])}
        xn = sb("pa_xn", [P, 2 * TPC, D])
        xT = sb("pa_xT", [P, 2, NC, CH])
        rest = sb("pa_rest", [P, 2, CH])
        parts = sb("pa_parts", [P, 2, 2, PARTS, CH], BF16)
        vT = sb("pa_vT", [P, CH])
        xt_ps = c.enter_context(nc.psum_tensor("pa_xt", [P, NC, CH], F32))
        qk_ps = c.enter_context(nc.psum_tensor("pa_qk", [P, 2, CH], F32))
        v_ps = c.enter_context(nc.psum_tensor("pa_v", [P, CH], F32))
        vt_ps = c.enter_context(nc.psum_tensor("pa_vt", [P, CH], F32))
        ns = {k: sem(f"pa_{k}") for k in ("dve_chain", "veps", "pow")}
        xn_ready, xt_done, xT_ready = sem("pa_xn_ready"), sem("pa_xt_done"), sem("pa_xT_ready")
        qk_done, qk_free = sem("pa_qk_done"), sem("pa_qk_free")
        high, mid, low = sem("pa_high"), sem("pa_mid"), sem("pa_low")
        v_done, vT_ready, vt_done, v_out = sem("pa_v_done"), sem("pa_vT_ready"), sem("pa_vt_done"), sem("pa_v_out")
        saved_q, saved_k = [sem("pa_saved_q0"), sem("pa_saved_q1")], [sem("pa_saved_k0"), sem("pa_saved_k1")]
        block = c.enter_context(nc.Block())

        @block.gpsimd
        def _(pool):
            pool.wait_ge(ns["veps"], 1)
            nc.gpsimd.tensor_tensor(s["small"][:, 3, :], s["small"][:, 2, :], t["neg_half"][:, :], ALU.pow
                                    ).then_inc(ns["pow"], 1)
            pool.wait_ge(ns["pow"], 1)
            nc.gpsimd.memset(t["kst"][64:KM, :, :, :], 1.0).then_inc(t["rows_set"], 1)
            nc.gpsimd.memset(t["qst"][64:KM, :, :, :], 0.0).then_inc(t["rows_set"], 1)
            for j in range(NCH):
                u, b, t0 = j % 2, j * CH // T, j * CH % T
                pool.wait_ge(mid, 2 * j + 2)
                pool.wait_ge(low, 2 * j + 2)
                for r in range(PARTS):
                    pool.dma_start(ks[b * HA:(b + 1) * HA, r, :, t0:t0 + CH], parts[:, u, 1, r, :]
                                   ).then_inc(saved_k[u], 16)

        @block.vector
        def _(dve):
            mean, rstd = norm_statistics(nc, dve, t, s, ns)
            def norm(j):
                if j >= 2:
                    dve.wait_ge(xt_done, j - 1)
                for k in range(TPC):
                    i = j * TPC + k
                    nc.vector.tensor_scalar(xn[:, j % 2 * TPC + k, :], x_sb[:, i, :], mean[:, i:i + 1],
                                            rstd[:, i:i + 1], ALU.subtract, ALU.mult).then_inc(xn_ready, 1)

            norm(0)
            for j in range(NCH):
                u = j % 2
                if j + 1 < NCH:
                    norm(j + 1)
                for g in range(2):
                    n = 2 * j + g
                    dve.wait_ge(high, n + 1)
                    if n >= 2:
                        dve.wait_ge(low, n - 1)
                    nc.vector.scalar_tensor_tensor(rest[:, g, :], qk_ps[:, g, :], bf[:, g:g + 1],
                                                   parts[:, u, g, 0, :], ALU.add, ALU.subtract).then_inc(qk_free, 1)
                for g in range(2):
                    n = 2 * j + g
                    dve.wait_ge(mid, n + 1)
                    nc.vector.tensor_tensor(parts[:, u, g, 2, :], rest[:, g, :], parts[:, u, g, 1, :],
                                            ALU.subtract).then_inc(low, 1)
                dve.wait_ge(vt_done, j + 1)
                b, k0 = j * TPC // NB, j * TPC % NB
                nc.vector.tensor_copy(t["v"][:, b * QPB:(b + 1) * QPB, k0:k0 + TPC, :],
                                      vt_ps[:, :].rearrange("p (i q n) -> p q i n", i=TPC, q=QPB)).then_inc(v_out, 1)

        @block.tensor
        def _(pe):
            def turn(j):
                for k in range(TPC):
                    pe.wait_ge(xn_ready, j * TPC + k + 1)
                    if j >= 1:
                        pe.wait_ge(xT_ready, 2 * j)
                    for m in range(NC):
                        ins = nc.tensor.transpose(xt_ps[:, m, k * P:(k + 1) * P],
                                                  xn[:, j % 2 * TPC + k, m * P:(m + 1) * P], ident[:, :])
                ins.then_inc(xt_done, 1)

            turn(0)
            for j in range(NCH):
                u = j % 2
                pe.wait_ge(xT_ready, 2 * j + 2)
                if j >= 1:
                    pe.wait_ge(qk_free, 2 * j)
                    pe.wait_ge(vT_ready, j)
                for g in range(3):
                    dst = v_ps[:, :] if g == 2 else qk_ps[:, g, :]
                    for m in range(NC):
                        ins = nc.tensor.matmul(dst, wf[:, g, m, :], xT[:, u, m, :], start=m == 0, stop=m == NC - 1)
                    ins.then_inc(v_done if g == 2 else qk_done, 1)
                if j + 1 < NCH:
                    turn(j + 1)
                pe.wait_ge(vT_ready, j + 1)
                if j >= 1:
                    pe.wait_ge(v_out, j)
                for k in range(TPC):
                    ins = nc.tensor.transpose(vt_ps[:, k * P:(k + 1) * P], vT[:, k * P:(k + 1) * P], ident[:, :])
                ins.then_inc(vt_done, 1)

        @block.scalar
        def _(act):
            def move(j):
                act.wait_ge(xt_done, j + 1)
                if j >= 2:
                    act.wait_ge(v_done, j - 1)
                for m in range(NC):
                    nc.scalar.activation(xT[:, j % 2, m, :], xt_ps[:, m, :], ACT.Copy).then_inc(xT_ready, 1)

            move(0)
            for j in range(NCH):
                u = j % 2
                for g in range(2):
                    act.wait_ge(qk_done, 2 * j + g + 1)
                    if j >= 2:
                        act.wait_ge((saved_q, saved_k)[g][u], 16 * (5, 3)[g] * (j // 2))
                    nc.scalar.activation(parts[:, u, g, 0, :], qk_ps[:, g, :], ACT.Identity,
                                         bias=bf[:, g:g + 1]).then_inc(high, 1)
                act.wait_ge(v_done, j + 1)
                if j >= 1:
                    act.wait_ge(vt_done, j)
                nc.scalar.activation(vT[:, :], v_ps[:, :], ACT.Identity, bias=bf[:, 2:3]).then_inc(vT_ready, 1)
                if j + 1 < NCH:
                    move(j + 1)
                for g in range(2):
                    act.wait_ge(qk_free, 2 * j + g + 1)
                    nc.scalar.activation(parts[:, u, g, 1, :], rest[:, g, :], ACT.Copy).then_inc(mid, 1)

        @block.sync
        def _(sp):
            for j in range(NCH):
                u, b, t0 = j % 2, j * CH // T, j * CH % T
                sp.wait_ge(mid, 2 * j + 1)
                sp.wait_ge(low, 2 * j + 1)
                for r in range(2 * PARTS - 1):
                    sp.dma_start(qs[b * HA:(b + 1) * HA, r, :, t0:t0 + CH], parts[:, u, 0, r % PARTS, :]
                                 ).then_inc(saved_q[u], 16)
                if (j + 1) * CH == T:
                    for k in range(2):
                        sp.wait_ge(saved_q[k], 16 * (2 * PARTS - 1))
                        sp.wait_ge(saved_k[k], 16 * PARTS)
                    sp.wait_ge(t["rows_set"], 2)
                    load_stack(sp, t, 0, 0)
            for u in range(2):
                sp.wait_ge(saved_q[u], 16 * (2 * PARTS - 1) * NCH // 2)
                sp.wait_ge(saved_k[u], 16 * PARTS * NCH // 2)


PIECES1 = [(tb, s0, min(s0 + CH, (tb + 1) * P)) for tb in range(NB) for s0 in range(0, (tb + 1) * P, CH)]
GROUPS2 = [(c, sb) for c in range(T // CH) for sb in range((c + 1) * CH // P)]
N1 = QUAD * len(PIECES1)
NG = len(GROUPS2)
N2 = QUAD * NG
SHARED_FROM, SHARED_TO = 2, NG - 3
TURN_GROUP = SHARED_TO
RS = 3


def share(g):
    k, n = g - SHARED_FROM, SHARED_TO - SHARED_FROM
    return range(k * N1 // n, (k + 1) * N1 // n) if 0 <= k < n else range(0)


def piece1(n):
    h, k = divmod(n, len(PIECES1))
    tb, s0, s1 = PIECES1[k]
    col = tb if s0 == 0 else NB + tb - CH // P
    return h, tb, s0, s1, col


def rotation_angles(nc, dve, t):
    a, H2 = t["angles"], HDB // 2
    freq, pos, angle, turns, red = (a[n] for n in ("freq", "pos", "angle", "turns", "red"))
    link = link_on(dve, a["chain"])
    dve.wait_ge(a["loaded"], 16)
    dve.wait_ge(a["pos_ready"], 1)
    link(nc.vector.tensor_tensor(
        angle[:, :, :], pos[:, :].rearrange("p (k o) -> p k o", o=1).broadcast_to([P, NB, H2]),
        freq[:, :].rearrange("p (o n) -> p o n", o=1).broadcast_to([P, NB, H2]), ALU.mult))
    for r in range(2):
        tr, rd = turns[:, r, :, :], red[:, r, :, :]
        link(nc.vector.tensor_scalar(tr, angle[:, :, :], 1.0 / TWO_PI, 0.25 * r, ALU.mult, ALU.add))
        link(nc.vector.tensor_scalar(tr, tr, MAGIC, -MAGIC, ALU.add, ALU.add))
        link(nc.vector.scalar_tensor_tensor(rd, tr, -C1, angle[:, :, :], ALU.mult, ALU.add))
        link(nc.vector.scalar_tensor_tensor(rd, tr, -C2, rd, ALU.mult, ALU.add))
        link(nc.vector.scalar_tensor_tensor(rd, tr, -C3, rd, ALU.mult, ALU.add))
        if r:
            link(nc.vector.tensor_scalar(rd, rd, TWO_PI / 4, None, ALU.add))
        nc.vector.tensor_scalar(rd, rd, PI_IN, -PI_IN, ALU.min, ALU.max).then_inc(a["reduced"], 1)
    dve.wait_ge(a["reduced"], 2)


class OutputSteps:

    def __init__(self, nc, t, tp, op):
        self.nc, self.t, self.tp, self.op = nc, t, tp, op
        self.a, self.aT = t["out_a"], t["out_aT"]
        self.picked, self.turned, self.ready, self.done, self.added, self.measured = (
            t["out_" + n] for n in ("picked", "turned", "ready", "done", "added", "measured"))
        self.view = t["att"][:, :, :].rearrange("p (b g c k h) d -> p b c k g (h d)", b=B, g=QPB, c=T // CH, k=TPC)

    def pick(self, pool, i):
        b, r = divmod(i, NB)
        if i >= 2:
            pool.wait_ge(self.turned, i - 1)
        self.nc.gpsimd.tensor_copy(self.a[:, i % 2, :].rearrange("p (g n) -> p g n", g=QPB),
                                   self.view[:, b, r // TPC, r % TPC, :, :]).then_inc(self.picked, 1)

    def turn(self, pe, i):
        pe.wait_ge(self.picked, i + 1)
        if i >= 2:
            pe.wait_ge(self.ready, i - 1)
        self.nc.tensor.transpose(self.tp[i % len(self.tp)][:, 0:P], self.a[:, i % 2, :], self.t["ident"][:, :]
                                 ).then_inc(self.turned, 1)

    def move(self, act, i):
        act.wait_ge(self.turned, i + 1)
        if i >= 2:
            act.wait_ge(self.done, i - 1)
        self.nc.scalar.activation(self.aT[:, i % 2, :], self.tp[i % len(self.tp)][:, 0:P], ACT.Copy
                                  ).then_inc(self.ready, 1)

    def product(self, pe, i):
        pe.wait_ge(self.ready, i + 1)
        if i >= len(self.op):
            pe.wait_ge(self.added, i - len(self.op) + 1)
        self.nc.tensor.matmul(self.op[i % len(self.op)][:, 0:D], self.aT[:, i % 2, :], self.t["wo_a"][:, :],
                              start=True, stop=True).then_inc(self.done, 1)

    def add(self, dve, i):
        xs = self.t["x"][:, i, :]
        dve.wait_ge(self.done, i + 1)
        self.nc.vector.tensor_tensor(xs, self.op[i % len(self.op)][:, 0:D], xs, ALU.add).then_inc(self.added, 1)
        if i:
            dve.wait_ge(self.added, i)
            tile_statistics(self.nc, self.t, i - 1).then_inc(self.measured, 1)

    def finish(self, dve):
        dve.wait_ge(self.added, NT)
        tile_statistics(self.nc, self.t, NT - 1).then_inc(self.measured, 1)
        dve.wait_ge(self.measured, NT)


def attention_a(nc, t, inv_freq):
    v_all, identb, ident = t["v"], t["identb"], t["ident"]
    att, qst, kst, stack = t["att"], t["qst"], t["kst"], t["stack"]
    NM = NB + NB - CH // P
    with ExitStack() as c:
        sb = lambda n, s, d=F32: c.enter_context(nc.sbuf_tensor(n, s, d))
        sem = lambda n: c.enter_context(nc.semaphore(n))
        vq = sb("vq", [P, 2, NB, QUAD, 32])
        pt = sb("pt", [P, RS, QUAD, CH])
        mx = sb("mx", [P, QUAD, NM])
        mrest = sb("mrest", [P, QUAD, NB])
        mparts = sb("mparts", [P, PARTS, QUAD, NB], BF16)
        mrow = sb("mrow", [PARTS * QUAD * NB, P], BF16)
        oT = sb("oT", [P, CH])
        rden = sb("rden", [P, TPC, QUAD])
        s1 = [c.enter_context(nc.psum_tensor(f"s1_{i}", [P, CH], F32)) for i in range(RS)]
        st = [c.enter_context(nc.psum_tensor(f"st_{i}", [P, CH], F32)) for i in range(RS)]
        o_ps = c.enter_context(nc.psum_tensor("o_ps", [P, CH], F32))
        tr = c.enter_context(nc.psum_tensor("tr", [P, CH], F32))
        v_set, bias_added = sem("aa_v_set"), sem("aa_bias_added")
        s1_done, s1_used = sem("aa_s1_done"), sem("aa_s1_used")
        max_chain, rden_ready = sem("aa_max_chain"), sem("aa_rden_ready")
        mparts_ready, mt_done, mrow_ready = sem("aa_mparts"), sem("aa_mt_done"), sem("aa_mrow_ready")
        mrow_in = [sem("aa_mrow_in0"), sem("aa_mrow_in1")]
        st_done, exp_done, av_done = sem("aa_st_done"), sem("aa_exp_done"), sem("aa_av_done")
        v_ready, oT_ready, ot_done, norm_done = (sem("aa_v_ready"), sem("aa_oT_ready"), sem("aa_ot_done"),
                                                 sem("aa_norm_done"))
        block = c.enter_context(nc.Block())
        STACK = 16 * 2 * PARTS
        MROW = 16

        steps = OutputSteps(nc, t, s1[0:2], s1[2:3])
        LINKS = 4

        def quads(eng, body):
            body(0, 0, 0, True, False)
            with eng.Fori(0, NQ // 2 - 1) as i:
                body(i * 2 + 1, i, 1, False, False)
                body(i * 2 + 2, i + 1, 0, False, False)
            body(NQ - 1, NQ // 2 - 1, 1, False, True)

        @block.sync
        def _(sp):
            def max_rows(q, u):
                sp.wait_ge(mrow_ready, q + 1)
                sp.dma_start(qst[KR:KM, u, :, :].rearrange("r h (k p) -> r (h k) p", p=P), mrow[:, :]
                             ).then_inc(mrow_in[u], 16)

            def step(q, u):
                max_rows(q + 1, 1 - u)
                sp.wait_ge(st_done, (q + 1) * N2)
                load_stack(sp, t, q + 2, u)

            load_stack(sp, t, 1, 1)
            max_rows(0, 0)
            sp.dma_start(t["angles"]["freq"][:, :], inv_freq.rearrange("(o n) -> o n", o=1).partition_broadcast(P)
                         ).then_inc(t["angles"]["loaded"], 16)
            with sp.Fori(0, NQ // 2 - 1) as i:
                step(i * 2, 0)
                step(i * 2 + 1, 1)
            max_rows(NQ - 1, 1)
            for u in range(2):
                sp.wait_ge(mrow_in[u], MROW * NQ // 2)
                sp.wait_ge(stack[u], STACK * NQ // 2)

        @block.gpsimd
        def _(pool):
            nc.gpsimd.iota(t["angles"]["pos"][:, :], [[P, NB]], base=0, channel_multiplier=1,
                           allow_small_or_imprecise_dtypes=True).then_inc(t["angles"]["pos_ready"], 1)
            nc.gpsimd.memset(vq[:, :, :, :, :], 0.0).then_inc(v_set, 1)
            pool.wait_ge(v_set, 1)
            nc.gpsimd.memset(vq[:, :, :, :, HDA:HDA + 1], 1.0).then_inc(v_set, 1)
            pool.wait_ge(v_set, 2)

            def copy_v(q, u):
                src = v_all[:, q, :, :] if isinstance(q, int) else v_all[:, bass.ds(q, 1), :, :]
                src = src.rearrange("p (o k) (h d) -> p (o k) h d" if isinstance(q, int) else
                                    "p o k (h d) -> p (o k) h d", h=QUAD, **({"o": 1} if isinstance(q, int) else {}))
                nc.gpsimd.tensor_copy(vq[:, u, :, :, 0:HDA], src).then_inc(v_ready, 1)

            copy_v(0, 0)
            copy_v(1, 1)
            with pool.Fori(0, NT) as i:
                xs = t["x"][:, bass.ds(i, 1), :]
                nc.gpsimd.tensor_tensor(xs, xs, t["bo_a"][:, :].rearrange("p (o n) -> p o n", o=1), ALU.add
                                        ).then_inc(bias_added, 1)
            def clear(j):
                pool.dma_start(t["x_sorted"][bass.ds(j * P, P), :], t["zeros"][:, :]
                               ).then_inc(t["x_sorted_cleared"], 16)

            rounds = NQ // 2 - 1
            with pool.Fori(0, rounds) as i:
                for u in range(2):
                    pool.wait_ge(av_done, (i * 2 + 1 + u) * NG)
                    copy_v(i * 2 + 2 + u, u)
                for k in range(TILES // rounds):
                    clear(i * (TILES // rounds) + k)
            for j in range(TILES // rounds * rounds, TILES):
                clear(j)
            pool.wait_ge(bias_added, NT)
            pool.wait_ge(v_ready, NQ)
            pool.wait_ge(norm_done, 2 * QPB)
            for i in range(NB):
                steps.pick(pool, i)
                pool.wait_ge(steps.picked, i + 1)

        @block.tensor
        def _(pe):
            def scores(q, u, n):
                h, tb, k0, k1, _col = piece1(n)
                if not (isinstance(q, int) and q == 0 and n < RS):
                    pe.wait_ge(s1_used, q * N1 + (n - RS + 1))
                diagonal = k1 == (tb + 1) * P
                ins = nc.tensor.matmul(s1[n % RS][:, 0:k1 - k0], qst[0:KR, u, h, tb * P:(tb + 1) * P],
                                       kst[0:KR, u, h, k0:k1], start=True, stop=not diagonal)
                if diagonal:
                    ins = nc.tensor.matmul(s1[n % RS][:, k1 - k0 - P:k1 - k0], identb[:, :], t["mask_s"][:, :],
                                           start=False, stop=True)
                ins.then_inc(s1_done, 1)

            def scores_t(q, u, g, h):
                c_, kb = GROUPS2[g]
                t0 = max(c_ * CH, kb * P)
                w = (c_ + 1) * CH - t0
                n = g * QUAD + h
                if not (isinstance(q, int) and q == 0 and n < RS):
                    pe.wait_ge(exp_done, q * N2 + (n - RS + 1))
                diagonal = kb * P >= c_ * CH
                ins = nc.tensor.matmul(st[n % RS][:, 0:w], kst[:, u, h, kb * P:(kb + 1) * P],
                                       qst[:, u, h, t0:t0 + w], start=True, stop=not diagonal)
                if diagonal:
                    ins = nc.tensor.matmul(st[n % RS][:, 0:P], identb[:, :], t["mask_t"][:, :],
                                           start=False, stop=True)
                ins.then_inc(st_done, 1)

            def values(q, u, g):
                c_, kb = GROUPS2[g]
                w = (c_ + 1) * CH - max(c_ * CH, kb * P)
                pe.wait_ge(exp_done, q * N2 + (g + 1) * QUAD)
                if kb == 0:
                    pe.wait_ge(v_ready, q + 1)
                    if not (isinstance(q, int) and q == 0 and c_ == 0):
                        pe.wait_ge(oT_ready, q * 2 + c_)
                last = kb == (c_ + 1) * CH // P - 1
                for h in range(QUAD):
                    ins = nc.tensor.matmul(o_ps[32 * h:32 * h + 32, CH - w:CH], vq[:, u, kb, h, :],
                                           pt[:, g % RS, h, 0:w], start=kb == 0, stop=last, skip_group_check=True)
                ins.then_inc(av_done, 1)

            def turn_output(q, c_):
                pe.wait_ge(oT_ready, q * 2 + (c_ + 1))
                for k in range(TPC):
                    ins = nc.tensor.transpose(tr[:, k * P:(k + 1) * P], oT[:, k * P:(k + 1) * P], ident[:, :])
                ins.then_inc(ot_done, 1)

            def turn_maxima(q):
                pe.wait_ge(mparts_ready, q + 1)
                n = PARTS * QUAD * NB
                nc.tensor.transpose(tr[0:n, 0:P // 2].bitcast(BF16),
                                    mparts[:, :, :, :].rearrange("p r h k -> p (r h k)"), identb[:, :]
                                    ).then_inc(mt_done, 1)

            def quad(q, k, u, first, last):
                pe.wait_ge(mrow_in[u], (k + 1) * MROW)
                for g in range(NG):
                    if g == SHARED_FROM and not last:
                        pe.wait_ge(stack[1 - u], (k + u + 1) * STACK)
                    todo = [] if last else list(share(g))
                    per = -(-len(todo) // QUAD)
                    for h in range(QUAD):
                        scores_t(q, u, g, h)
                        for n in todo[h * per:(h + 1) * per]:
                            scores(q + 1, 1 - u, n)
                    if g > 0:
                        values(q, u, g - 1)
                    elif not first:
                        values(q - 1, 1 - u, NG - 1)
                    if g == 1 and not first:
                        pe.wait_ge(mrow_ready, q + 1)
                        turn_output(q - 1, 1)
                    if g == 5:
                        if first:
                            pe.wait_ge(mrow_ready, 1)
                        else:
                            pe.wait_ge(norm_done, q * 2)
                        turn_output(q, 0)
                    if g == TURN_GROUP and not last:
                        pe.wait_ge(norm_done, q * 2 + 1)
                        turn_maxima(q + 1)
                    if last and g == 0:
                        pe.wait_ge(s1_used, NQ * N1)
                        pe.wait_ge(t["wo_loaded"], 32)
                    if last and g < NB:
                        steps.turn(pe, g)
                    if last and 2 <= g < NB + 2:
                        steps.product(pe, g - 2)
                if last:
                    values(q, u, NG - 1)
                    pe.wait_ge(norm_done, q * 2 + 1)
                    turn_output(q, 1)

            pe.wait_ge(stack[0], STACK)
            for n in range(N1):
                scores(0, 0, n)
            turn_maxima(0)
            quads(pe, quad)

        @block.scalar
        def _(act):
            nc.scalar.preload_act_table(ACT.Exp)

            def move_maxima(q, k, u):
                act.wait_ge(mt_done, q + 1)
                if not (isinstance(q, int) and q == 0):
                    act.wait_ge(mrow_in[1 - u], (k + u) * MROW)
                n = PARTS * QUAD * NB
                nc.scalar.activation(mrow[:, :], tr[0:n, 0:P // 2].bitcast(BF16), ACT.Copy).then_inc(mrow_ready, 1)

            def move_output(q, c_):
                act.wait_ge(av_done, q * NG + (NG if c_ else CH // P))
                if not (isinstance(q, int) and q == 0 and c_ == 0):
                    act.wait_ge(ot_done, q * 2 + c_)
                nc.scalar.activation(oT[:, :], o_ps[:, :], ACT.Copy).then_inc(oT_ready, 1)

            def quad(q, k, u, first, last):
                for g in range(NG):
                    c_, kb = GROUPS2[g]
                    w = (c_ + 1) * CH - max(c_ * CH, kb * P)
                    if not (first and g < RS):
                        act.wait_ge(av_done, q * NG + (g - RS + 1))
                    for h in range(QUAD):
                        n = g * QUAD + h
                        act.wait_ge(st_done, q * N2 + (n + 1))
                        nc.scalar.activation(pt[:, g % RS, h, 0:w], st[n % RS][:, 0:w], ACT.Exp,
                                             scale=float(HDA) ** -0.5).then_inc(exp_done, 1)
                    if g == 0 and not first:
                        move_output(q - 1, 1)
                    if g == CH // P:
                        move_output(q, 0)
                    if g == TURN_GROUP and not last:
                        move_maxima(q + 1, k + u, 1 - u)
                    if last and 1 <= g < NB + 1:
                        steps.move(act, g - 1)
                if last:
                    move_output(q, 1)

            move_maxima(0, 0, 0)
            quads(act, quad)

        @block.vector
        def _(dve):
            def maximum(q, n):
                h, tb, k0, k1, col = piece1(n)
                dve.wait_ge(s1_done, q * N1 + (n + 1))
                nc.vector.reduce_max(mx[:, h, col:col + 1], s1[n % RS][:, 0:k1 - k0], AX.X).then_inc(s1_used, 1)

            def split_maxima(q):
                dve.wait_ge(s1_used, q * N1 + N1)
                link = link_on(dve, max_chain, q * LINKS)
                two = CH // P
                link(nc.vector.tensor_tensor(mx[:, :, two:NB], mx[:, :, two:NB], mx[:, :, NB:NM], ALU.max))
                if not (isinstance(q, int) and q == 0):
                    dve.wait_ge(mt_done, q)
                link(nc.vector.tensor_scalar(mparts[:, 0, :, :], mx[:, :, 0:NB], -1.0, None, ALU.mult))
                link(nc.vector.scalar_tensor_tensor(mrest[:, :, :], mx[:, :, 0:NB], -1.0, mparts[:, 0, :, :],
                                                    ALU.mult, ALU.subtract))
                link(nc.vector.tensor_copy(mparts[:, 1, :, :], mrest[:, :, :]))
                nc.vector.tensor_tensor(mparts[:, 2, :, :], mrest[:, :, :], mparts[:, 1, :, :], ALU.subtract
                                        ).then_inc(mparts_ready, 1)

            def normalise(q, c_):
                dve.wait_ge(ot_done, q * 2 + (c_ + 1))
                o = tr[:, :].rearrange("p (k h n) -> p k h n", k=TPC, h=QUAD)
                nc.vector.reciprocal(rden[:, :, :], o[:, :, :, HDA]).then_inc(rden_ready, 1)
                dve.wait_ge(rden_ready, q * 2 + (c_ + 1))
                dst = att[:, bass.ds((q * 2 + c_) * TPC * QUAD, TPC * QUAD), :]
                nc.vector.tensor_tensor(dst, o[:, :, :, 0:HDA].rearrange("p k h d -> p (k h) d"),
                                        rden[:, :, :].rearrange("p k (h o) -> p (k h) o", o=1)
                                        .broadcast_to([P, TPC * QUAD, HDA]), ALU.mult).then_inc(norm_done, 1)

            def quad(q, k, u, first, last):
                for g in range(NG):
                    if not last:
                        for n in share(g):
                            maximum(q + 1, n)
                    if g == 1 and not first:
                        normalise(q - 1, 1)
                    if g == 5:
                        normalise(q, 0)
                    if g == SHARED_TO and not last:
                        split_maxima(q + 1)
                    if last and g == 0:
                        rotation_angles(nc, dve, t)
                    if last and g == 2:
                        dve.wait_ge(bias_added, NT)
                    if last and 2 <= g < NB + 2:
                        steps.add(dve, g - 2)
                if last:
                    normalise(q, 1)

            for n in range(N1):
                maximum(0, n)
            split_maxima(0)
            quads(dve, quad)
            dve.wait_ge(norm_done, 2 * NQ)


def output_a(nc, t, w):
    ident = t["ident"]
    with ExitStack() as c:
        sb = lambda n, s, d=F32: c.enter_context(nc.sbuf_tensor(n, s, d))
        sem = lambda n: c.enter_context(nc.semaphore(n))
        tp = [c.enter_context(nc.psum_tensor(f"oa_tp{i}", [P, CH], F32)) for i in range(2)]
        op = [c.enter_context(nc.psum_tensor(f"oa_op{i}", [P, CH], F32)) for i in range(2)]
        steps = OutputSteps(nc, t, tp, op)
        raw = {k: sb("rt_raw_" + k, [P, NC, D]) for k in "qkvo"}
        w_tp = [c.enter_context(nc.psum_tensor(f"rt_tp{i}", [P, NC, D], F32)) for i in range(4)]
        w_loaded, w_turned, copied, made = (sem("rt_" + n) for n in ("w_loaded", "turned", "copied", "made"))
        red = t["angles"]["red"]
        block = c.enter_context(nc.Block())

        @block.sync
        def _(sp):
            for k in "qkvo":
                sp.dma_start(raw[k][:, :, :], w["w" + k].rearrange("(c p) n -> p c n", p=P)).then_inc(w_loaded, 16)
            sp.wait_ge(w_loaded, 64)

        @block.gpsimd
        def _(pool):
            for i in range(NB, NT):
                steps.pick(pool, i)

        @block.tensor
        def _(pe):
            for i in range(NB, NT):
                steps.turn(pe, i)
                if i > NB:
                    steps.product(pe, i - 1)
            steps.product(pe, NT - 1)

            pe.wait_ge(w_loaded, 64)
            for i, k in enumerate("qkvo"):
                for m in range(NC):
                    for n in range(NC):
                        ins = nc.tensor.transpose(w_tp[i][:, n, m * P:(m + 1) * P], raw[k][:, m, n * P:(n + 1) * P],
                                                  ident[:, :])
                ins.then_inc(w_turned, 1)

        @block.scalar
        def _(act):
            for r in range(2):
                for f, e, sign in (((0, 1, -1.0), (1, 0, 1.0)), ((0, 0, 1.0), (1, 1, 1.0)))[r]:
                    for b in range(B):
                        table = t["rotation"][:, b * NB:(b + 1) * NB, f, :].rearrange("p i (n e) -> p i n e", e=2)
                        nc.scalar.activation(
                            table[:, :, :, e],
                            red[:, r, :, :], ACT.Sin, scale=sign).then_inc(made, 1)
            for i in range(NB, NT):
                steps.move(act, i)
            act.wait_ge(made, 4 * B)

        @block.vector
        def _(dve):
            for i in range(NB, NT):
                steps.add(dve, i)
            steps.finish(dve)

            for i, k in enumerate("qkvo"):
                dve.wait_ge(w_turned, i + 1)
                dst = {"q": t["wqk"][:, :, 0:D], "k": t["wqk"][:, :, D:2 * D], "v": t["wv"][:, :, :],
                       "o": t["wo_b"][:, :, :]}[k]
                nc.vector.tensor_copy(dst, w_tp[i][:, :, :]).then_inc(copied, 1)
            dve.wait_ge(copied, 4)


E, SH, F = 16, 2, 128


SLOTS = 2 * TOK
TILES = (SLOTS + E * (P - 1)) // P
NBIAS = E * (2 * F + D)
XIN = 4
GIN = 4


def expert_layer(nc, t, w, tag, load_weights, out=None):
    x_sb, ident, wt = t["x"], t["ident"], t["expert_w"]
    up_r, down_r = wt["up"], wt["down"]
    bias_up = wt["bias"][:, 0:2 * E * F].rearrange("r (a e f) -> r a e f", a=2, e=E)
    bias_down = wt["bias"][:, 2 * E * F:NBIAS].rearrange("r (e d) -> r e d", e=E)
    semaphores = []
    with ExitStack() as c:
        sb = lambda n, s, d=F32: c.enter_context(nc.sbuf_tensor(tag + n, s, d))

        def sem(n):
            semaphores.append(nc.alloc_semaphore(tag + n))
            return semaphores[-1]

        s = {"small": sb("small", [P, 7, NT])}
        xn, xT = sb("xn", [P, NT, D]), sb("xT", [P, NC, TOK])
        lgT = sb("lgT", [E, 2, CH])
        aff, key, second = (sb(n, [P, NT, E]) for n in ("aff", "key", "second"))
        one = [sb("one0", [P, NT, E]), sb("one1", [P, NT, E])]
        chosen = sb("chosen", [P, E, NT], BF16)
        top, idx, den = sb("top", [P, 2, NT]), sb("idx", [P, NT]), sb("den", [P, NT])
        before, total = sb("before", [P, E, NT]), sb("total", [P, E, NT])
        tiles_of, tiles_to = sb("tiles_of", [P, E]), sb("tiles_to", [P, E])
        ended = sb("ended", [1, TILES, E])
        expert_of, expert_id = sb("expert_of", [1, TILES]), sb("expert_id", [1, TILES], I32)
        placef, place = sb("placef", [P, 2, NT]), sb("place", [P, 2, NT], U32)
        bias_in, bias_parts = sb("bias_in", [P, NBIAS // P]), sb("bias_parts", [P, PARTS, NBIAS // P], BF16)
        gel, y = sb("gel", [P, 2, CH]), sb("y", [P, 2, SH, CH])
        xin, xsT = sb("xin", [P, XIN, D]), sb("xsT", [P, 2, NC, P])
        hg, yr, yT, yo = sb("hg", [P, 2, F]), sb("yr", [P, 2, F]), sb("yT", [P, 2, P]), sb("yo", [P, XIN, D])
        back = sb("back", [P, GIN, 2, D])
        bank = [c.enter_context(nc.psum_tensor(tag + f"bank{i}", [P, CH], F32)) for i in range(8)]

        ns = {k: sem(k) for k in ("dve_chain", "veps", "pow")}
        xn_ready, xt_done, xT_ready = sem("xn_ready"), sem("xt_done"), sem("xT_ready")
        lg_done, lg_out, lg_turned, exp_done = sem("lg_done"), sem("lg_out"), sem("lg_turned"), sem("exp_done")
        chain, chosen_ready, counted, place_ready = sem("chain"), sem("chosen"), sem("counted"), sem("place")
        scattered = sem("scattered")
        bias_raw, bias_split, bias_rest = sem("bias_raw"), sem("bias_split"), sem("bias_rest")
        gu_done, gel_ready, y_ready, sh_done, sh_added = (sem("gu"), sem("gel"), sem("y"), sem("sh_done"),
                                                          sem("sh_added"))
        x_in = [sem(f"x_in{i}") for i in range(XIN)]
        y_out = [sem(f"y_out{i}") for i in range(XIN)]
        t1_done, t1_out, u_done, hg_ready, yr_ready, t2_done, t2_out, d_done, yo_ready = (
            sem(n) for n in ("t1_done", "t1_out", "u_done", "hg_ready", "yr_ready", "t2_done", "t2_out",
                             "d_done", "yo_ready"))
        kept = sem("kept")
        g_in = [sem(f"g_in{i}") for i in range(GIN)]
        joined, measured, stored = sem("joined"), sem("measured"), sem("stored")
        block = c.enter_context(nc.Block())

        def steps(eng, step, ahead):
            for j in range(2 * XIN):
                step(j, j % XIN, j // XIN)
            with eng.Fori(2, TILES // XIN) as r:
                for m in range(XIN):
                    step(r * XIN + m, m, r)
            for j in range(TILES // XIN * XIN, TILES + ahead):
                step(j, j % XIN, j // XIN)

        def round_of(m, r, back):
            return r if m >= back else r - 1

        def live(j, first=0):
            return not isinstance(j, int) or first <= j < TILES

        @block.sync
        def _(sp):
            if load_weights:
                sp.dma_start(bias_in[0:P // 4, :], w["rgb"].rearrange("e (k n) -> (e k) n", n=NBIAS // P)
                             ).then_inc(bias_raw, 16)
                sp.dma_start(bias_in[P // 4:P // 2, :], w["rb1"].rearrange("e (k n) -> (e k) n", n=NBIAS // P)
                             ).then_inc(bias_raw, 16)
                sp.dma_start(bias_in[P // 2:P, :], w["rb2"].rearrange("e (k n) -> (e k) n", n=NBIAS // P)
                             ).then_inc(bias_raw, 16)
                sp.dma_start(wt["wa"][:, :, :], w["wa"].rearrange("(c p) e -> p c e", p=P)).then_inc(wt["wa_loaded"], 16)
                for e in range(SH):
                    for a, name in enumerate(("sg", "sw1")):
                        sp.dma_start(wt["up_s"][:, e, a, :, :], w[name][e].rearrange("(c p) f -> p c f", p=P)
                                     ).then_inc(wt["s_loaded"], 16)
                    sp.dma_start(wt["down_s"][:, e, :], w["sw2"][e]).then_inc(wt["s_loaded"], 16)
                for a, name in enumerate(("sgb", "sb1")):
                    sp.dma_start(wt["bias_s"][:, a, :], w[name].rearrange("e f -> f e"),
                                 allow_slow_non_contiguous=True).then_inc(wt["s_loaded"], 16)
                for e in range(SH):
                    sp.dma_start(wt["bias2_s"][:, e, :], w["sb2"][e:e + 1, :].partition_broadcast(P)
                                 ).then_inc(wt["s_loaded"], 16)
                for a, name in enumerate(("rg", "rw1")):
                    for m in range(NC):
                        sp.dma_start(up_r[:, :, m, a, :], w[name][:, m * P:(m + 1) * P, :].rearrange("e p f -> p e f")
                                     ).then_inc(wt["r_loaded"], 16)
                sp.dma_start(down_r[:, :, :], w["rw2"].rearrange("e f d -> f e d")).then_inc(wt["r_loaded"], 16)
                sp.wait_ge(bias_split, 3)
                for r in range(PARTS):
                    sp.dma_start(wt["bias"][r:r + 1, :].rearrange("o (p n) -> o p n", p=P), bias_parts[:, r, :]
                                 ).then_inc(wt["bias_loaded"], 16)

            sp.wait_ge(scattered, 16 * 2 * NT)

            def step(j, m, r):
                if not (isinstance(j, int) and j < XIN):
                    sp.wait_ge(t1_done, j - (XIN - 1))
                sp.dma_start(xin[:, m, :], t["x_sorted"][bass.ds(j * P, P), :]).then_inc(x_in[m], 16)
            steps(sp, step, 0)
            for m in range(XIN):
                sp.wait_ge(y_out[m], 16 * len(range(m, TILES, XIN)))
            if out is not None:
                tiles = out.rearrange("b (i p) d -> (b i) p d", p=P)
                for i in range(NT):
                    sp.wait_ge(joined, i + 1)
                    sp.dma_start(tiles[i], x_sb[:, i, :]).then_inc(stored, 16)
                sp.wait_ge(stored, 16 * NT)

        @block.gpsimd
        def _(pool):
            pool.wait_ge(ns["veps"], 1)
            nc.gpsimd.tensor_tensor(s["small"][:, 3, :], s["small"][:, 2, :], t["neg_half"][:, :], ALU.pow
                                    ).then_inc(ns["pow"], 1)
            if load_weights:
                pool.wait_ge(bias_raw, 48)
                nc.gpsimd.tensor_copy(bias_parts[:, 0, :], bias_in[:, :]).then_inc(bias_split, 1)
                pool.wait_ge(bias_split, 1)
                nc.gpsimd.tensor_tensor(bias_in[:, :], bias_in[:, :], bias_parts[:, 0, :], ALU.subtract
                                        ).then_inc(bias_rest, 1)
                pool.wait_ge(bias_rest, 1)
                nc.gpsimd.tensor_copy(bias_parts[:, 1, :], bias_in[:, :]).then_inc(bias_split, 1)
                pool.wait_ge(bias_split, 2)
                nc.gpsimd.tensor_tensor(bias_parts[:, 2, :], bias_in[:, :], bias_parts[:, 1, :], ALU.subtract
                                        ).then_inc(bias_split, 1)
            pool.wait_ge(place_ready, 1)
            if load_weights:
                pool.wait_ge(t["x_sorted_cleared"], 16 * TILES)
            for i in range(NT):
                for r in range(2):
                    nc.gpsimd.indirect_dma_start(t["x_sorted"],
                                                 bass.IndirectOffsetOnAxis(ap=place[:, r, i:i + 1], axis=0), xn[:, i, :], None).then_inc(scattered, 16)
            for i in range(NT):
                pool.wait_ge(sh_added, i // 2 + 1)
                nc.gpsimd.tensor_tensor(x_sb[:, i, :], x_sb[:, i, :], xn[:, i, :], ALU.add).then_inc(kept, 1)
            for e in range(SH):
                for i in range(NT):
                    pool.wait_ge(kept, e * NT + i + 1)
                    nc.gpsimd.tensor_tensor(x_sb[:, i, :], x_sb[:, i, :], wt["bias2_s"][:, e, :], ALU.add
                                            ).then_inc(kept, 1)
            for m in range(XIN):
                pool.wait_ge(y_out[m], 16 * len(range(m, TILES, XIN)))
            for i in range(NT):
                if i >= GIN:
                    pool.wait_ge(joined, i - GIN + 1)
                for r in range(2):
                    nc.gpsimd.indirect_dma_start(back[:, i % GIN, r, :], None, t["y_sorted"],
                                                 bass.IndirectOffsetOnAxis(ap=place[:, r, i:i + 1], axis=0)
                                                 ).then_inc(g_in[i % GIN], 16)

        @block.vector
        def _(dve):
            mean, rstd = norm_statistics(nc, dve, t, s, ns)
            for i in range(NT):
                nc.vector.tensor_scalar(xn[:, i, :], x_sb[:, i, :], mean[:, i:i + 1], rstd[:, i:i + 1],
                                        ALU.subtract, ALU.mult).then_inc(xn_ready, 1)
            link = link_on(dve, chain)
            wide = lambda a: a.rearrange("p (i o) -> p i o", o=1).broadcast_to([P, NT, E])
            dve.wait_ge(exp_done, 1)
            link(nc.vector.tensor_scalar(aff[:, :, :], aff[:, :, :], 1.0, None, ALU.add))
            link(nc.vector.reciprocal(aff[:, :, :], aff[:, :, :]))
            src = aff
            for r in range(2):
                link(nc.vector.tensor_reduce(top[:, r, :], src[:, :, :], AX.X, ALU.max))
                link(nc.vector.tensor_tensor(key[:, :, :], src[:, :, :], wide(top[:, r, :]), ALU.is_equal))
                link(nc.vector.scalar_tensor_tensor(key[:, :, :], key[:, :, :], -float(E), t["experts"][:, :, :],
                                                    ALU.mult, ALU.add))
                link(nc.vector.tensor_reduce(idx[:, :], key[:, :, :], AX.X, ALU.min))
                link(nc.vector.tensor_tensor(one[r][:, :, :], key[:, :, :], wide(idx[:, :]), ALU.is_equal))
                if r == 0:
                    link(nc.vector.scalar_tensor_tensor(second[:, :, :], one[0][:, :, :], -4.0, aff[:, :, :],
                                                        ALU.mult, ALU.add))
                    src = second
            nc.vector.tensor_tensor(chosen[:, :, :].rearrange("p e i -> p i e"), one[0][:, :, :], one[1][:, :, :],
                                    ALU.add).then_inc(chosen_ready, 1)
            link(nc.vector.tensor_tensor(den[:, :], top[:, 0, :], top[:, 1, :], ALU.add))
            link(nc.vector.reciprocal(den[:, :], den[:, :]))
            for r in range(2):
                link(nc.vector.tensor_tensor(top[:, r, :], top[:, r, :], den[:, :], ALU.mult))
            dve.wait_ge(counted, 1)
            cnt = bank[7][:, :].rearrange("p (k e i) -> p k e i", k=2, e=E)
            link(nc.vector.tensor_copy(total[:, :, :], cnt[:, 1, :, :]))
            flat = lambda a: a[:, :, :].rearrange("p e i -> p (e i)")
            link(nc.vector.tensor_tensor_scan(flat(before), flat(t["restart"]), flat(total), 0.0, ALU.mult, ALU.add))
            link(nc.vector.tensor_scalar(tiles_of[:, :], before[:, :, NT - 1], 1.0 / P, (P - 1 - 63.75) / P,
                                         ALU.mult, ALU.add))
            link(nc.vector.tensor_scalar(tiles_of[:, :], tiles_of[:, :], MAGIC, -MAGIC, ALU.add, ALU.add))
            link(nc.vector.tensor_tensor_scan(tiles_to[:, :], t["ones_e"][:, :], tiles_of[:, :], 0.0, ALU.mult,
                                              ALU.add))
            link(nc.vector.tensor_tensor(before[:, :, :], before[:, :, :], total[:, :, :], ALU.subtract))
            link(nc.vector.tensor_tensor(before[:, :, :], cnt[:, 0, :, :], before[:, :, :], ALU.add))
            nc.vector.tensor_tensor(ended[:, :, :], tiles_to[0:1, :].rearrange("p (o e) -> p o e", o=1)
                                    .broadcast_to([1, TILES, E]), t["tile_no"][:, :, :], ALU.is_le)
            link(nc.vector.tensor_tensor(tiles_of[:, :], tiles_to[:, :], tiles_of[:, :], ALU.subtract))
            link(nc.vector.scalar_tensor_tensor(before[:, :, :], tiles_of[:, :].rearrange("p (e o) -> p e o", o=1)
                                                .broadcast_to([P, E, NT]), float(P), before[:, :, :],
                                                ALU.mult, ALU.add))
            for r in range(2):
                link(nc.vector.tensor_tensor(key[:, :, :], one[r][:, :, :], before[:, :, :].rearrange("p e i -> p i e"),
                                             ALU.mult))
                link(nc.vector.tensor_reduce(placef[:, r, :], key[:, :, :], AX.X, ALU.add))
            nc.vector.tensor_copy(place[:, :, :], placef[:, :, :]).then_inc(place_ready, 1)
            link(nc.vector.tensor_reduce(expert_of[:, :], ended[:, :, :], AX.X, ALU.add))
            nc.vector.tensor_scalar(expert_id[:, :], expert_of[:, :], float(E - 1), None, ALU.min
                                    ).then_inc(place_ready, 1)

            def add_shared(j):
                for k in range(TPC // 2):
                    i = j * TPC + 2 * k
                    dve.wait_ge(sh_done, i // 2 + 1)
                    xs = x_sb[:, i:i + 2, :]
                    nc.vector.tensor_tensor(xs, bank[4 + k][:, :].rearrange("p (i d) -> p i d", i=2), xs, ALU.add
                                            ).then_inc(sh_added, 1)

            for j in range(NCH):
                for e in range(SH):
                    dve.wait_ge(gel_ready, j * SH + e + 1)
                    if j >= 2:
                        dve.wait_ge(sh_done, (j - 1) * TPC // 2)
                    nc.vector.scalar_tensor_tensor(y[:, j % 2, e, :], bank[2 * e + 1][:, :], wt["bias_s"][:, 1, e:e + 1],
                                                   gel[:, e, :], ALU.add, ALU.mult).then_inc(y_ready, 1)
                if j:
                    add_shared(j - 1)
            add_shared(NCH - 1)

            def step(j, m, r):
                a, d = j - 1, j - 3
                if live(d):
                    dve.wait_ge(d_done, d + 1)
                    if not (isinstance(d, int) and d < XIN):
                        dve.wait_ge(y_out[(m - 3) % XIN], round_of(m, r, 3) * 16)
                    nc.vector.tensor_copy(yo[:, (m - 3) % XIN, :], bank[6 + (m - 3) % 2][:, 0:D]).then_inc(yo_ready, 1)
                if live(a):
                    dve.wait_ge(hg_ready, a + 1)
                    if not (isinstance(a, int) and a < 2):
                        dve.wait_ge(t2_done, a - 1)
                    nc.vector.tensor_tensor(yr[:, (m - 1) % 2, :], hg[:, (m - 1) % 2, :],
                                            bank[2 + (m - 1) % 2][:, F:2 * F], ALU.mult).then_inc(yr_ready, 1)
            steps(dve, step, 3)

            dve.wait_ge(kept, (1 + SH) * NT)
            for i in range(NT):
                dve.wait_ge(g_in[i % GIN], 32 * (i // GIN + 1))
                link(nc.vector.scalar_tensor_tensor(x_sb[:, i, :], back[:, i % GIN, 0, :], top[:, 0, i:i + 1],
                                                    x_sb[:, i, :], ALU.mult, ALU.add))
                nc.vector.scalar_tensor_tensor(x_sb[:, i, :], back[:, i % GIN, 1, :], top[:, 1, i:i + 1],
                                               x_sb[:, i, :], ALU.mult, ALU.add).then_inc(joined, 1)
                if out is None:
                    dve.wait_ge(joined, i + 1)
                    tile_statistics(nc, t, i).then_inc(measured, 1)
            dve.wait_ge(joined, NT)
            if out is None:
                dve.wait_ge(measured, NT)

        @block.tensor
        def _(pe):
            def turn(j):
                for k in range(TPC):
                    i = j * TPC + k
                    pe.wait_ge(xn_ready, i + 1)
                    if j >= 2:
                        pe.wait_ge(xT_ready, NC * (j - 1))
                    for m in range(NC):
                        ins = nc.tensor.transpose(bank[j % 2 * NC + m][:, k * P:(k + 1) * P],
                                                  xn[:, i, m * P:(m + 1) * P], ident[:, :])
                ins.then_inc(xt_done, 1)

            def logits(j):
                pe.wait_ge(xT_ready, NC * (j + 1))
                if j >= 2:
                    pe.wait_ge(lg_out, j - 1)
                for m in range(NC):
                    ins = nc.tensor.matmul(bank[4 + j % 2][0:E, :], wt["wa"][:, m, :], xT[:, m, j * CH:(j + 1) * CH],
                                           start=m == 0, stop=m == NC - 1)
                ins.then_inc(lg_done, 1)

            def turn_logits(j):
                pe.wait_ge(lg_out, j + 1)
                for k in range(TPC):
                    i = j * TPC + k
                    ins = nc.tensor.transpose(bank[6][:, i * E:(i + 1) * E], lgT[:, j % 2, k * P:(k + 1) * P],
                                              ident[0:E, 0:E])
                ins.then_inc(lg_turned, 1)

            turn(0)
            pe.wait_ge(wt["wa_loaded"], 16)
            for j in range(NCH):
                if j + 1 < NCH:
                    turn(j + 1)
                logits(j)
                if j:
                    turn_logits(j - 1)
            turn_logits(NCH - 1)

            def shared_up(j):
                for e in range(SH):
                    if j:
                        pe.wait_ge(y_ready, (j - 1) * SH + e + 1)
                    for a in range(2):
                        for m in range(NC):
                            ins = nc.tensor.matmul(bank[2 * e + a][:, :], wt["up_s"][:, e, a, m, :],
                                                   xT[:, m, j * CH:(j + 1) * CH], start=m == 0, stop=m == NC - 1)
                    ins.then_inc(gu_done, 1)

            def shared_down(j):
                pe.wait_ge(y_ready, SH * (j + 1))
                for k in range(TPC):
                    if j:
                        pe.wait_ge(sh_added, (j - 1) * TPC // 2 + k // 2 + 1)
                    for e in range(SH):
                        ins = nc.tensor.matmul(bank[4 + k // 2][:, k % 2 * D:(k % 2 + 1) * D],
                                               y[:, j % 2, e, k * P:(k + 1) * P], wt["down_s"][:, e, :],
                                               start=e == 0, stop=e == SH - 1)
                    if k % 2:
                        ins.then_inc(sh_done, 1)

            if load_weights:
                pe.wait_ge(wt["s_loaded"], 16 * (3 * SH + 2 + SH))
            shared_up(0)
            pe.wait_ge(chosen_ready, 1)
            ch = chosen[:, :, :].rearrange("p e i -> p (e i)")
            nc.tensor.matmul(bank[7][:, 0:NT * E], t["before_me"][:, :], ch, start=True, stop=True)
            nc.tensor.matmul(bank[7][:, NT * E:2 * NT * E], t["ones"][:, :], ch, start=True, stop=True
                             ).then_inc(counted, 1)
            for j in range(1, NCH):
                shared_up(j)
                shared_down(j - 1)
            shared_down(NCH - 1)

            pe.wait_ge(place_ready, 2)
            if load_weights:
                pe.wait_ge(wt["r_loaded"], 16 * 5)
                pe.wait_ge(wt["bias_loaded"], 16 * PARTS)
            pe.wait_ge(y_ready, SH * NCH)
            pe.wait_ge(sh_added, NT // 2)

            number = [pe.alloc_register(f"{tag}expert{m}") for m in range(XIN)]

            def step(j, m, r):
                a, b, d = j - 1, j - 2, j - 3
                if live(j):
                    pe.load(number[m], expert_id[0:1, bass.ds(j, 1)])
                    pe.wait_ge(x_in[m], r * 16 + 16)
                    if not (isinstance(j, int) and j < 2):
                        pe.wait_ge(t1_out, j - 1)
                    for n in range(NC):
                        ins = nc.tensor.transpose(bank[m % 2][:, n * P:(n + 1) * P], xin[:, m, n * P:(n + 1) * P],
                                                  ident[:, :])
                    ins.then_inc(t1_done, 1)
                if live(a):
                    pe.wait_ge(t1_out, a + 1)
                    if not (isinstance(a, int) and a < 2):
                        pe.wait_ge(yr_ready, a - 1)
                    e = pe.snap(number[(m - 1) % XIN], min_val=0, max_val=E - 1)
                    u = (m - 1) % 2
                    nc.tensor.matmul(bank[2 + u][:, 0:2 * F], t["one_rows"][:, :], bias_up[:, :, bass.ds(e, 1), :],
                                     start=True, stop=False)
                    for n in range(NC):
                        ins = nc.tensor.matmul(bank[2 + u][:, 0:2 * F], xsT[:, u, n, :],
                                               up_r[:, bass.ds(e, 1), n, :, :].rearrange("p o a f -> p (o a f)"),
                                               start=False, stop=n == NC - 1)
                    ins.then_inc(u_done, 1)
                if live(b):
                    pe.wait_ge(yr_ready, b + 1)
                    if not (isinstance(b, int) and b < 2):
                        pe.wait_ge(t2_out, b - 1)
                    nc.tensor.transpose(bank[4 + m % 2][:, 0:P], yr[:, m % 2, :], ident[:, :]).then_inc(t2_done, 1)
                if live(d):
                    pe.wait_ge(t2_out, d + 1)
                    if not (isinstance(d, int) and d < 2):
                        pe.wait_ge(yo_ready, d - 1)
                    e = pe.snap(number[(m - 3) % XIN], min_val=0, max_val=E - 1)
                    u = (m - 3) % 2
                    nc.tensor.matmul(bank[6 + u][:, 0:D], t["one_rows"][:, :],
                                     bias_down[:, bass.ds(e, 1), :].rearrange("p o d -> p (o d)"), start=True,
                                     stop=False)
                    nc.tensor.matmul(bank[6 + u][:, 0:D], yT[:, u, :],
                                     down_r[:, bass.ds(e, 1), :].rearrange("p o d -> p (o d)"), start=False, stop=True
                                     ).then_inc(d_done, 1)
            steps(pe, step, 3)

        @block.scalar
        def _(act):
            nc.scalar.preload_act_table(ACT.Exp)
            def move(j):
                act.wait_ge(xt_done, j + 1)
                for m in range(NC):
                    nc.scalar.activation(xT[:, m, j * CH:(j + 1) * CH], bank[j % 2 * NC + m][:, :], ACT.Copy
                                         ).then_inc(xT_ready, 1)

            move(0)
            for j in range(NCH):
                if j + 1 < NCH:
                    move(j + 1)
                act.wait_ge(lg_done, j + 1)
                if j >= 2:
                    act.wait_ge(lg_turned, j - 1)
                nc.scalar.activation(lgT[:, j % 2, :], bank[4 + j % 2][0:E, :], ACT.Copy).then_inc(lg_out, 1)
            act.wait_ge(lg_turned, NCH)
            nc.scalar.activation(aff[:, :, :], bank[6][:, 0:NT * E].rearrange("p (i e) -> p i e", e=E), ACT.Exp,
                                 scale=-1.0).then_inc(exp_done, 1)
            nc.scalar.preload_act_table(ACT.Gelu)
            if load_weights:
                act.wait_ge(wt["s_loaded"], 16 * (3 * SH + 2 + SH))
            for j in range(NCH):
                for e in range(SH):
                    n = j * SH + e
                    act.wait_ge(gu_done, n + 1)
                    if j:
                        act.wait_ge(y_ready, n - 1)
                    nc.scalar.activation(gel[:, e, :], bank[2 * e][:, :], ACT.Gelu, bias=wt["bias_s"][:, 0, e:e + 1]
                                         ).then_inc(gel_ready, 1)

            def step(j, m, r):
                a, b, o = j - 1, j - 2, j - XIN
                if live(o):
                    act.wait_ge(yo_ready, o + 1)
                    act.dma_start(t["y_sorted"][bass.ds(o * P, P), :], yo[:, m, :]).then_inc(y_out[m], 16)
                if live(j):
                    act.wait_ge(t1_done, j + 1)
                    if not (isinstance(j, int) and j < 2):
                        act.wait_ge(u_done, j - 1)
                    nc.scalar.activation(xsT[:, m % 2, :, :], bank[m % 2][:, 0:D].rearrange("p (c n) -> p c n", c=NC),
                                         ACT.Copy).then_inc(t1_out, 1)
                if live(a):
                    u = (m - 1) % 2
                    act.wait_ge(u_done, a + 1)
                    if not (isinstance(a, int) and a < 2):
                        act.wait_ge(yr_ready, a - 1)
                    nc.scalar.activation(hg[:, u, :], bank[2 + u][:, 0:F], ACT.Gelu).then_inc(hg_ready, 1)
                if live(b):
                    act.wait_ge(t2_done, b + 1)
                    if not (isinstance(b, int) and b < 2):
                        act.wait_ge(d_done, b - 1)
                    nc.scalar.activation(yT[:, m % 2, :], bank[4 + m % 2][:, 0:P], ACT.Copy).then_inc(t2_out, 1)
            steps(act, step, XIN)

    nc.all_engine_barrier()
    nc.clear_and_free_semaphores(semaphores)
    nc.all_engine_barrier()


def attention_b(nc, t):
    x_sb, ident = t["x"], t["ident"]
    HV = HB - HP
    with ExitStack() as c:
        sb = lambda n, s, d=F32: c.enter_context(nc.sbuf_tensor("ab_" + n, s, d))
        sem = lambda n: c.enter_context(nc.semaphore("ab_" + n))
        s = {"small": sb("small", [P, 7, NT])}
        shift = sb("shift", [P, NT])
        xn, xT = sb("xn", [P, 2, D]), sb("xT", [P, 2, NC, P])
        rot = sb("rot", [P, 2, 2 * HB, HDB])
        turned = sb("turned", [P, 2, 2 * HB, HDB])
        v = sb("v", [P, 2, HB, HDB])
        prod = sb("prod", [P, HV, HB, HDB])
        prod_s, prod_v = sb("prod_s", [P, HP, HB, HDB]), sb("prod_v", [P, HP, HDB, HB])
        sc, ex = sb("sc", [P, 2, HB, HB]), sb("ex", [P, 2, HB, HB])
        mx, dn = sb("mx", [P, HB]), sb("dn", [P, 2, HB])
        o, oT = sb("o", [P, 2, HB, HDB]), sb("oT", [P, NC, P])
        ps = lambda n: c.enter_context(nc.psum_tensor("ab_" + n, [P, CH], F32))
        xt_ps, v_ps, ot_ps, y_ps = (ps(n)[:, 0:D] for n in ("xt_ps", "v_ps", "ot_ps", "y_ps"))
        qk_ps, sum_s, sum_v = [ps("qk0"), ps("qk1")], ps("sum_s_ps"), ps("sum_v_ps")
        ns = {k: sem(k) for k in ("dve_chain", "veps", "pow")}
        norm_known, xn_ready, xt_done, xT_ready, qkv_done = (
            sem("norm_known"), sem("xn_ready"), sem("xt_done"), sem("xT_ready"), sem("qkv_done"))
        turned_ready, score_chain, max_chain, value_chain, den_known, den_inverted = (
            sem(n) for n in ("turned", "score_chain", "max_chain", "value_chain", "den_known", "den_inverted"))
        prod_s_ready, prod_v_ready, sum_s_done, sum_v_done = (
            sem(n) for n in ("prod_s", "prod_v", "sum_s_done", "sum_v_done"))
        rot_ready, v_ready, scores_p, less_max, ex_ready, out_v, out_p = (
            sem(n) for n in ("rot_ready", "v_ready", "scores_p", "less_max", "ex_ready", "out_v", "out_p"))
        o_ready, ot_done, oT_ready, y_done, added, measured = (
            sem(n) for n in ("o_ready", "ot_done", "oT_ready", "y_done", "added", "measured"))
        block = c.enter_context(nc.Block())
        LAG = 3

        def steps(eng, step):
            for j in range(6):
                step(j, j % 2)
            with eng.Fori(3, NT // 2 - 1) as r:
                step(r * 2, 0)
                step(r * 2 + 1, 1)
            for j in range(NT - 2, NT + LAG):
                step(j, j % 2)

        def live(i):
            return not isinstance(i, int) or 0 <= i < NT

        def free(eng, sem, i, slots):
            if not (isinstance(i, int) and i < slots):
                eng.wait_ge(sem, i - slots + 1)

        def along(a, b, heads):
            n = len(heads)
            return (a[:, heads[0]:heads[0] + n, :].rearrange("p h (o n) -> p h o n", o=1).broadcast_to([P, n, HB, HDB]),
                    b.broadcast_to([P, n, HB, HDB]))

        def score_operands(u, heads):
            return along(rot[:, u, :, :], rot[:, u, HB:2 * HB, :].rearrange("p (o h) n -> p o h n", o=1), heads)

        def value_operands(u, heads):
            return along(ex[:, u, :, :], v[:, u, :, :].rearrange("p (o t) n -> p o n t", o=1), heads)

        def wide(a, n):
            return a.rearrange("p (h o) -> p h o", o=1).broadcast_to([P, HB, n])

        @block.gpsimd
        def _(pool):
            pool.wait_ge(ns["veps"], 1)
            nc.gpsimd.tensor_tensor(s["small"][:, 3, :], s["small"][:, 2, :], t["neg_half"][:, :], ALU.pow
                                    ).then_inc(ns["pow"], 1)
            heads = range(HV, HB)

            def step(j, u):
                a, b, d = j - 1, j - 2, j - LAG
                if live(a):
                    pool.wait_ge(rot_ready, a + 1)
                    free(pool, sum_s_done, a, 1)
                    nc.gpsimd.tensor_tensor(prod_s[:, :, :, :], *score_operands(1 - u, heads), ALU.mult
                                            ).then_inc(prod_s_ready, 1)
                    pool.wait_ge(prod_s_ready, a + 1)
                if live(d):
                    pool.wait_ge(out_v, d + 1)
                    pool.wait_ge(den_inverted, d + 1)
                    pool.wait_ge(out_p, d + 1)
                    nc.gpsimd.tensor_tensor(o[:, 1 - u, :, :], o[:, 1 - u, :, :], wide(dn[:, 1 - u, :], HDB), ALU.mult
                                            ).then_inc(o_ready, 1)
                    pool.wait_ge(o_ready, d + 1)
                if live(b):
                    pool.wait_ge(v_ready, b + 1)
                    pool.wait_ge(ex_ready, b + 1)
                    free(pool, sum_v_done, b, 1)
                    nc.gpsimd.tensor_tensor(prod_v[:, :, :, :], *value_operands(u, heads), ALU.mult
                                            ).then_inc(prod_v_ready, 1)
                    pool.wait_ge(prod_v_ready, b + 1)
            steps(pool, step)

        @block.vector
        def _(dve):
            mean, rstd = norm_statistics(nc, dve, t, s, ns)
            nc.vector.scalar_tensor_tensor(shift[:, :], mean, -1.0, rstd, ALU.mult, ALU.mult).then_inc(norm_known, 1)
            heads = range(HV)

            def rotation_products(i, u):
                dve.wait_ge(qkv_done, i + 1)
                shape = [P, 2, 2 * HB, HDB]
                nc.vector.tensor_tensor(turned[:, :, :, :], qk_ps[u][:, :].rearrange(
                    "p (o h n) -> p o h n", o=1, h=2 * HB).broadcast_to(shape), t["rotation"][:, bass.ds(i, 1), :, :]
                    .rearrange("p i f n -> p f i n").broadcast_to(shape), ALU.mult).then_inc(turned_ready, 1)

            def rotation_sums(i, u):
                dve.wait_ge(turned_ready, i + 1)
                pair = turned[:, :, :, :].rearrange("p f h (n e) -> p f h n e", e=2)
                nc.vector.tensor_tensor(rot[:, u, :, :].rearrange("p h (f n) -> p f h n", f=2), pair[:, :, :, :, 0],
                                        pair[:, :, :, :, 1], ALU.add).then_inc(rot_ready, 1)

            def step(j, u):
                a, b, f = j - 1, j - 2, j - LAG - 1
                if live(a):
                    dve.wait_ge(rot_ready, a + 1)
                    nc.vector.tensor_tensor(prod[:, :, :, :], *score_operands(1 - u, heads), ALU.mult
                                            ).then_inc(score_chain, 1)
                if live(a):
                    if live(f):
                        dve.wait_ge(added, f + 1)
                        tile_statistics(nc, t, f).then_inc(measured, 1)
                    dve.wait_ge(score_chain, a * 2 + 1)
                    nc.vector.tensor_reduce(sc[:, 1 - u, 0:HV, :], prod[:, :, :, :], AX.X, ALU.add
                                            ).then_inc(score_chain, 1)
                if live(b):
                    dve.wait_ge(v_ready, b + 1)
                    dve.wait_ge(ex_ready, b + 1)
                    free(dve, o_ready, b, 2)
                    nc.vector.tensor_reduce(dn[:, u, :], ex[:, u, :, :], AX.X, ALU.add).then_inc(den_known, 1)
                    dve.wait_ge(score_chain, a * 2 + 2 if live(a) else 2 * NT)
                    nc.vector.tensor_tensor(prod[:, :, :, :], *value_operands(u, heads), ALU.mult
                                            ).then_inc(value_chain, 1)
                    dve.wait_ge(den_known, b + 1)
                    nc.vector.reciprocal(dn[:, u, :], dn[:, u, :]).then_inc(den_inverted, 1)
                    dve.wait_ge(value_chain, b + 1)
                    free(dve, ot_done, b, 2)
                    nc.vector.tensor_reduce(o[:, u, 0:HV, :], prod[:, :, :, :], AX.X, ALU.add).then_inc(out_v, 1)
                if live(j):
                    rotation_products(j, u)
                if live(a):
                    dve.wait_ge(scores_p, a + 1)
                    dve.wait_ge(score_chain, a * 2 + 2)
                    nc.vector.tensor_reduce(mx[:, :], sc[:, 1 - u, :, :], AX.X, ALU.max).then_inc(max_chain, 1)
                if live(j):
                    rotation_sums(j, u)
                if live(a):
                    dve.wait_ge(max_chain, a + 1)
                    nc.vector.tensor_tensor(sc[:, 1 - u, :, :], sc[:, 1 - u, :, :], wide(mx[:, :], HB), ALU.subtract
                                            ).then_inc(less_max, 1)
                if live(b):
                    dve.wait_ge(out_v, b + 1)
                    dve.wait_ge(den_inverted, b + 1)
            steps(dve, step)
            for i in range(NT - LAG, NT):
                dve.wait_ge(added, i + 1)
                tile_statistics(nc, t, i).then_inc(measured, 1)
            dve.wait_ge(measured, NT)

        @block.tensor
        def _(pe):
            def add_up(bank, products):
                n = HP * HB
                flat = products[:, :, :, :].rearrange("p h t n -> p (h t) n")
                for k in range(HDB):
                    ins = nc.tensor.matmul(bank[:, 0:n], ident[:, :], flat[:, :, k], start=k == 0, stop=k == HDB - 1)
                return ins

            def step(j, u):
                a, b, d = j - 1, j - 2, j - LAG
                if live(j):
                    pe.wait_ge(xn_ready, j + 1)
                    free(pe, xT_ready, j, 1)
                    for m in range(NC):
                        ins = nc.tensor.transpose(xt_ps[:, m * P:(m + 1) * P], xn[:, u, m * P:(m + 1) * P],
                                                  ident[:, :])
                    ins.then_inc(xt_done, 1)
                    pe.wait_ge(xT_ready, j + 1)
                    free(pe, rot_ready, j, 2)
                    free(pe, v_ready, j, 1)
                    for m in range(NC):
                        nc.tensor.matmul(qk_ps[u][:, :], xT[:, u, m, :], t["wqk"][:, m, :], start=m == 0,
                                         stop=m == NC - 1)
                    for m in range(NC):
                        ins = nc.tensor.matmul(v_ps, xT[:, u, m, :], t["wv"][:, m, :], start=m == 0,
                                               stop=m == NC - 1)
                    ins.then_inc(qkv_done, 1)
                if live(a):
                    pe.wait_ge(prod_s_ready, a + 1)
                    free(pe, scores_p, a, 1)
                    add_up(sum_s, prod_s).then_inc(sum_s_done, 1)
                if live(d):
                    pe.wait_ge(o_ready, d + 1)
                    free(pe, oT_ready, d, 1)
                    flat = o[:, 1 - u, :, :].rearrange("p h n -> p (h n)")
                    for m in range(NC):
                        ins = nc.tensor.transpose(ot_ps[:, m * P:(m + 1) * P], flat[:, m * P:(m + 1) * P], ident[:, :])
                    ins.then_inc(ot_done, 1)
                    pe.wait_ge(oT_ready, d + 1)
                    free(pe, added, d, 1)
                    nc.tensor.matmul(y_ps, ident[:, :], x_sb[:, bass.ds(d, 1), :].rearrange("p o d -> p (o d)"),
                                     start=True, stop=False)
                    for m in range(NC):
                        ins = nc.tensor.matmul(y_ps, oT[:, m, :], t["wo_b"][:, m, :], start=False, stop=m == NC - 1)
                    ins.then_inc(y_done, 1)
                if live(b):
                    pe.wait_ge(prod_v_ready, b + 1)
                    free(pe, out_p, b, 1)
                    add_up(sum_v, prod_v).then_inc(sum_v_done, 1)
            steps(pe, step)

        @block.scalar
        def _(act):
            nc.scalar.preload_act_table(ACT.Exp)
            act.wait_ge(norm_known, 1)

            def norm(i, u):
                free(act, xt_done, i, 2)
                nc.scalar.activation(xn[:, u, :], x_sb[:, bass.ds(i, 1), :].rearrange("p o d -> p (o d)"),
                                     ACT.Identity, scale=s["small"][:, 1, bass.ds(i, 1)],
                                     bias=shift[:, bass.ds(i, 1)]).then_inc(xn_ready, 1)

            def step(j, u):
                a, b, d = j - 1, j - 2, j - LAG
                if live(a):
                    act.wait_ge(qkv_done, a + 1)
                    free(act, out_v, a, 2)
                    free(act, out_p, a, 2)
                    nc.scalar.activation(v[:, 1 - u, :, :], v_ps.rearrange("p (h n) -> p h n", h=HB),
                                         ACT.Copy).then_inc(v_ready, 1)
                if live(j):
                    act.wait_ge(xt_done, j + 1)
                    free(act, qkv_done, j, 2)
                    nc.scalar.activation(xT[:, u, :, :], xt_ps.rearrange("p (c n) -> p c n", c=NC),
                                         ACT.Copy).then_inc(xT_ready, 1)
                if live(a):
                    act.wait_ge(sum_s_done, a + 1)
                    nc.scalar.activation(sc[:, 1 - u, HV:HB, :], sum_s[:, 0:HP * HB].rearrange(
                        "p (h t) -> p h t", h=HP), ACT.Copy).then_inc(scores_p, 1)
                if live(d):
                    act.wait_ge(ot_done, d + 1)
                    free(act, y_done, d, 1)
                    nc.scalar.activation(oT[:, :, :], ot_ps.rearrange("p (c n) -> p c n", c=NC), ACT.Copy
                                         ).then_inc(oT_ready, 1)
                    act.wait_ge(y_done, d + 1)
                    nc.scalar.activation(x_sb[:, bass.ds(d, 1), :].rearrange("p o d -> p (o d)"), y_ps, ACT.Copy
                                         ).then_inc(added, 1)
                if live(j + 1):
                    norm(j + 1, 1 - u)
                if live(a):
                    act.wait_ge(less_max, a + 1)
                    nc.scalar.activation(ex[:, 1 - u, :, :], sc[:, 1 - u, :, :], ACT.Exp, scale=float(HDB) ** -0.5
                                         ).then_inc(ex_ready, 1)
                if live(b):
                    act.wait_ge(sum_v_done, b + 1)
                    free(act, ot_done, b, 2)
                    nc.scalar.activation(o[:, u, HV:HB, :], sum_v[:, 0:HP * HDB].rearrange(
                        "p (h n) -> p h n", h=HP), ACT.Copy).then_inc(out_p, 1)

            norm(0, 0)
            steps(act, step)
            act.wait_ge(added, NT)


def rest_of_layers(nc, t, w, stop, out):
    ffn = {k.removeprefix("L0_ffn_"): v for k, v in w.items() if "ffn" in k}
    expert_layer(nc, t, ffn, "l2", True)
    if stop > 2:
        attention_b(nc, t)
    if stop > 3:
        expert_layer(nc, t, ffn, "l4", False, out)


def build(nc, stop=9, out=None, **w):
    nc.disable_value_cache = True
    with ExitStack() as c:
        sb = lambda n, s, d=F32: c.enter_context(nc.sbuf_tensor(n, s, d))
        t = {
            "x": sb("x_sb", [P, NT, D]), "ident": sb("ident", [P, P]), "identb": sb("identb", [P, P], BF16),
            "mask_s": sb("mask_s", [P, P], BF16), "mask_t": sb("mask_t", [P, P], BF16),
            "neg_half": sb("neg_half", [P, NT]), "experts": sb("experts", [P, NT, E]),
            "restart": sb("restart", [P, E, NT]), "ones_e": sb("ones_e", [P, E]),
            "tile_no": sb("tile_no", [1, TILES, E]), "one_rows": sb("one_rows", [PARTS, P], BF16),
            "before_me": sb("before_me", [P, P], BF16), "ones": sb("ones", [P, P], BF16), "zeros": sb("zeros", [P, D]),
            "x_sorted": nc.dram_tensor("x_sorted", (TILES * P, D), F32, kind="Internal").ap(),
            "y_sorted": nc.dram_tensor("y_sorted", (TILES * P, D), F32, kind="Internal").ap(),
        }
        t["stats"] = sb("stats", [P, NT, 6])
        t["rotation"] = sb("rotation", [P, NT, 2, HDB])
        t["wqk"], t["wv"], t["wo_b"] = sb("wqk", [P, NC, 2 * D]), sb("wv", [P, NC, D]), sb("wo_b", [P, NC, D])
        t["wo_loaded"] = c.enter_context(nc.semaphore("wo_loaded"))
        t["x_sorted_cleared"] = c.enter_context(nc.semaphore("x_sorted_cleared"))
        a = {k.removeprefix("L0_attn_a_"): v for k, v in w.items() if "attn_a" in k}
        with ExitStack() as ca:
            sa = lambda n, s, d=F32: ca.enter_context(nc.sbuf_tensor(n, s, d))
            t["wf"], t["bf"] = sa("wf", [P, 3, NC, DL]), sa("bf", [P, 3])
            t["wo_a"], t["bo_a"] = sa("wo_a", [P, D]), sa("bo_a", [P, D])
            t["v"] = sa("v_all", [P, NQ, NB, QUAD * HDA])
            t["qst"], t["kst"] = sa("qst", [KM, 2, QUAD, T], BF16), sa("kst", [KM, 2, QUAD, T], BF16)
            t["stack"] = [ca.enter_context(nc.semaphore(f"aa_stack{u}")) for u in range(2)]
            H2 = HDB // 2
            t["angles"] = {
                "freq": sa("rt_freq", [P, H2]), "pos": sa("rt_pos", [P, NB]), "angle": sa("rt_angle", [P, NB, H2]),
                "turns": sa("rt_turns", [P, 2, NB, H2]), "red": sa("rt_red", [P, 2, NB, H2]),
                **{n: ca.enter_context(nc.semaphore("rt_" + n)) for n in ("loaded", "pos_ready", "chain", "reduced")},
            }
            t["out_a"], t["out_aT"] = sa("out_a", [P, 2, DL]), sa("out_aT", [P, 2, DL])
            for n in ("picked", "turned", "ready", "done", "added", "measured"):
                t["out_" + n] = ca.enter_context(nc.semaphore("oa_" + n))
            t["rows_set"] = ca.enter_context(nc.semaphore("aa_rows_set"))
            t["att"] = sa("att", [P, NQ * NB * QUAD, HDA])
            t["q_parts"] = nc.dram_tensor("q_parts", (B * HA, 2 * PARTS - 1, HDA, T), BF16, kind="Internal").ap()
            t["k_parts"] = nc.dram_tensor("k_parts", (B * HA, PARTS, HDA, T), BF16, kind="Internal").ap()
            fold_weights(nc, t, a)
            project_a(nc, t)
            attention_a(nc, t, w["L0_attn_b_inv_freq"])
            output_a(nc, t, {k.removeprefix("L0_attn_b_"): v for k, v in w.items() if "attn_b" in k})
        if stop > 1:
            with ExitStack() as ce:
                se = lambda n, s, d=F32: ce.enter_context(nc.sbuf_tensor("ew_" + n, s, d))
                t["expert_w"] = {
                    "up": se("up", [P, E, NC, 2, F]), "down": se("down", [P, E, D]),
                    "bias": se("bias", [PARTS, NBIAS], BF16),
                    "up_s": se("up_s", [P, SH, 2, NC, F]), "down_s": se("down_s", [P, SH, D]),
                    "bias_s": se("bias_s", [P, 2, SH]), "bias2_s": se("bias2_s", [P, SH, D]),
                    "wa": se("wa", [P, NC, E]),
                    **{n: ce.enter_context(nc.semaphore("ew_" + n)) for n in ("wa_loaded", "s_loaded", "r_loaded",
                                                                             "bias_loaded")},
                }
                rest_of_layers(nc, t, w, stop, out)
        if stop < 4:
            stored = c.enter_context(nc.semaphore("stored"))
            with nc.Block() as block:
                @block.sync
                def _(sp):
                    sp.dma_start(out.rearrange("b (i p) d -> p (b i) d", p=P), t["x"][:, :, :]).then_inc(stored, 16)
                    sp.wait_ge(stored, 16)


_OUT = (B, T, D)


def kernel(**inputs):
    import numpy as np
    import concourse.bacc as bacc
    from concourse.bass_utils import run_bass_kernel_spmd

    nc = bacc.Bacc("TRN2", target_bir_lowering=False, num_devices=1)
    arrays = {name: np.ascontiguousarray(a) for name, a in inputs.items()}
    args = {name: nc.dram_tensor("in_" + name, a.shape, mybir.dt.from_np(a.dtype), kind="ExternalInput").ap()
            for name, a in arrays.items()}
    out = nc.dram_tensor("out_x", _OUT, F32, kind="ExternalOutput").ap()
    build(nc, out=out, **args)
    r = run_bass_kernel_spmd(nc, [{"in_" + name: a for name, a in arrays.items()}], core_ids=[0])
    return r.results[0]["out_x"]
```
